# Optimizing a Trainium2 kernel written in Bass

```python
import numpy as np
import jax
import jax.numpy as jnp

def _softmax(x, axis=-1):
    return jax.nn.softmax(x, axis=axis)

def _gelu(x):
    return jax.nn.gelu(x, approximate=True)

def _silu(x):
    return jax.nn.silu(x)

def _sigmoid(x):
    return jax.nn.sigmoid(x)

def _layernorm(x, axis=-1, eps=1e-05):
    m = jnp.mean(x, axis=axis, keepdims=True)
    v = jnp.var(x, axis=axis, keepdims=True)
    return (x - m) / jnp.sqrt(v + eps)

def _scatter_add(tgt, idx, src, axis=0):
    return tgt.at[idx].add(src)

def _segment_sum(src, seg, n):
    return jax.ops.segment_sum(src, seg, n)
kernel_name = 'mk_metaformer_d2_conv_nhwc256_r4_540b03'

def setup_inputs(seed: int=0):
    np.random.seed(seed)
    _w = jnp.asarray

    def _rec_inputs():
        import jax
        import jax.numpy as jnp
        _gk = jax.random.key(seed)
        x = -0.000125 + 0.9999 * jax.random.normal(jax.random.fold_in(_gk, 1), (8, 32, 32, 64), jnp.float32)
        return x
    x = _rec_inputs()

    def _L0_conv_setup():
        import jax, jax.numpy as jnp
        import numpy as np
        B, H, W, C = (8, 32, 32, 64)
        key = jax.random.key(seed)
        k1, k2 = jax.random.split(key)
        x = jax.random.normal(k1, (B, H, W, C), dtype=jnp.float32)
        gamma = jax.random.normal(k2, (), dtype=jnp.float32)
        return {'x': x, 'gamma': gamma}
    _L0_conv_all = _L0_conv_setup()
    _L0_conv_in = {k: v for k, v in _L0_conv_all.items() if k in ('gamma',)}
    del _L0_conv_all

    def _L0_ffn_setup():
        import jax, jax.numpy as jnp
        import numpy as np
        D_MODEL = 64
        N_EXPERTS = 16
        HIDDEN = 128
        SCALE = 0.02
        key = jax.random.key(seed)
        ks = jax.random.split(key, 5)
        x = jax.random.normal(ks[0], (4, 2048, D_MODEL), dtype=jnp.float32)
        gate_w = jax.random.normal(ks[1], (D_MODEL, N_EXPERTS), dtype=jnp.float32) * SCALE
        gate_b = jnp.zeros((N_EXPERTS,), dtype=jnp.float32)
        w1 = jax.random.normal(ks[2], (N_EXPERTS, D_MODEL, HIDDEN), dtype=jnp.float32) * SCALE
        w2 = jax.random.normal(ks[3], (N_EXPERTS, D_MODEL, HIDDEN), dtype=jnp.float32) * SCALE
        w3 = jax.random.normal(ks[4], (N_EXPERTS, HIDDEN, D_MODEL), dtype=jnp.float32) * SCALE
        return {'x': x, 'gate_w': gate_w, 'gate_b': gate_b, 'w1': w1, 'w2': w2, 'w3': w3}
    _L0_ffn_all = _L0_ffn_setup()
    _L0_ffn_in = {k: v for k, v in _L0_ffn_all.items() if k in ('gate_w', 'gate_b', 'w1', 'w2', 'w3')}
    del _L0_ffn_all

    def _L1_conv_setup():
        import jax, jax.numpy as jnp
        import numpy as np
        H_CONST = 1.0

        def binarize(w, H=H_CONST):
            return jnp.where(w >= 0, H, -H).astype(w.dtype)
        key = jax.random.key(seed)
        k1, k2 = jax.random.split(key)
        x = jax.random.normal(k1, (32, 56, 56, 64), dtype=jnp.float32)
        kernel = jax.random.normal(k2, (3, 3, 64, 64), dtype=jnp.float32) * 0.05
        return {'x': x, 'kernel': kernel}
    _L1_conv_all = _L1_conv_setup()
    _L1_conv_in = {k: v for k, v in _L1_conv_all.items() if k in ('kernel',)}
    del _L1_conv_all

    def _L1_ffn_setup():
        import jax, jax.numpy as jnp
        import numpy as np
        B, N, D = (16, 1024, 64)
        NUM_EXPERTS, TOP_K, HEADS = (4, 2, 4)
        N_EDGES = 262144
        LN_EPS = 1e-05

        def _layernorm(x, g, b):
            mu = x.mean(-1, keepdims=True)
            var = ((x - mu) ** 2).mean(-1, keepdims=True)
            return (x - mu) * jax.lax.rsqrt(var + LN_EPS) * g + b

        def _forward(x, edge_index, W_gat, att_src, att_dst, b_gat, ln_gamma, ln_beta, W1, b1, W2, b2):
            Bc, Nc, Dc = x.shape
            M = Bc * Nc
            x_flat = x.reshape(M, Dc)
            h = (x_flat @ W_gat).reshape(M, HEADS, NUM_EXPERTS)
            loops = jnp.arange(M, dtype=edge_index.dtype)
            src = jnp.concatenate([edge_index[0], loops])
            dst = jnp.concatenate([edge_index[1], loops])
            a_src = (h * att_src).sum(-1)
            a_dst = (h * att_dst).sum(-1)
            e = jax.nn.leaky_relu(a_src[src] + a_dst[dst], negative_slope=0.2)
            e_max = jax.ops.segment_max(e, dst, num_segments=M)
            ee = jnp.exp(e - e_max[dst])
            denom = jax.ops.segment_sum(ee, dst, num_segments=M)
            alpha = ee / (denom[dst] + 1e-16)
            msg = h[src] * alpha[:, :, None]
            agg = jax.ops.segment_sum(msg, dst, num_segments=M).reshape(M, HEADS * NUM_EXPERTS) + b_gat
            scores = _layernorm(agg, ln_gamma, ln_beta).reshape(M, HEADS, NUM_EXPERTS).mean(1)
            scores = scores.reshape(Bc, Nc, NUM_EXPERTS)
            topk_s, topk_i = jax.lax.top_k(scores, TOP_K)
            w = jax.nn.softmax(topk_s, axis=-1)
            out = jnp.zeros_like(x)
            for ei in range(NUM_EXPERTS):
                g = jnp.where(topk_i == ei, w, 0.0).sum(-1)
                hh = jax.nn.gelu(x @ W1[ei] + b1[ei], approximate=False)
                out = out + g[..., None] * (hh @ W2[ei] + b2[ei])
            return out
        key = jax.random.key(seed)
        ks = jax.random.split(key, 8)
        s = 0.05
        return {'x': jax.random.normal(ks[0], (B, N, D), jnp.float32), 'W_gat': jax.random.normal(ks[1], (D, HEADS * NUM_EXPERTS), jnp.float32) * s, 'att_src': jax.random.normal(ks[2], (HEADS, NUM_EXPERTS), jnp.float32) * s, 'att_dst': jax.random.normal(ks[3], (HEADS, NUM_EXPERTS), jnp.float32) * s, 'b_gat': jnp.zeros((HEADS * NUM_EXPERTS,), jnp.float32), 'ln_gamma': jnp.ones((HEADS * NUM_EXPERTS,), jnp.float32), 'ln_beta': jnp.zeros((HEADS * NUM_EXPERTS,), jnp.float32), 'W1': jax.random.normal(ks[4], (NUM_EXPERTS, D, 2 * D), jnp.float32) * s, 'b1': jnp.zeros((NUM_EXPERTS, 2 * D), jnp.float32), 'W2': jax.random.normal(ks[5], (NUM_EXPERTS, 2 * D, D), jnp.float32) * s, 'b2': jnp.zeros((NUM_EXPERTS, D), jnp.float32), 'edge_index': jax.random.randint(ks[6], (2, N_EDGES), 0, B * N, jnp.int32)}
    _L1_ffn_all = _L1_ffn_setup()
    _L1_ffn_in = {k: v for k, v in _L1_ffn_all.items() if k in ('W_gat', 'att_src', 'att_dst', 'b_gat', 'ln_gamma', 'ln_beta', 'W1', 'b1', 'W2', 'b2', 'edge_index')}
    del _L1_ffn_all
    return {'x': x, 'L0_conv_gamma': _L0_conv_in['gamma'], 'L0_ffn_gate_w': _L0_ffn_in['gate_w'], 'L0_ffn_gate_b': _L0_ffn_in['gate_b'], 'L0_ffn_w1': _L0_ffn_in['w1'], 'L0_ffn_w2': _L0_ffn_in['w2'], 'L0_ffn_w3': _L0_ffn_in['w3'], 'L1_conv_kernel': _L1_conv_in['kernel'], 'L1_ffn_W_gat': _L1_ffn_in['W_gat'], 'L1_ffn_att_src': _L1_ffn_in['att_src'], 'L1_ffn_att_dst': _L1_ffn_in['att_dst'], 'L1_ffn_b_gat': _L1_ffn_in['b_gat'], 'L1_ffn_ln_gamma': _L1_ffn_in['ln_gamma'], 'L1_ffn_ln_beta': _L1_ffn_in['ln_beta'], 'L1_ffn_W1': _L1_ffn_in['W1'], 'L1_ffn_b1': _L1_ffn_in['b1'], 'L1_ffn_W2': _L1_ffn_in['W2'], 'L1_ffn_b2': _L1_ffn_in['b2'], 'L1_ffn_edge_index': _L1_ffn_in['edge_index']}

def reference(x, L0_conv_gamma, L0_ffn_gate_w, L0_ffn_gate_b, L0_ffn_w1, L0_ffn_w2, L0_ffn_w3, L1_conv_kernel, L1_ffn_W_gat, L1_ffn_att_src, L1_ffn_att_dst, L1_ffn_b_gat, L1_ffn_ln_gamma, L1_ffn_ln_beta, L1_ffn_W1, L1_ffn_b1, L1_ffn_W2, L1_ffn_b2, L1_ffn_edge_index):
    import jax
    import jax.numpy as jnp

    def _L0_conv_ref(x, gamma):
        import jax, jax.numpy as jnp
        import numpy as np
        B, H, W, C = (8, 32, 32, 64)
        xp = jnp.transpose(x, (0, 3, 2, 1))
        b, c, w, h = xp.shape
        p = xp.reshape(b, c, w * h)
        q = jnp.swapaxes(p, 1, 2)
        s = jnp.einsum('bcn,bnd->bcd', p, q)
        m = jax.nn.softmax(s, axis=-1)
        n = jnp.einsum('bnc,bcd->bnd', q, m)
        n_new = jnp.swapaxes(n, 1, 2).reshape(b, c, w, h)
        out = gamma * n_new + xp
        return jnp.transpose(out, (0, 3, 2, 1))

    def _L0_ffn_ref(x, gate_w, gate_b, w1, w2, w3):
        import jax, jax.numpy as jnp
        import numpy as np
        D_MODEL = 64
        N_EXPERTS = 16
        HIDDEN = 128
        SCALE = 0.02
        n_experts = w1.shape[0]
        logits = jnp.einsum('bsd,de->bse', x, gate_w) + gate_b
        probs = jax.nn.softmax(logits, axis=-1)
        top_probs, top_idx = jax.lax.top_k(probs, 2)
        top_probs = top_probs / jnp.sum(top_probs, axis=-1, keepdims=True)
        dispatch = jnp.sum(jax.nn.one_hot(top_idx, n_experts, dtype=x.dtype) * top_probs[..., None], axis=-2)
        h1 = jnp.einsum('bsd,edh->bseh', x, w1)
        h2 = jnp.einsum('bsd,edh->bseh', x, w2)
        hidden = jax.nn.silu(h1) * h2
        expert_out = jnp.einsum('bseh,eho->bseo', hidden, w3)
        return jnp.einsum('bseo,bse->bso', expert_out, dispatch)

    def _L1_conv_ref(x, kernel):
        import jax, jax.numpy as jnp
        import numpy as np
        H_CONST = 1.0

        def binarize(w, H=H_CONST):
            return jnp.where(w >= 0, H, -H).astype(w.dtype)
        Wb = binarize(kernel)
        out = jax.lax.conv_general_dilated(x, Wb, window_strides=(1, 1), padding='SAME', dimension_numbers=('NHWC', 'HWIO', 'NHWC'))
        return out

    def _L1_ffn_ref(x, W_gat, att_src, att_dst, b_gat, ln_gamma, ln_beta, W1, b1, W2, b2, edge_index):
        import jax, jax.numpy as jnp
        import numpy as np
        B, N, D = (16, 1024, 64)
        NUM_EXPERTS, TOP_K, HEADS = (4, 2, 4)
        N_EDGES = 262144
        LN_EPS = 1e-05

        def _layernorm(x, g, b):
            mu = x.mean(-1, keepdims=True)
            var = ((x - mu) ** 2).mean(-1, keepdims=True)
            return (x - mu) * jax.lax.rsqrt(var + LN_EPS) * g + b

        def _forward(x, edge_index, W_gat, att_src, att_dst, b_gat, ln_gamma, ln_beta, W1, b1, W2, b2):
            Bc, Nc, Dc = x.shape
            M = Bc * Nc
            x_flat = x.reshape(M, Dc)
            h = (x_flat @ W_gat).reshape(M, HEADS, NUM_EXPERTS)
            loops = jnp.arange(M, dtype=edge_index.dtype)
            src = jnp.concatenate([edge_index[0], loops])
            dst = jnp.concatenate([edge_index[1], loops])
            a_src = (h * att_src).sum(-1)
            a_dst = (h * att_dst).sum(-1)
            e = jax.nn.leaky_relu(a_src[src] + a_dst[dst], negative_slope=0.2)
            e_max = jax.ops.segment_max(e, dst, num_segments=M)
            ee = jnp.exp(e - e_max[dst])
            denom = jax.ops.segment_sum(ee, dst, num_segments=M)
            alpha = ee / (denom[dst] + 1e-16)
            msg = h[src] * alpha[:, :, None]
            agg = jax.ops.segment_sum(msg, dst, num_segments=M).reshape(M, HEADS * NUM_EXPERTS) + b_gat
            scores = _layernorm(agg, ln_gamma, ln_beta).reshape(M, HEADS, NUM_EXPERTS).mean(1)
            scores = scores.reshape(Bc, Nc, NUM_EXPERTS)
            topk_s, topk_i = jax.lax.top_k(scores, TOP_K)
            w = jax.nn.softmax(topk_s, axis=-1)
            out = jnp.zeros_like(x)
            for ei in range(NUM_EXPERTS):
                g = jnp.where(topk_i == ei, w, 0.0).sum(-1)
                hh = jax.nn.gelu(x @ W1[ei] + b1[ei], approximate=False)
                out = out + g[..., None] * (hh @ W2[ei] + b2[ei])
            return out
        return _forward(x, edge_index, W_gat, att_src, att_dst, b_gat, ln_gamma, ln_beta, W1, b1, W2, b2)

    def _gn(v, G=32, eps=1e-05):
        B_, H_, W_, C_ = v.shape
        g = v.reshape(B_, H_, W_, G, C_ // G)
        m = jnp.mean(g, axis=(1, 2, 4), keepdims=True)
        s = jnp.var(g, axis=(1, 2, 4), keepdims=True)
        return ((g - m) / jnp.sqrt(s + eps)).reshape(v.shape)

    def _ln_c(v, eps=1e-06):
        m = jnp.mean(v, axis=-1, keepdims=True)
        s = jnp.var(v, axis=-1, keepdims=True)
        return (v - m) / jnp.sqrt(s + eps)

    def _ln_t(v, eps=1e-05):
        m = jnp.mean(v, axis=-1, keepdims=True)
        s = jnp.var(v, axis=-1, keepdims=True)
        return (v - m) / jnp.sqrt(s + eps)

    def _to_tokens(v):
        B_, H_, W_, C_ = v.shape
        return v.reshape(B_, H_ * W_, C_)

    def _from_tokens(t, like):
        return t.reshape(like.shape)
    x = x + _L0_conv_ref(_ln_c(x), L0_conv_gamma)
    t = _to_tokens(x)
    t = t + _L0_ffn_ref(_ln_t(t), L0_ffn_gate_w, L0_ffn_gate_b, L0_ffn_w1, L0_ffn_w2, L0_ffn_w3)
    x = _from_tokens(t, x)
    x = x + _L1_conv_ref(_ln_c(x), L1_conv_kernel)
    t = _to_tokens(x)
    t = t + _L1_ffn_ref(_ln_t(t), L1_ffn_W_gat, L1_ffn_att_src, L1_ffn_att_dst, L1_ffn_b_gat, L1_ffn_ln_gamma, L1_ffn_ln_beta, L1_ffn_W1, L1_ffn_b1, L1_ffn_W2, L1_ffn_b2, L1_ffn_edge_index)
    x = _from_tokens(t, x)
    return x

_drawn_inputs = setup_inputs


def setup_inputs(seed=0):
    import zlib

    import numpy as np

    out = dict(_drawn_inputs(seed))
    spreads = {'L0_ffn_gate_b': (0.0, 0.8),
     'L1_ffn_b_gat': (0.0, 0.8),
     'L1_ffn_ln_gamma': (1.0, 0.6),
     'L1_ffn_ln_beta': (0.0, 0.8),
     'L1_ffn_b1': (0.0, 0.8),
     'L1_ffn_b2': (0.0, 2.0)}
    factors = {'L0_ffn_gate_w': 8.0,
     'L0_ffn_w1': 8.0,
     'L0_ffn_w2': 8.0,
     'L0_ffn_w3': 8.0,
     'L1_ffn_W_gat': 8.0,
     'L1_ffn_att_src': 8.0,
     'L1_ffn_att_dst': 8.0,
     'L1_ffn_W1': 8.0,
     'L1_ffn_W2': 8.0}
    for name, (base, spread) in spreads.items():
        noise = np.random.default_rng([zlib.crc32(name.encode()), seed]).standard_normal(out[name].shape)
        drawn = base * np.exp(spread * noise) if base else spread * noise
        out[name] = jnp.asarray(drawn.astype(out[name].dtype))
    for name, factor in factors.items():
        out[name] = (out[name] * factor).astype(out[name].dtype)
    return out
```

```python
from contextlib import ExitStack

import concourse.bass as bass
from concourse import mybir

F32 = mybir.dt.float32
I32 = mybir.dt.int32
U32 = mybir.dt.uint32
ALU = mybir.AluOpType
ACT = mybir.ActivationFunctionType
X = mybir.AxisListType.X

P = 128
B, HW_, C = 8, 1024, 64
N = B * HW_
T = N // P
E = 262144
EC = E // P
SRC_BITS = 13
KEY_ONE = 1 << 27
BLK = 64
ROW = 24
HEADS, NE = 4, 4
Q = HEADS * (NE + 1)
FAR = -3.0e38
NONE = -1.0e30


class Steps:

    def __init__(self, engine, sem):
        self.engine, self.sem, self.n = engine, sem, 0

    def mark(self, ins):
        ins.then_inc(self.sem, 1)
        self.n += 1
        return self.n

    def link(self, ins):
        self.mark(ins)
        self.engine.wait_ge(self.sem, self.n)


class Arena:

    def __init__(self, nc, ctx, phase):
        self.nc, self.ctx, self.phase = nc, ctx, phase

    def sb(self, name, shape, dt=F32):
        return self.ctx.enter_context(self.nc.sbuf_tensor(f"{self.phase}_{name}", shape, dt))

    def ps(self, name, shape):
        return self.ctx.enter_context(self.nc.psum_tensor(f"{self.phase}_{name}", shape, F32))

    def sem(self, name):
        return self.nc.alloc_semaphore(f"{self.phase}_{name}")


def constants(nc, ident, p_sign):
    with ExitStack() as ctx:
        a = Arena(nc, ctx, "constants")
        part = a.sb("part", [P, 1], I32)
        bit = a.sb("bit", [P, 1])
        made = a.sem("constants_made")
        signs = a.sem("signs_made")
        block = ctx.enter_context(nc.Block())

        @block.gpsimd
        def _(pool):
            st = Steps(pool, made)
            st.link(pool.memset(ident[:, :], 0.0))
            st.link(pool.affine_select(out=ident[:, :], in_=ident[:, :], compare_op=ALU.not_equal, fill=1.0,
                                       base=0, pattern=[[-1, P]], channel_multiplier=1))
            st.link(pool.iota(part[:, :], pattern=[[0, 1]], base=0, channel_multiplier=1))

        @block.vector
        def _(dve):
            dve.wait_ge(made, 3)
            st = Steps(dve, signs)
            st.link(dve.tensor_scalar(part[:, :], part[:, :], 1, None, ALU.bitwise_and))
            st.link(dve.tensor_copy(bit[:, :], part[:, :]))
            st.mark(dve.tensor_scalar(p_sign[:, 0:1], bit[:, :], -2.0, 1.0, ALU.mult, ALU.add))
            st.link(dve.tensor_scalar(p_sign[:, 1:2], bit[:, :], 2.0, -1.0, ALU.mult, ALU.add))


def sort_edges(nc, edge_index, ident, p_sign, sorted_keys, pivots, cleared):
    with ExitStack() as ctx:
        a = Arena(nc, ctx, "sort_edges")
        src_i = a.sb("src_i", [P, EC], I32)
        dst_i = a.sb("dst_i", [P, EC], I32)
        keys = [a.sb("keys_a", [P, EC]), a.sb("keys_b", [P, EC])]
        turned = a.ps("turned", [P, EC])
        loaded = a.sem("edges_loaded")
        sorting = a.sem("sort_steps")
        turns = a.sem("banks_turned")
        copies = a.sem("banks_copied")
        stored = a.sem("keys_stored")
        zeros = a.sb("zeros", [P, 4096])
        zeros_made = a.sem("zeros_made")
        clearing = a.sem("clearing")
        BANK = 512
        NB = EC // BANK
        plan = {"turn_at": [], "done": 0}

        def halves(buf, j):
            v = buf[:, :].rearrange("p (b h d) -> p b h d", h=2, d=1 << j)
            return v[:, :, 0, :], v[:, :, 1, :]

        block = ctx.enter_context(nc.Block())

        @block.vector
        def _(dve):
            st = Steps(dve, sorting)
            cur = 0

            def exchange(j):
                nonlocal cur
                lo, hi = halves(keys[cur], j)
                to_lo, to_hi = halves(keys[1 - cur], j)
                st.mark(dve.tensor_tensor(to_lo, lo, hi, ALU.min))
                st.link(dve.tensor_tensor(to_hi, lo, hi, ALU.max))
                cur = 1 - cur

            def exchange_first(j, last=False):
                nonlocal cur
                if last:
                    lo, hi = halves(keys[cur], j)
                    to_lo, to_hi = halves(keys[1 - cur], j)
                    st.mark(dve.scalar_tensor_tensor(to_lo, hi, -1.0, lo, ALU.mult, ALU.min))
                    st.link(dve.scalar_tensor_tensor(to_hi, hi, -1.0, lo, ALU.mult, ALU.max))
                else:
                    v = keys[cur][:, :].rearrange("p (b r h d) -> p b r h d", r=2, h=2, d=1 << j)
                    w = keys[1 - cur][:, :].rearrange("p (b r h d) -> p b r h d", r=2, h=2, d=1 << j)
                    for r in range(2):
                        lo, hi = v[:, :, r, 0, :], v[:, :, r, 1, :]
                        flip, keep = (hi, lo) if r == 0 else (lo, hi)
                        st.mark(dve.scalar_tensor_tensor(w[:, :, r, 0, :], flip, -1.0, keep, ALU.mult, ALU.min))
                        ins = dve.scalar_tensor_tensor(w[:, :, r, 1, :], flip, -1.0, keep, ALU.mult, ALU.max)
                        st.mark(ins)
                    dve.wait_ge(sorting, st.n)
                cur = 1 - cur

            def turn():
                nonlocal cur
                plan["turn_at"].append((st.n, cur))
                cur = 1 - cur
                dve.wait_ge(copies, NB * len(plan["turn_at"]))

            dve.wait_ge(loaded, 32)
            st.mark(dve.tensor_scalar(src_i[:, :], src_i[:, :], float(N - 1), None, ALU.min))
            st.link(dve.tensor_scalar(dst_i[:, :], dst_i[:, :], float(N), None, ALU.min))
            st.link(dve.scalar_tensor_tensor(src_i[:, :], dst_i[:, :], SRC_BITS, src_i[:, :],
                                             ALU.logical_shift_left, ALU.bitwise_or))
            key_i = keys[0][:, :].bitcast(I32)
            st.link(dve.tensor_scalar(key_i, src_i[:, :], KEY_ONE, None, ALU.bitwise_or))
            odd = keys[0][:, 1::2]
            st.link(dve.tensor_scalar(odd, odd, -1.0, None, ALU.mult))
            for k in range(1, 19):
                if k == 11:
                    lo, hi = halves(keys[cur], 10)
                    st.mark(dve.tensor_scalar(lo, lo, p_sign[:, 0:1], None, ALU.mult))
                    st.link(dve.tensor_scalar(hi, hi, p_sign[:, 1:2], None, ALU.mult))
                    exchange(10)
                elif k > 11:
                    turn()
                    exchange_first(k - 12, last=k == 18)
                    for j in range(k - 13, -1, -1):
                        exchange(j)
                    turn()
                    exchange(10)
                else:
                    exchange_first(k - 1)
                for j in range(min(k - 1, 10) - 1, -1, -1):
                    exchange(j)
            plan["done"] = (st.n, cur)

        @block.tensor
        def _(pe):
            for n, (step, cur) in enumerate(plan["turn_at"]):
                pe.wait_ge(sorting, step)
                if n:
                    pe.wait_ge(copies, NB * n)
                for b in range(NB):
                    for t in range(b * 4, b * 4 + 4):
                        ins = pe.transpose(turned[:, t * P:(t + 1) * P], keys[cur][:, t * P:(t + 1) * P], ident[:, :])
                    ins.then_inc(turns, 1)

        @block.scalar
        def _(act):
            for n, (step, cur) in enumerate(plan["turn_at"]):
                for b in range(NB):
                    act.wait_ge(turns, NB * n + b + 1)
                    act.activation(keys[1 - cur][:, b * BANK:(b + 1) * BANK], turned[:, b * BANK:(b + 1) * BANK],
                                   ACT.Copy).then_inc(copies, 1)

        @block.gpsimd
        def _(pool):
            pool.memset(zeros[:, :], 0.0).then_inc(zeros_made, 1)

        @block.sync
        def _(sp):
            sp.dma_start(src_i[:, :], edge_index[0, :].rearrange("(p c) -> p c", p=P)).then_inc(loaded, 16)
            sp.dma_start(dst_i[:, :], edge_index[1, :].rearrange("(p c) -> p c", p=P)).then_inc(loaded, 16)
            sp.wait_ge(zeros_made, 1)
            for flat in cleared:
                for piece in range(flat.shape[0] // (P * 4096)):
                    sp.dma_start(flat[piece * P * 4096:(piece + 1) * P * 4096].rearrange("(p c) -> p c", p=P), zeros[:, :])\
                        .then_inc(clearing, 16)
            sp.wait_ge(clearing, 16 * sum(flat.shape[0] // (P * 4096) for flat in cleared))
            n, cur = plan["done"]
            sp.wait_ge(sorting, n)
            sp.dma_start(sorted_keys.rearrange("(p c) -> p c", p=P), keys[cur][:, :]).then_inc(stored, 16)
            sp.dma_start(pivots.rearrange("(p c) -> p c", p=P), keys[cur][:, BLK - 1::BLK],
                         allow_slow_non_contiguous=True).then_inc(stored, 16)
            sp.wait_ge(stored, 32)


def per_channel(v, n):
    return v.unsqueeze(2).to_broadcast([v.shape[0], v.shape[1], n])


class Norm:

    def __init__(self, a, name, groups, width, eps):
        self.groups, self.width, self.eps = groups, width, eps
        self.squares = a.sb(name + "_squares", [P, groups, width])
        self.mean = a.sb(name + "_mean", [P, groups])
        self.var = a.sb(name + "_var", [P, groups])
        self.root = a.sb(name + "_root", [P, groups])
        self.rstd = a.sb(name + "_rstd", [P, groups])
        self.var_ready = a.sem(name + "_var_ready")
        self.root_ready = a.sem(name + "_root_ready")

    def vector(self, dve, st, y, x, nth, y_ready):
        w = self.width
        st.link(dve.tensor_reduce(self.mean[:, :], x, X, ALU.add))
        st.link(dve.tensor_scalar(self.mean[:, :], self.mean[:, :], -1.0 / w, None, ALU.mult))
        st.link(dve.tensor_tensor(y, x, per_channel(self.mean[:, :], w), ALU.add))
        st.link(dve.tensor_tensor(self.squares[:, :, :], y, y, ALU.mult))
        st.link(dve.tensor_reduce(self.var[:, :], self.squares[:, :, :], X, ALU.add))
        dve.tensor_scalar(self.var[:, :], self.var[:, :], 1.0 / w, self.eps, ALU.mult, ALU.add)\
            .then_inc(self.var_ready, 1)
        dve.wait_ge(self.root_ready, nth + 1)
        st.link(dve.reciprocal(self.rstd[:, :], self.root[:, :]))
        dve.tensor_tensor(y, y, per_channel(self.rstd[:, :], w), ALU.mult).then_inc(y_ready, 1)
        dve.wait_ge(y_ready, nth + 1)

    def scalar(self, act, nth):
        act.wait_ge(self.var_ready, nth + 1)
        act.activation(self.root[:, :], self.var[:, :], ACT.Sqrt).then_inc(self.root_ready, 1)


def wait_apart(engine, sem, value, spare):
    register, met, least = spare
    engine.reg_mov(register, value)
    engine.wait_ge(met, least)
    engine.wait_ge(sem, register)


class LoopSteps:

    def __init__(self, engine, sem, i, per):
        self.engine, self.sem, self.i, self.per, self.n = engine, sem, i, per, 0

    def mark(self, ins):
        ins.then_inc(self.sem, 1)
        self.n += 1

    def link(self, ins):
        self.mark(ins)
        self.engine.wait_ge(self.sem, self.i * self.per + self.n)

    def link_apart(self, ins, spare):
        self.mark(ins)
        wait_apart(self.engine, self.sem, self.i * self.per + self.n, spare)

    def end(self):
        assert self.n == self.per, (self.n, self.per)


def top_two(dve, st, a, name, values, G, K):
    order = a.sb(name + "_order", [P, K])
    pick = a.sb(name + "_pick", [P, G, K])
    rest = a.sb(name + "_rest", [P, G, K])
    best = a.sb(name + "_best", [P, G])
    masks = [a.sb(name + f"_mask{n}", [P, G, K]) for n in range(2)]
    tops = [a.sb(name + f"_top{n}", [P, G]) for n in range(2)]
    rank = order[:, :].unsqueeze(1).to_broadcast([P, G, K])
    for k in range(K):
        st.mark(dve.memset(order[:, k:k + 1], float(K - k)))
    for n in range(2):
        now = values if n == 0 else rest[:, :, :]
        st.link(dve.tensor_reduce(tops[n][:, :], now, X, ALU.max))
        st.link(dve.tensor_tensor(pick[:, :, :], now, per_channel(tops[n][:, :], K), ALU.is_equal))
        st.link(dve.tensor_tensor(pick[:, :, :], pick[:, :, :], rank, ALU.mult))
        st.link(dve.tensor_reduce(best[:, :], pick[:, :, :], X, ALU.max))
        st.link(dve.tensor_tensor(masks[n][:, :, :], rank, per_channel(best[:, :], K), ALU.is_equal))
        if n == 0:
            st.link(dve.scalar_tensor_tensor(rest[:, :, :], masks[0][:, :, :], FAR, values, ALU.mult, ALU.add))
    return masks, tops


def two_weights(dve, st, a, name, out, tops, masks, gap, gap_exp, gap_ready, exp_ready):
    G, K = out.shape[1], out.shape[2]
    w = [a.sb(name + f"_w{n}", [P, G]) for n in range(2)]
    dve.tensor_tensor(gap[:, :], tops[1][:, :], tops[0][:, :], ALU.subtract).then_inc(gap_ready, 1)
    dve.wait_ge(exp_ready, 1)
    st.link(dve.tensor_scalar(w[1][:, :], gap_exp[:, :], 1.0, None, ALU.add))
    st.link(dve.reciprocal(w[0][:, :], w[1][:, :]))
    st.link(dve.tensor_tensor(w[1][:, :], w[0][:, :], gap_exp[:, :], ALU.mult))
    st.mark(dve.tensor_tensor(masks[0][:, :, :], masks[0][:, :, :], per_channel(w[0][:, :], K), ALU.mult))
    st.link(dve.tensor_tensor(masks[1][:, :, :], masks[1][:, :, :], per_channel(w[1][:, :], K), ALU.mult))
    st.link(dve.tensor_tensor(out, masks[0][:, :, :], masks[1][:, :, :], ALU.add))


TB = T // B


def attention(nc, x, gamma, x_sb, yT, ident):
    with ExitStack() as ctx:
        a = Arena(nc, ctx, "attention")
        y = a.sb("y", [P, TB, C])
        y1 = a.sb("y1", [P, TB, C])
        aT = a.sb("aT", [C, TB * P])
        gam = a.sb("gam", [P, 1])
        top = a.sb("top", [C, 1])
        probs = a.sb("probs", [C, C])
        total = a.sb("total", [C, 1])
        part = a.sb("part", [C, 1])
        gram = a.ps("gram", [C, 512])
        mix = a.ps("mix", [P, TB * C])
        turned = a.ps("turned", [C, TB * P])
        turned1 = a.ps("turned1", [C, TB * P])
        n0 = Norm(a, "n0", TB, C, 1e-6)
        n1 = Norm(a, "n1", TB, C, 1e-5)
        x_in = a.sem("x_in")
        gam_in = a.sem("gam_in")
        steps = a.sem("dve_steps")
        y_ready = a.sem("y_ready")
        y_turned = a.sem("y_turned")
        aT_ready = a.sem("aT_ready")
        gram_ready = a.sem("gram_ready")
        shift_ready = a.sem("shift_ready")
        exp_ready = a.sem("exp_ready")
        probs_ready = a.sem("probs_ready")
        mix_ready = a.sem("mix_ready")
        y1_ready = a.sem("y1_ready")
        y1_turned = a.sem("y1_turned")
        y1_copied = a.sem("y1_copied")
        block = ctx.enter_context(nc.Block())

        @block.sync
        def _(sp):
            sp.dma_start(gam[:, :], gamma.to_broadcast([P, 1])).then_inc(gam_in, 16)
            with nc.allow_non_contiguous_dma(reason="256 B rows"):
                sp.dma_start(x_sb[:, :, :], x.rearrange("b (t r) w c -> (r w) (b t) c", t=TB)).then_inc(x_in, 16)

        @block.vector
        def _(dve):
            dve.wait_ge(gam_in, 16)
            dve.wait_ge(x_in, 16)
            spare = dve.alloc_register(f"dve_spare_{a.phase}"), x_in, 16
            with dve.Fori(0, B) as b:
                st = LoopSteps(dve, steps, b, 15)
                xb = x_sb[:, bass.ds(b * TB, TB), :]
                n0.vector(dve, st, y[:, :, :], xb, b, y_ready)
                st.link(dve.tensor_tensor(xb, xb, y[:, :, :], ALU.add))
                dve.wait_ge(gram_ready, b + 1)
                dve.tensor_reduce(top[:, :], gram[:, 0:C], X, ALU.max, negate=True).then_inc(shift_ready, 1)
                dve.wait_ge(exp_ready, b + 1)
                st.link(dve.reciprocal(part[:, :], total[:, :]))
                dve.tensor_scalar(probs[:, :], probs[:, :], part[:, 0:1], None, ALU.mult).then_inc(probs_ready, 1)
                dve.wait_ge(mix_ready, b + 1)
                st.link_apart(dve.scalar_tensor_tensor(xb, mix[:, :].rearrange("p (t c) -> p t c", t=TB), gam[:, 0:1],
                                                       xb, ALU.mult, ALU.add), spare)
                n1.vector(dve, st, y1[:, :, :], xb, b, y1_ready)
                dve.wait_ge(y1_turned, b + 1)
                st.end()

        @block.scalar
        def _(act):
            with act.Fori(0, B) as b:
                n0.scalar(act, b)
                act.wait_ge(y_turned, b + 1)
                act.activation(aT[:, :], turned[:, :], ACT.Copy).then_inc(aT_ready, 1)
                act.wait_ge(shift_ready, b + 1)
                act.activation(probs[:, :], gram[:, 0:C], ACT.Exp, bias=top[:, 0:1], accum_out=total[:, :])\
                    .then_inc(exp_ready, 1)
                n1.scalar(act, b)
                act.wait_ge(y1_turned, b + 1)
                act.activation(yT[:, bass.ds(b * TB * P, TB * P)], turned1[:, :], ACT.Copy).then_inc(y1_copied, 1)

        @block.tensor
        def _(pe):
            spare = pe.alloc_register(f"pe_spare_{a.phase}"), gam_in, 16
            with pe.Fori(0, B) as b:
                pe.wait_ge(y_ready, b + 1)
                for t in range(TB):
                    ins = pe.matmul(gram[:, 0:C], y[:, t, :], y[:, t, :], start=(t == 0), stop=(t == TB - 1))
                ins.then_inc(gram_ready, 1)
                for t in range(TB):
                    ins = pe.transpose(turned[:, t * P:(t + 1) * P], y[:, t, :], ident[:, :])
                ins.then_inc(y_turned, 1)
                pe.wait_ge(aT_ready, b + 1)
                pe.wait_ge(probs_ready, b + 1)
                for t in range(TB):
                    ins = pe.matmul(mix[:, t * C:(t + 1) * C], aT[:, t * P:(t + 1) * P], probs[:, :],
                                    start=True, stop=True)
                ins.then_inc(mix_ready, 1)
                wait_apart(pe, y1_ready, b + 1, spare)
                for t in range(TB):
                    ins = pe.transpose(turned1[:, t * P:(t + 1) * P], y1[:, t, :], ident[:, :])
                ins.then_inc(y1_turned, 1)


def gates(nc, gate_w, gate_b, yT, dispatch):
    K = gate_w.shape[1]
    with ExitStack() as ctx:
        a = Arena(nc, ctx, "gates")
        gw = a.sb("gw", [C, K])
        gb = a.sb("gb", [P, K])
        logits = a.sb("logits", [P, T, K])
        gap, gap_exp = a.sb("gap", [P, T]), a.sb("gap_exp", [P, T])
        logit_ps = a.ps("logit_ps", [P, 2, 512])
        loaded = a.sem("gate_in")
        logits_ready = a.sem("logits_ready")
        steps = a.sem("gate_steps")
        gap_ready = a.sem("gap_ready")
        gap_exp_ready = a.sem("gap_exp_ready")
        block = ctx.enter_context(nc.Block())

        @block.sync
        def _(sp):
            sp.dma_start(gw[:, :], gate_w).then_inc(loaded, 16)
            sp.dma_start(gb[:, :], gate_b.partition_broadcast(P)).then_inc(loaded, 16)

        @block.tensor
        def _(pe):
            pe.wait_ge(loaded, 32)
            for t in range(T):
                ins = pe.matmul(logit_ps[:, t // 32, (t % 32) * K:(t % 32 + 1) * K], yT[:, t * P:(t + 1) * P],
                                gw[:, :], start=True, stop=True)
            ins.then_inc(logits_ready, 1)

        @block.vector
        def _(dve):
            st = Steps(dve, steps)
            dve.wait_ge(logits_ready, 1)
            dve.wait_ge(loaded, 32)
            bias = gb[:, :].unsqueeze(1).to_broadcast([P, 32, K])
            for n in range(2):
                st.mark(dve.tensor_tensor(logits[:, 32 * n:32 * n + 32, :],
                                          logit_ps[:, n, :].rearrange("p (t k) -> p t k", k=K), bias, ALU.add))
            dve.wait_ge(steps, st.n)
            masks, tops = top_two(dve, st, a, "gate", logits[:, :, :], T, K)
            two_weights(dve, st, a, "gate", dispatch[:, :, :], tops, masks, gap, gap_exp, gap_ready, gap_exp_ready)

        @block.scalar
        def _(act):
            act.wait_ge(gap_ready, 1)
            act.activation(gap_exp[:, :], gap[:, :], ACT.Exp).then_inc(gap_exp_ready, 1)


def experts(nc, w1, w2, w3, x_sb, yT, dispatch):
    K, H = w1.shape[0], w1.shape[2]
    G = 4 * P
    with ExitStack() as ctx:
        a = Arena(nc, ctx, "experts")
        u1 = a.sb("u1", [C, K, H])
        u2 = a.sb("u2", [C, K, H])
        u3 = a.sb("u3", [H, K, C])
        gated = a.sb("gated", [H, 2, G])
        hidden = a.sb("hidden", [H, K, G])
        scaled = a.sb("scaled", [P, K, C])
        summed = a.sb("summed", [P, C])
        h1 = a.ps("h1", [H, 2, G])
        h2 = a.ps("h2", [H, 2, G])
        outs = a.ps("outs", [P, 2, K * C])
        loaded = a.sem("weights_in")
        steps = a.sem("expert_steps")
        h1_ready = a.sem("h1_ready")
        h2_ready = a.sem("h2_ready")
        gated_ready = a.sem("gated_ready")
        hidden_ready = a.sem("hidden_ready")
        outs_ready = a.sem("outs_ready")
        outs_free = a.sem("outs_free")
        block = ctx.enter_context(nc.Block())

        @block.sync
        def _(sp):
            sp.dma_start(u1[:, :, :], w1.rearrange("e c h -> c e h")).then_inc(loaded, 16)
            sp.dma_start(u2[:, :, :], w2.rearrange("e c h -> c e h")).then_inc(loaded, 16)
            sp.dma_start(u3[:, :, :], w3.rearrange("e h c -> h e c")).then_inc(loaded, 16)

        @block.tensor
        def _(pe):
            pe.wait_ge(loaded, 48)
            spare = pe.alloc_register(f"pe_spare_{a.phase}"), loaded, 48
            with pe.Fori(0, T // 4) as g:
                tokens = yT[:, bass.ds(g * G, G)]
                for e in range(K):
                    if e >= 2:
                        wait_apart(pe, gated_ready, g * K + e - 1, spare)
                    pe.matmul(h1[:, e % 2, :], u1[:, e, :], tokens, start=True, stop=True).then_inc(h1_ready, 1)
                    if e >= 2:
                        wait_apart(pe, hidden_ready, g * K + e - 1, spare)
                    pe.matmul(h2[:, e % 2, :], u2[:, e, :], tokens, start=True, stop=True).then_inc(h2_ready, 1)
                pe.wait_ge(hidden_ready, g * K + K)
                for q in range(4):
                    pe.wait_ge(outs_free, g * 4 + q + 1)
                    for e in range(K):
                        ins = pe.matmul(outs[:, q % 2, e * C:(e + 1) * C], hidden[:, e, q * P:(q + 1) * P],
                                        u3[:, e, :], start=True, stop=True)
                    ins.then_inc(outs_ready, 1)

        @block.scalar
        def _(act):
            with act.Fori(0, T // 4) as g:
                for e in range(K):
                    act.wait_ge(h1_ready, g * K + e + 1)
                    if e >= 2:
                        act.wait_ge(hidden_ready, g * K + e - 1)
                    act.activation(gated[:, e % 2, :], h1[:, e % 2, :], ACT.Silu).then_inc(gated_ready, 1)

        @block.vector
        def _(dve):
            dve.sem_inc(outs_free, 2)
            spare = dve.alloc_register(f"dve_spare_{a.phase}"), loaded, 48
            with dve.Fori(0, T // 4) as g:
                st = LoopSteps(dve, steps, g, 8)
                for e in range(K):
                    dve.wait_ge(gated_ready, g * K + e + 1)
                    dve.wait_ge(h2_ready, g * K + e + 1)
                    dve.tensor_tensor(hidden[:, e, :], gated[:, e % 2, :], h2[:, e % 2, :], ALU.mult)\
                        .then_inc(hidden_ready, 1)
                for q in range(4):
                    dve.wait_ge(outs_ready, g * 4 + q + 1)
                    part = outs[:, q % 2, :].rearrange("p (e c) -> p e c", e=K)
                    weight = dispatch[:, bass.ds(g * 4 + q, 1), :].rearrange("p t k -> p (t k)")
                    dve.tensor_tensor(scaled[:, :, :], part, per_channel(weight, C), ALU.mult).then_inc(outs_free, 1)
                    dve.wait_ge(outs_free, g * 4 + q + 3)
                    st.link(dve.tensor_reduce(summed[:, :], scaled[:, :, :].rearrange("p e c -> p c e"), X, ALU.add))
                    xt = x_sb[:, bass.ds(g * 4 + q, 1), :].rearrange("p t c -> p (t c)")
                    st.link(dve.tensor_tensor(xt, xt, summed[:, :], ALU.add))
                st.end()


def convolve(nc, kernel_w, W_gat, att_src, att_dst, W1, b1, W2, b2, x_sb, eo, h_sb, as_sb, ad_sb, ident):
    S = 32
    PAD = S + 2
    K, H = W1.shape[0], W1.shape[2]
    with ExitStack() as ctx:
        a = Arena(nc, ctx, "convolve")
        y = a.sb("y", [P, TB, C])
        y4 = a.sb("y4", [P, TB, C])
        padded = a.sb("padded", [C, 3, PAD, S])
        y4T = a.sb("y4T", [C, TB * P])
        cw = a.sb("cw", [C, 9, C])
        wg = a.sb("wg", [C, HEADS * NE])
        att = a.sb("att", [P, 2, HEADS * NE])
        u1 = a.sb("u1", [C, K, H])
        ub1 = a.sb("ub1", [H, K])
        u2 = a.sb("u2", [H, K, C])
        ub2 = a.sb("ub2", [P, K * C])
        hidden = a.sb("hidden", [H, K, TB * P])
        products = a.sb("products", [P, TB, HEADS * NE])
        n2 = Norm(a, "n2", TB, C, 1e-6)
        n3 = Norm(a, "n3", TB, C, 1e-5)
        turned = a.ps("turned", [C, TB * P])
        conv = a.ps("conv", [P, TB * C])
        feats = a.ps("feats", [P, 512])
        h1 = a.ps("h1", [H, 2, 512])
        outs = a.ps("outs", [P, 2, 512])
        loaded = a.sem("weights_in")
        signed = a.sem("signs_ready")
        steps = a.sem("dve_steps")
        y_ready = a.sem("y_ready")
        y_turned = a.sem("y_turned")
        padded_ready = a.sem("padded_ready")
        conv_ready = a.sem("conv_ready")
        y4_ready = a.sem("y4_ready")
        y4_turned = a.sem("y4_turned")
        y4T_ready = a.sem("y4T_ready")
        feats_ready = a.sem("feats_ready")
        h1_ready = a.sem("h1_ready")
        hidden_ready = a.sem("hidden_ready")
        outs_ready = a.sem("outs_ready")
        outs_free = a.sem("outs_free")
        block = ctx.enter_context(nc.Block())

        @block.sync
        def _(sp):
            sp.dma_start(cw[:, :, :], kernel_w.rearrange("a b c d -> c (a b) d")).then_inc(loaded, 16)
            sp.dma_start(wg[:, :], W_gat).then_inc(loaded, 16)
            sp.dma_start(att[:, 0, :], att_src.rearrange("h k -> (h k)").partition_broadcast(P)).then_inc(loaded, 16)
            sp.dma_start(att[:, 1, :], att_dst.rearrange("h k -> (h k)").partition_broadcast(P)).then_inc(loaded, 16)
            sp.dma_start(u1[:, :, :], W1.rearrange("e c h -> c e h")).then_inc(loaded, 16)
            with nc.allow_non_contiguous_dma(reason="small bias"):
                sp.dma_start(ub1[:, :], b1.rearrange("e h -> h e")).then_inc(loaded, 16)
            sp.dma_start(u2[:, :, :], W2.rearrange("e h c -> h e c")).then_inc(loaded, 16)
            sp.dma_start(ub2[:, :], b2.rearrange("e c -> (e c)").partition_broadcast(P)).then_inc(loaded, 16)

        @block.vector
        def _(dve):
            dve.wait_ge(loaded, 128)
            st = Steps(dve, signed)
            st.link(dve.tensor_scalar(cw[:, :, :], cw[:, :, :], 0.0, None, ALU.is_ge))
            st.link(dve.tensor_scalar(cw[:, :, :], cw[:, :, :], 2.0, -1.0, ALU.mult, ALU.add))
            st.link(dve.memset(padded[:, :, :, :], 0.0))
            dve.sem_inc(outs_free, 2)
            spare = dve.alloc_register(f"dve_spare_{a.phase}"), signed, 3
            with dve.Fori(0, B) as b:
                st = LoopSteps(dve, steps, b, 18)
                xb = x_sb[:, bass.ds(b * TB, TB), :]
                n2.vector(dve, st, y[:, :, :], xb, b, y_ready)
                dve.wait_ge(conv_ready, b + 1)
                st.link_apart(dve.tensor_tensor(xb, xb, conv[:, :].rearrange("p (t c) -> p t c", t=TB), ALU.add), spare)
                n3.vector(dve, st, y4[:, :, :], xb, b, y4_ready)
                dve.wait_ge(feats_ready, b + 1)
                h = h_sb[:, bass.ds(b * TB, TB), :]
                st.link(dve.tensor_copy(h, feats[:, 0:TB * HEADS * NE].rearrange("p (t k) -> p t k", t=TB)))
                for n, to in enumerate((as_sb, ad_sb)):
                    st.link(dve.tensor_tensor(products[:, :, :], h,
                                              att[:, n, :].unsqueeze(1).to_broadcast([P, TB, HEADS * NE]), ALU.mult))
                    st.link(dve.tensor_reduce(to[:, bass.ds(b * TB, TB), :],
                                              products[:, :, :].rearrange("p t (h k) -> p t h k", k=NE), X, ALU.add))
                for n in range(TB // 2):
                    dve.wait_ge(outs_ready, b * (TB // 2) + n + 1)
                    dve.tensor_tensor(eo[:, bass.ds(b * TB + 2 * n, 2), :],
                                      outs[:, n % 2, :].rearrange("p (t k) -> p t k", t=2),
                                      ub2[:, :].unsqueeze(1).to_broadcast([P, 2, K * C]), ALU.add)\
                        .then_inc(outs_free, 1)
                st.end()

        @block.scalar
        def _(act):
            act.wait_ge(signed, 3)
            with act.Fori(0, B) as b:
                n2.scalar(act, b)
                act.wait_ge(y_turned, b + 1)
                image = turned[:, :].rearrange("c (r w) -> c r w", w=S)
                for w in range(3):
                    left, right = max(1 - w, 0), min(S, S + 1 - w)
                    act.activation(padded[:, w, 1:S + 1, left:right], image[:, :, left + w - 1:right + w - 1],
                                   ACT.Copy).then_inc(padded_ready, 1)
                n3.scalar(act, b)
                act.wait_ge(y4_turned, b + 1)
                act.activation(y4T[:, :], turned[:, :], ACT.Copy).then_inc(y4T_ready, 1)
                for e in range(K):
                    for s in range(2):
                        act.wait_ge(h1_ready, b * 2 * K + 2 * e + s + 1)
                        act.activation(hidden[:, e, s * 512:(s + 1) * 512], h1[:, s, :], ACT.Gelu, bias=ub1[:, e:e + 1])\
                            .then_inc(hidden_ready, 1)

        @block.tensor
        def _(pe):
            pe.wait_ge(signed, 3)
            spare = pe.alloc_register(f"pe_spare_{a.phase}"), signed, 3
            with pe.Fori(0, B) as b:
                wait_apart(pe, y_ready, b + 1, spare)
                for t in range(TB):
                    ins = pe.transpose(turned[:, t * P:(t + 1) * P], y[:, t, :], ident[:, :])
                ins.then_inc(y_turned, 1)
                pe.wait_ge(padded_ready, 3 * b + 3)
                for t in range(TB):
                    for tap in range(9):
                        r, w = 4 * t + tap // 3, tap % 3
                        ins = pe.matmul(conv[:, t * C:(t + 1) * C], padded[:, w, r:r + 4, :], cw[:, tap, :],
                                        start=(tap == 0), stop=(tap == 8))
                ins.then_inc(conv_ready, 1)
                wait_apart(pe, y4_ready, b + 1, spare)
                for t in range(TB):
                    ins = pe.transpose(turned[:, t * P:(t + 1) * P], y4[:, t, :], ident[:, :])
                ins.then_inc(y4_turned, 1)
                pe.wait_ge(y4T_ready, b + 1)
                for t in range(TB):
                    ins = pe.matmul(feats[:, t * HEADS * NE:(t + 1) * HEADS * NE], y4T[:, t * P:(t + 1) * P], wg[:, :],
                                    start=True, stop=True)
                ins.then_inc(feats_ready, 1)
                for e in range(K):
                    for s in range(2):
                        if e:
                            pe.wait_ge(hidden_ready, b * 2 * K + 2 * e + s - 1)
                        pe.matmul(h1[:, s, :], u1[:, e, :], y4T[:, s * 512:(s + 1) * 512], start=True, stop=True)\
                            .then_inc(h1_ready, 1)
                pe.wait_ge(hidden_ready, (b + 1) * 2 * K)
                for n in range(TB // 2):
                    pe.wait_ge(outs_free, b * (TB // 2) + n + 1)
                    for t in range(2 * n, 2 * n + 2):
                        for e in range(K):
                            at = (t % 2) * K * C + e * C
                            ins = pe.matmul(outs[:, n % 2, at:at + C], hidden[:, e, t * P:(t + 1) * P], u2[:, e, :],
                                            start=True, stop=True)
                    ins.then_inc(outs_ready, 1)


def write_table(nc, h_sb, as_sb, ad_sb, rows, table, a_dst):
    with ExitStack() as ctx:
        a = Arena(nc, ctx, "write_table")
        made = a.sem("rows_made")
        stored = a.sem("rows_stored")
        block = ctx.enter_context(nc.Block())

        @block.vector
        def _(dve):
            st = Steps(dve, made)
            st.link(dve.memset(rows[:, :, :], 1.0))
            for h in range(HEADS):
                st.mark(dve.tensor_copy(rows[:, :, h * 5 + 1:h * 5 + 5], h_sb[:, :, h * NE:(h + 1) * NE]))
            st.link(dve.tensor_copy(rows[:, :, Q:ROW], as_sb[:, :, :]))

        @block.sync
        def _(sp):
            sp.wait_ge(made, 6)
            sp.dma_start(table.rearrange("(t p) k -> p t k", p=P), rows[:, :, :]).then_inc(stored, 16)
            sp.dma_start(a_dst.rearrange("(t p) k -> p t k", p=P), ad_sb[:, :, :]).then_inc(stored, 16)
            sp.wait_ge(stored, 32)


def gather(pool, to, rows, index, done, bound=None):
    where = bass.IndirectOffsetOnAxis(ap=index, axis=0)
    if bound is None:
        pool.indirect_dma_start(to, None, rows, where).then_inc(done, 16)
    else:
        pool.indirect_dma_start(to, None, rows, where, bounds_check=bound, oob_is_err=False).then_inc(done, 16)


def search(nc, keys_dram, pivots_dram, ends_dram, blocks_i, ends_f, starts_f):
    L = 64
    with ExitStack() as ctx:
        a = Arena(nc, ctx, "search")
        node = a.sb("node", [P, T], I32)
        bound = a.sb("bound", [P, T], I32)
        tops = a.sb("tops", [P, L])
        found = a.sb("found", [P, T, L])
        less = a.sb("less", [P, T, L])
        counts = [a.sb(f"count{n}", [P, T]) for n in range(3)]
        at = a.sb("at", [P, T])
        index = [a.sb(f"index{n}", [P, T], U32) for n in range(2)]
        zero = a.sb("zero", [1, 1])
        kept = a.sb("kept", [P, 1])
        kept_i = a.sb("kept_i", [P, 1], I32)
        made = a.sem("nodes_made")
        tops_in = a.sem("tops_in")
        steps = a.sem("search_steps")
        level = a.sem("index_ready")
        rows_in = [a.sem(f"rows_in{n}") for n in range(2)]
        ends_ready = a.sem("ends_ready")
        stored = a.sem("ends_stored")
        reloaded = a.sem("ends_reloaded")
        block = ctx.enter_context(nc.Block())

        @block.gpsimd
        def _(pool):
            pool.iota(node[:, :], pattern=[[P, T]], base=1, channel_multiplier=1).then_inc(made, 1)
            for n, table in enumerate((pivots_dram, keys_dram)):
                pool.wait_ge(level, n + 1)
                for t in range(T):
                    gather(pool, found[:, t, :], table.rearrange("(r c) -> r c", c=L), index[n][:, t:t + 1], rows_in[n])

        @block.vector
        def _(dve):
            st = Steps(dve, steps)
            dve.wait_ge(made, 1)
            st.link(dve.tensor_scalar(bound[:, :], node[:, :], SRC_BITS, KEY_ONE, ALU.logical_shift_left,
                                      ALU.bitwise_or))
            limit = per_channel(bound[:, :].bitcast(F32), L)
            dve.wait_ge(tops_in, 16)
            st.link(dve.tensor_tensor(less[:, :, :], tops[:, :].unsqueeze(1).to_broadcast([P, T, L]), limit, ALU.is_lt))
            for n in range(3):
                st.link(dve.tensor_reduce(counts[n][:, :], less[:, :, :], X, ALU.add))
                if n == 0:
                    st.link(dve.tensor_scalar(at[:, :], counts[0][:, :], L - 1.0, None, ALU.min))
                elif n == 1:
                    st.link(dve.tensor_scalar(counts[1][:, :], counts[1][:, :], L - 1.0, None, ALU.min))
                    st.link(dve.scalar_tensor_tensor(at[:, :], at[:, :], float(L), counts[1][:, :], ALU.mult, ALU.add))
                if n < 2:
                    dve.tensor_copy(index[n][:, :], at[:, :]).then_inc(level, 1)
                    dve.wait_ge(rows_in[n], 16 * T)
                    st.link(dve.tensor_tensor(less[:, :, :], found[:, :, :], limit, ALU.is_lt))
            dve.scalar_tensor_tensor(ends_f[:, :], at[:, :], float(L), counts[2][:, :], ALU.mult, ALU.add)\
                .then_inc(ends_ready, 1)
            dve.memset(zero[:, :], 0.0).then_inc(ends_ready, 1)
            dve.wait_ge(reloaded, 32)
            st.link(dve.tensor_scalar(kept[:, :], kept[:, :], 1.0, float(P * BLK - 1), ALU.max, ALU.add))
            st.link(dve.tensor_copy(kept_i[:, :], kept[:, :]))
            st.link(dve.tensor_scalar(blocks_i[:, :], kept_i[:, :], 13, None, ALU.logical_shift_right))

        @block.sync
        def _(sp):
            with nc.allow_non_contiguous_dma(reason="a value per node"):
                sp.dma_start(tops[:, :], pivots_dram.rearrange("(i c) -> c i", c=L)[L - 1, :].partition_broadcast(P))\
                    .then_inc(tops_in, 16)
                sp.wait_ge(ends_ready, 2)
                sp.dma_start(ends_dram[1:N + 1].rearrange("(t p) -> p t", p=P), ends_f[:, :]).then_inc(stored, 16)
                sp.dma_start(ends_dram[0:1].rearrange("(a b) -> a b", a=1), zero[:, :]).then_inc(stored, 16)
                sp.wait_ge(stored, 32)
                sp.dma_start(starts_f[:, :], ends_dram[0:N].rearrange("(t p) -> p t", p=P)).then_inc(reloaded, 16)
                sp.dma_start(kept[:, :], ends_dram[N:N + 1].partition_broadcast(P)).then_inc(reloaded, 16)
                sp.wait_ge(reloaded, 32)


def spread(nc, keys_dram, ends_f, starts_f, ad_sb, a_dst_dram, edge_ad_dram, blocks_i, chunk_f, first_dst):
    with ExitStack() as ctx:
        a = Arena(nc, ctx, "spread")
        empty = a.sb("empty", [P, T])
        to_f = a.sb("to_f", [P, T])
        to = a.sb("to", [P, T], U32)
        part = a.sb("part", [P, 1], I32)
        part_f = a.sb("part_f", [P, 1])
        blocks_f = a.sb("blocks_f", [P, 1])
        chunk_i = a.sb("chunk_i", [P, 1], U32)
        keys = a.sb("keys", [P, BLK], I32)
        dst = a.sb("dst", [P, 1], I32)
        known = a.sb("known", [P, 1])
        first_i = a.sb("first_i", [P, 1], U32)
        first_ad = a.sb("first_ad", [P, HEADS])
        cut_f = a.sb("cut_f", [P, 1])
        cut_i = a.sb("cut_i", [P, 1], U32)
        steps = a.sem("spread_steps")
        made = a.sem("made")
        keys_in = a.sem("keys_in")
        ad_in = a.sem("ad_in")
        written = a.sem("edge_ad_written")
        block = ctx.enter_context(nc.Block())

        @block.vector
        def _(dve):
            st = Steps(dve, steps)
            st.link(dve.tensor_tensor(empty[:, :], starts_f[:, :], ends_f[:, :], ALU.is_equal))
            st.link(dve.scalar_tensor_tensor(to_f[:, :], empty[:, :], float(2 * E), starts_f[:, :], ALU.mult, ALU.add))
            st.link(dve.tensor_copy(to[:, :], to_f[:, :]))
            dve.wait_ge(made, 1)
            st.mark(dve.tensor_copy(part_f[:, :], part[:, :]))
            st.link(dve.tensor_copy(blocks_f[:, :], blocks_i[:, :]))
            st.link(dve.tensor_tensor(chunk_f[:, :], part_f[:, :], blocks_f[:, :], ALU.mult))
            st.link(dve.tensor_copy(chunk_i[:, :], chunk_f[:, :]))
            dve.wait_ge(keys_in, 16)
            st.link(dve.tensor_scalar(dst[:, :], keys[:, 0:1], SRC_BITS, 2 * N - 1, ALU.logical_shift_right,
                                      ALU.bitwise_and))
            st.link(dve.tensor_copy(first_dst[:, :], dst[:, :]))
            st.link(dve.tensor_scalar(known[:, :], first_dst[:, :], N - 1.0, None, ALU.min))
            st.link(dve.tensor_copy(first_i[:, :], known[:, :]))
            st.link(dve.tensor_scalar(cut_f[:, :], chunk_f[:, :], float(BLK), None, ALU.mult))
            st.link(dve.tensor_copy(cut_i[:, :], cut_f[:, :]))

        @block.gpsimd
        def _(pool):
            pool.iota(part[:, :], pattern=[[0, 1]], base=0, channel_multiplier=1).then_inc(made, 1)
            pool.wait_ge(steps, 3)
            for t in range(T):
                pool.indirect_dma_start(edge_ad_dram, bass.IndirectOffsetOnAxis(ap=to[:, t:t + 1], axis=0),
                                        ad_sb[:, t, :], None, bounds_check=E - 1, oob_is_err=False)\
                    .then_inc(written, 16)
            pool.wait_ge(steps, 7)
            gather(pool, keys[:, :].bitcast(F32), keys_dram.rearrange("(r c) -> r c", c=BLK), chunk_i[:, :], keys_in)
            pool.wait_ge(steps, 13)
            gather(pool, first_ad[:, :], a_dst_dram, first_i[:, :], ad_in)
            pool.wait_ge(ad_in, 16)
            pool.wait_ge(written, 16 * T)
            pool.indirect_dma_start(edge_ad_dram, bass.IndirectOffsetOnAxis(ap=cut_i[:, :], axis=0),
                                    first_ad[:, :], None).then_inc(written, 16)
            pool.wait_ge(written, 16 * (T + 1))


def edge_loop(nc, keys_dram, table, edge_ad_dram, edge_rows_dram, blocks_i, chunk_f, last_dst, state):
    W = BLK // 2
    W1 = W + 1
    with ExitStack() as ctx:
        a = Arena(nc, ctx, "edges")

        def slots(name, shape, dt=F32):
            return [a.sb(f"{name}{s}", shape, dt) for s in range(2)]

        def slot_sems(name):
            return [a.sem(f"{name}{s}") for s in range(2)]

        keys = slots("keys", [P, W], I32)
        dst = a.sb("dst", [P, W], I32)
        src = slots("src", [P, W], I32)
        dst_f = slots("dst_f", [P, W1])
        keep = slots("keep", [P, HEADS, W1])
        fresh = slots("fresh", [P, HEADS, W1])
        key_f = slots("key_f", [P, 1])
        key_i = slots("key_i", [P, 1], U32)
        out_f = slots("out_f", [P, 1])
        out_i = slots("out_i", [P, 1], U32)
        ad_i = slots("ad_i", [P, 1], U32)
        rows = slots("rows", [P, W, ROW])
        ad = slots("ad", [P, W, HEADS])
        out = slots("out", [P, W, ROW])
        starts = a.sb("starts", [P, HEADS, W1])
        held = a.sb("held", [P, HEADS, W1])
        raw = a.sb("raw", [P, HEADS, W])
        score = a.sb("score", [P, HEADS, W1])
        tops = a.sb("tops", [P, HEADS, W1])
        before = a.sb("before", [P, HEADS, W])
        gaps = a.sb("gaps", [P, 2, HEADS, W])
        weight = a.sb("weight", [P, HEADS, W])
        decay = a.sb("decay", [P, Q, W1])
        terms = a.sb("terms", [P, Q, W1])
        sums = a.sb("sums", [P, Q, W1])
        key_i_ready = slot_sems("key_i_ready")
        keys_in = slot_sems("keys_in")
        ad_in = slot_sems("ad_in")
        src_ready = slot_sems("src_ready")
        rows_in = slot_sems("rows_in")
        summed = slot_sems("summed")
        copied = slot_sems("copied")
        stored = slot_sems("stored")
        steps = a.sem("edge_steps")
        first = a.sem("first_steps")
        gaps_ready = a.sem("gaps_ready")
        weights_ready = a.sem("weights_ready")
        block = ctx.enter_context(nc.Block())
        key_rows = keys_dram.rearrange("(r c) -> r c", c=W)
        ad_rows = edge_ad_dram.rearrange("(r c) k -> r (c k)", c=W)
        out_rows = edge_rows_dram.rearrange("(r c) k -> r (c k)", c=W)
        LAST = E // W - 1

        def flat(v):
            return v[:, :, :].rearrange("p h w -> p (h w)")

        def wide(v):
            return v.unsqueeze(1).to_broadcast([P, HEADS, W])

        def prepare(dve, st, s):
            st.link(dve.tensor_scalar(key_f[s][:, :], key_f[s][:, :], 2.0, None, ALU.add))
            dve.tensor_copy(key_i[s][:, :], key_f[s][:, :]).then_inc(key_i_ready[s], 1)
            st.link(dve.tensor_scalar(dst[:, :], keys[s][:, :], SRC_BITS, 2 * N - 1, ALU.logical_shift_right,
                                      ALU.bitwise_and))
            dve.tensor_scalar(src[s][:, :], keys[s][:, :], N - 1, None, ALU.bitwise_and).then_inc(src_ready[s], 1)
            st.mark(dve.tensor_copy(dst_f[s][:, 0:1], dst_f[1 - s][:, W:W1]))
            st.link(dve.tensor_copy(dst_f[s][:, 1:W1], dst[:, :]))
            st.link(dve.tensor_tensor(keep[s][:, :, 1:W1], wide(dst_f[s][:, 1:W1]), wide(dst_f[s][:, 0:W]),
                                      ALU.is_equal))
            st.link(dve.tensor_scalar(fresh[s][:, :, 1:W1], keep[s][:, :, 1:W1], 1.0, -FAR, ALU.subtract, ALU.mult))

        @block.gpsimd
        def _(pool):
            blocks = pool.value_load(blocks_i[0:1, 0:1], min_val=1, max_val=EC // BLK)
            last = pool.alloc_register("pool_last_block")
            pool.reg_mov(last, LAST)
            pool.wait_ge(first, 22)
            for s in range(2):
                gather(pool, keys[s][:, :].bitcast(F32), key_rows, key_i[s][:, :], keys_in[s], bound=last)
            gather(pool, ad[0][:, :, :].rearrange("p c k -> p (c k)"), ad_rows, ad_i[0][:, :], ad_in[0], bound=last)
            spare = pool.alloc_register("pool_spare"), first, 22
            with pool.Fori(0, blocks) as i:
                for s in range(2):
                    o = 1 - s
                    wait_apart(pool, src_ready[s], i + 1, spare)
                    pool.wait_ge(key_i_ready[s], i + 1)
                    pool.wait_ge(summed[s], i)
                    gather(pool, keys[s][:, :].bitcast(F32), key_rows, key_i[s][:, :], keys_in[s], bound=last)
                    for c in range(W):
                        gather(pool, rows[s][:, c, :], table, src[s][:, c:c + 1].bitcast(U32), rows_in[s])
                    wait_apart(pool, copied[o], i + s, spare)
                    pool.indirect_dma_start(out_rows, bass.IndirectOffsetOnAxis(ap=out_i[o][:, :], axis=0),
                                            out[o][:, :, :].rearrange("p c k -> p (c k)"), None,
                                            bounds_check=last, oob_is_err=False).then_inc(stored[o], 16)
                    wait_apart(pool, summed[o], i + s, spare)
                    gather(pool, ad[o][:, :, :].rearrange("p c k -> p (c k)"), ad_rows, ad_i[o][:, :], ad_in[o],
                           bound=last)
            wait_apart(pool, copied[1], blocks, spare)
            pool.indirect_dma_start(out_rows, bass.IndirectOffsetOnAxis(ap=out_i[1][:, :], axis=0),
                                    out[1][:, :, :].rearrange("p c k -> p (c k)"), None,
                                    bounds_check=last, oob_is_err=False).then_inc(stored[1], 16)
            for s in range(2):
                pool.wait_ge(stored[s], blocks * 16 + 16 * s)
                pool.wait_ge(keys_in[s], blocks * 16 + 16)
                pool.wait_ge(ad_in[s], blocks * 16 + 16 * (1 - s))

        @block.vector
        def _(dve):
            blocks = dve.value_load(blocks_i[0:1, 0:1], min_val=1, max_val=EC // BLK)
            st = Steps(dve, first)
            for s in range(2):
                st.mark(dve.memset(keep[s][:, :, 0:1], 0.0))
                st.mark(dve.memset(fresh[s][:, :, 0:1], FAR))
                st.mark(dve.memset(ad[s][:, :, :], 0.0))
                st.mark(dve.memset(out[s][:, :, :], 0.0))
                st.mark(dve.memset(keys[s][:, :], 0))
                st.mark(dve.tensor_scalar(key_f[s][:, :], chunk_f[:, :], 2.0, float(s), ALU.mult, ALU.add))
                st.link(dve.tensor_scalar(out_f[s][:, :], chunk_f[:, :], 2.0, float(s), ALU.mult, ALU.add))
                st.mark(dve.tensor_copy(key_i[s][:, :], key_f[s][:, :]))
                st.mark(dve.tensor_copy(ad_i[s][:, :], out_f[s][:, :]))
            st.link(dve.memset(starts[:, :, :], 0.0))
            st.link(dve.memset(dst_f[1][:, W:W1], float(2 * E)))
            st.link(dve.tensor_copy(out_i[1][:, :], dst_f[1][:, W:W1]))
            st.link(dve.memset(dst_f[1][:, W:W1], -1.0))
            assert st.n == 22
            st.mark(dve.memset(decay[:, :, 0:1], 0.0))
            st.mark(dve.memset(held[:, :, W:W1], 0.0))
            st.mark(dve.memset(tops[:, :, W:W1], NONE))
            st.link(dve.memset(sums[:, :, W:W1], 0.0))
            for s in range(2):
                dve.wait_ge(keys_in[s], 16)
                prepare(dve, st, s)
            spare = dve.alloc_register("dve_spare_edges"), first, 22
            with dve.Fori(0, blocks) as i:
                st = LoopSteps(dve, steps, i, 42)
                for s in range(2):
                    o = 1 - s
                    dve.wait_ge(ad_in[s], i * 16 + 16)
                    st.mark(dve.tensor_copy(starts[:, :, 0:1], held[:, :, W:W1]))
                    st.link(dve.tensor_copy(starts[:, :, 1:W1], ad[s][:, :, :].rearrange("p w h -> p h w")))
                    st.link(dve.tensor_tensor_scan(flat(held), flat(keep[s]), flat(starts), 0.0, ALU.mult, ALU.add))
                    dve.wait_ge(rows_in[s], i * (16 * W) + 16 * W)
                    st.link(dve.tensor_tensor(raw[:, :, :], rows[s][:, :, Q:ROW].rearrange("p w h -> p h w"),
                                              held[:, :, 1:W1], ALU.add))
                    st.mark(dve.tensor_copy(score[:, :, 0:1], tops[:, :, W:W1]))
                    st.link(dve.scalar_tensor_tensor(score[:, :, 1:W1], raw[:, :, :], 0.2, raw[:, :, :],
                                                     ALU.mult, ALU.max))
                    dve.wait_ge(copied[o], i + s)
                    st.link(dve.tensor_tensor_scan(flat(tops), flat(fresh[s]), flat(score), 0.0, ALU.add, ALU.max))
                    st.mark(dve.tensor_tensor(gaps[:, 1, :, :], score[:, :, 1:W1], tops[:, :, 1:W1], ALU.subtract))
                    st.link(dve.tensor_tensor(before[:, :, :], tops[:, :, 0:W], fresh[s][:, :, 1:W1], ALU.add))
                    dve.tensor_tensor(gaps[:, 0, :, :], before[:, :, :], tops[:, :, 1:W1], ALU.subtract)\
                        .then_inc(gaps_ready, 1)
                    dve.wait_ge(stored[s], i * 16 + 16 * s)
                    st.mark(dve.tensor_copy(out_i[s][:, :], out_f[s][:, :]))
                    st.mark(dve.tensor_copy(last_dst[:, :], dst_f[s][:, W:W1]))
                    st.link(dve.tensor_copy(terms[:, :, 0:1], sums[:, :, W:W1]))
                    st.link(dve.tensor_scalar(out_f[s][:, :], out_f[s][:, :], 2.0, None, ALU.add))
                    st.mark(dve.tensor_copy(ad_i[s][:, :], out_f[s][:, :]))
                    dve.wait_ge(weights_ready, i * 2 + s + 1)
                    per_head = terms[:, :, 1:W1].rearrange("p (h k) w -> p h k w", h=HEADS)
                    st.link(dve.tensor_tensor(per_head, rows[s][:, :, 0:Q].rearrange("p w (h k) -> p h k w", h=HEADS),
                                              weight[:, :, :].unsqueeze(2).to_broadcast([P, HEADS, NE + 1, W]),
                                              ALU.mult))
                    dve.tensor_tensor_scan(flat(sums), flat(decay), flat(terms), 0.0, ALU.mult, ALU.add)\
                        .then_inc(summed[s], 1)
                    dve.wait_ge(keys_in[s], i * 16 + 32)
                    prepare(dve, st, s)
                st.end()
            dve.wait_ge(summed[1], blocks)
            dve.tensor_copy(state[:, 0:Q], sums[:, :, W]).then_inc(first, 1)
            dve.tensor_copy(state[:, Q:ROW], tops[:, :, W]).then_inc(first, 1)

        @block.scalar
        def _(act):
            blocks = act.value_load(blocks_i[0:1, 0:1], min_val=1, max_val=EC // BLK)
            with act.Fori(0, blocks) as i:
                for s in range(2):
                    act.wait_ge(gaps_ready, i * 2 + s + 1)
                    act.activation(weight[:, :, :], gaps[:, 1, :, :], ACT.Exp)
                    act.activation(decay[:, :, 1:W1].rearrange("p (h k) w -> p h k w", h=HEADS),
                                   gaps[:, 0, :, :].unsqueeze(2).to_broadcast([P, HEADS, NE + 1, W]), ACT.Exp)\
                        .then_inc(weights_ready, 1)
                    act.wait_ge(summed[s], i + 1)
                    act.activation(out[s][:, :, 0:Q], sums[:, :, 1:W1].rearrange("p q w -> p w q"), ACT.Copy)
                    act.activation(out[s][:, :, Q:ROW], tops[:, :, 1:W1].rearrange("p h w -> p w h"), ACT.Copy)\
                        .then_inc(copied[s], 1)


def join_chunks(nc, ends_dram, edge_rows_dram, ident, chunk_f, blocks_i, first_dst, last_dst, state):
    W1 = P + 1
    with ExitStack() as ctx:
        a = Arena(nc, ctx, "join")
        cols = a.sb("cols", [P, 4, Q])
        row = a.sb("row", [Q, 4, P])
        same = a.sb("same", [Q, P])
        pens = a.sb("pens", [Q, P])
        joined = a.sb("joined", [Q, P])
        none = a.sb("none", [Q, P])
        tops = a.sb("tops", [Q, P])
        gaps = a.sb("gaps", [Q, 2, P])
        exps = a.sb("exps", [Q, 2, P])
        terms = a.sb("terms", [Q, P])
        sums = a.sb("sums", [Q, P])
        carry = a.sb("carry", [Q, 2, P])
        back = a.sb("back", [P, 2, Q])
        node_f = a.sb("node_f", [P, 1])
        node_i = a.sb("node_i", [P, 1], U32)
        end_f = a.sb("end_f", [P, 1])
        limit = a.sb("limit", [P, 1])
        blocks_f = a.sb("blocks_f", [P, 1])
        beyond = a.sb("beyond", [P, 1])
        last_i = a.sb("last_i", [P, 1], U32)
        old = a.sb("old", [P, ROW])
        new = a.sb("new", [P, ROW])
        gap2 = a.sb("gap2", [P, 2, HEADS])
        exp2 = a.sb("exp2", [P, 2, HEADS])
        part2 = a.sb("part2", [P, 2, Q])
        turned = a.ps("turned", [Q, 4 * P])
        returned = a.ps("returned", [P, 2 * Q])
        steps = a.sem("join_steps")
        cols_turned = a.sem("cols_turned")
        gaps_ready = a.sem("gaps_ready")
        exps_ready = a.sem("exps_ready")
        carry_turned = a.sem("carry_turned")
        end_in = a.sem("end_in")
        old_in = a.sem("old_in")
        gap2_ready = a.sem("gap2_ready")
        exp2_ready = a.sem("exp2_ready")
        fixed = a.sem("rows_fixed")
        marks = {}
        block = ctx.enter_context(nc.Block())

        @block.vector
        def _(dve):
            st = Steps(dve, steps)
            per_head = cols[:, 1, :].rearrange("p (h k) -> p h k", h=HEADS)
            st.mark(dve.tensor_copy(cols[:, 0, :], state[:, 0:Q]))
            st.mark(dve.tensor_copy(per_head, per_channel(state[:, Q:ROW], NE + 1)))
            st.mark(dve.tensor_copy(cols[:, 2, :], last_dst[:, :].to_broadcast([P, Q])))
            st.link(dve.tensor_copy(cols[:, 3, :], first_dst[:, :].to_broadcast([P, Q])))
            marks["cols"] = st.n
            st.link(dve.tensor_scalar(node_f[:, :], first_dst[:, :], 1.0, float(N), ALU.add, ALU.min))
            st.link(dve.tensor_copy(node_i[:, :], node_f[:, :]))
            marks["node"] = st.n
            st.mark(dve.memset(old[:, :], 0.0))
            st.link(dve.tensor_copy(blocks_f[:, :], blocks_i[:, :]))
            st.link(dve.tensor_tensor(limit[:, :], chunk_f[:, :], blocks_f[:, :], ALU.add))
            st.link(dve.tensor_scalar(limit[:, :], limit[:, :], float(BLK), None, ALU.mult))
            dve.wait_ge(end_in, 16)
            st.link(dve.tensor_tensor(beyond[:, :], end_f[:, :], limit[:, :], ALU.is_gt))
            st.link(dve.scalar_tensor_tensor(beyond[:, :], first_dst[:, :], float(N), beyond[:, :], ALU.is_ge, ALU.add))
            st.link(dve.tensor_scalar(end_f[:, :], end_f[:, :], 1.0, None, ALU.subtract))
            st.link(dve.scalar_tensor_tensor(end_f[:, :], beyond[:, :], float(2 * E), end_f[:, :], ALU.mult, ALU.add))
            st.link(dve.tensor_copy(last_i[:, :], end_f[:, :]))
            marks["last"] = st.n
            dve.wait_ge(cols_turned, 1)
            st.link(dve.tensor_copy(row[:, :, :], turned[:, :].rearrange("q (n p) -> q n p", n=4)))
            st.mark(dve.memset(same[:, 0:1], 0.0))
            st.mark(dve.memset(joined[:, 0:1], 0.0))
            st.mark(dve.tensor_tensor(same[:, 1:P], row[:, 2, 1:P], row[:, 2, 0:P - 1], ALU.is_equal))
            st.link(dve.tensor_tensor(joined[:, 1:P], row[:, 3, 1:P], row[:, 2, 0:P - 1], ALU.is_equal))
            st.link(dve.tensor_scalar(pens[:, :], same[:, :], 1.0, -FAR, ALU.subtract, ALU.mult))
            st.link(dve.tensor_tensor_scan(tops[:, :], pens[:, :], row[:, 1, :], 0.0, ALU.add, ALU.max))
            st.mark(dve.tensor_tensor(gaps[:, 1, :], row[:, 1, :], tops[:, :], ALU.subtract))
            st.mark(dve.memset(gaps[:, 0, 0:1], FAR))
            st.link(dve.tensor_tensor(gaps[:, 0, 1:P], tops[:, 0:P - 1], pens[:, 1:P], ALU.add))
            dve.tensor_tensor(gaps[:, 0, 1:P], gaps[:, 0, 1:P], tops[:, 1:P], ALU.subtract).then_inc(gaps_ready, 1)
            dve.wait_ge(exps_ready, 1)
            st.link(dve.tensor_tensor(terms[:, :], row[:, 0, :], exps[:, 1, :], ALU.mult))
            st.link(dve.tensor_tensor_scan(sums[:, :], exps[:, 0, :], terms[:, :], 0.0, ALU.mult, ALU.add))
            st.link(dve.memset(carry[:, :, :], 0.0))
            st.mark(dve.tensor_tensor(carry[:, 0, 1:P], sums[:, 0:P - 1], joined[:, 1:P], ALU.mult))
            st.link(dve.tensor_tensor(carry[:, 1, 1:P], tops[:, 0:P - 1], joined[:, 1:P], ALU.mult))
            st.link(dve.tensor_scalar(none[:, :], joined[:, :], 1.0, -NONE, ALU.subtract, ALU.mult))
            st.link(dve.tensor_tensor(carry[:, 1, :], carry[:, 1, :], none[:, :], ALU.add))
            marks["carry"] = st.n
            dve.wait_ge(carry_turned, 1)
            st.link(dve.tensor_copy(back[:, :, :], returned[:, :].rearrange("p (n q) -> p n q", n=2)))
            dve.wait_ge(old_in, 16)
            carried = back[:, 1, 0:Q:NE + 1]
            st.link(dve.tensor_tensor(new[:, Q:ROW], old[:, Q:ROW], carried, ALU.max))
            st.mark(dve.tensor_tensor(gap2[:, 0, :], old[:, Q:ROW], new[:, Q:ROW], ALU.subtract))
            dve.tensor_tensor(gap2[:, 1, :], carried, new[:, Q:ROW], ALU.subtract).then_inc(gap2_ready, 1)
            dve.wait_ge(steps, st.n)
            dve.wait_ge(exp2_ready, 1)
            for n, sums_n in enumerate((old[:, 0:Q], back[:, 0, :])):
                st.link(dve.tensor_tensor(part2[:, n, :].rearrange("p (h k) -> p h k", h=HEADS),
                                          sums_n.rearrange("p (h k) -> p h k", h=HEADS),
                                          per_channel(exp2[:, n, :], NE + 1), ALU.mult))
            st.link(dve.tensor_tensor(new[:, 0:Q], part2[:, 0, :], part2[:, 1, :], ALU.add))
            marks["new"] = st.n

        @block.tensor
        def _(pe):
            pe.wait_ge(steps, marks["cols"])
            for n in range(4):
                ins = pe.transpose(turned[:, n * P:(n + 1) * P], cols[:, n, :], ident[:, :])
            ins.then_inc(cols_turned, 1)
            pe.wait_ge(steps, marks["carry"])
            for n in range(2):
                ins = pe.transpose(returned[:, n * Q:(n + 1) * Q], carry[:, n, :], ident[0:Q, 0:Q])
            ins.then_inc(carry_turned, 1)

        @block.scalar
        def _(act):
            act.wait_ge(gaps_ready, 1)
            act.wait_ge(steps, marks["last"])
            act.activation(exps[:, :, :], gaps[:, :, :], ACT.Exp).then_inc(exps_ready, 1)
            act.wait_ge(gap2_ready, 1)
            act.activation(exp2[:, :, :], gap2[:, :, :], ACT.Exp).then_inc(exp2_ready, 1)

        @block.gpsimd
        def _(pool):
            pool.wait_ge(steps, marks["node"])
            gather(pool, end_f[:, :], ends_dram.rearrange("(n a) -> n a", a=1), node_i[:, :], end_in)
            pool.wait_ge(steps, marks["last"])
            gather(pool, old[:, :], edge_rows_dram, last_i[:, :], old_in, bound=E - 1)
            pool.wait_ge(steps, marks["new"])
            pool.indirect_dma_start(edge_rows_dram, bass.IndirectOffsetOnAxis(ap=last_i[:, :], axis=0), new[:, :], None,
                                    bounds_check=E - 1, oob_is_err=False).then_inc(fixed, 16)
            pool.wait_ge(fixed, 16)


def route(nc, b_gat, ln_gamma, ln_beta, edge_rows_dram, ends_f, starts_f, rows, ad_sb, x_sb, eo, out_dram):
    F = HEADS * NE
    with ExitStack() as ctx:
        a = Arena(nc, ctx, "route")
        edge = a.sb("edge", [P, T, ROW])
        empty = a.sb("empty", [P, T])
        at_f = a.sb("at_f", [P, T])
        at = a.sb("at", [P, T], U32)
        vec = a.sb("vec", [P, 3, F])
        mine = a.sb("mine", [P, T, HEADS])
        top = a.sb("top", [P, T, HEADS])
        gap = a.sb("gap", [P, 2, T, HEADS])
        e2 = a.sb("e2", [P, 2, T, HEADS])
        part = a.sb("part", [P, T, Q])
        total = a.sb("total", [P, T, Q])
        inverse = a.sb("inverse", [P, T, HEADS])
        agg = a.sb("agg", [P, T, F])
        scores = a.sb("scores", [P, T, NE])
        gate = a.sb("gate", [P, T, NE])
        gap2, gap2_exp = a.sb("gap2", [P, T]), a.sb("gap2_exp", [P, T])
        weighted = a.sb("weighted", [P, TB, NE * C])
        summed = a.sb("summed", [P, TB, C])
        norm = Norm(a, "norm", T, F, 1e-5)
        vec_in = a.sem("vec_in")
        steps = a.sem("route_steps")
        edge_in = a.sem("edge_in")
        gaps_ready = a.sem("gaps_ready")
        exps_ready = a.sem("exps_ready")
        normed = a.sem("normed")
        gap2_ready = a.sem("gap2_ready")
        gap2_exp_ready = a.sem("gap2_exp_ready")
        result = a.sem("result_ready")
        stored = a.sem("result_stored")
        marks = {}
        block = ctx.enter_context(nc.Block())

        @block.vector
        def _(dve):
            st = Steps(dve, steps)
            st.mark(dve.memset(edge[:, :, 0:Q], 0.0))
            st.mark(dve.memset(edge[:, :, Q:ROW], NONE))
            st.mark(dve.tensor_tensor(empty[:, :], starts_f[:, :], ends_f[:, :], ALU.is_equal))
            st.link(dve.tensor_scalar(at_f[:, :], ends_f[:, :], 1.0, None, ALU.subtract))
            st.link(dve.scalar_tensor_tensor(at_f[:, :], empty[:, :], float(2 * E), at_f[:, :], ALU.mult, ALU.add))
            st.link(dve.tensor_scalar(at_f[:, :], at_f[:, :], 0.0, None, ALU.max))
            st.link(dve.tensor_copy(at[:, :], at_f[:, :]))
            marks["at"] = st.n
            st.link(dve.tensor_tensor(mine[:, :, :], rows[:, :, Q:ROW], ad_sb[:, :, :], ALU.add))
            st.link(dve.scalar_tensor_tensor(mine[:, :, :], mine[:, :, :], 0.2, mine[:, :, :], ALU.mult, ALU.max))
            dve.wait_ge(edge_in, 16 * T)
            st.link(dve.tensor_tensor(top[:, :, :], mine[:, :, :], edge[:, :, Q:ROW], ALU.max))
            st.mark(dve.tensor_tensor(gap[:, 0, :, :], edge[:, :, Q:ROW], top[:, :, :], ALU.subtract))
            dve.tensor_tensor(gap[:, 1, :, :], mine[:, :, :], top[:, :, :], ALU.subtract).then_inc(gaps_ready, 1)
            dve.wait_ge(exps_ready, 1)

            def by_head(v):
                return v.rearrange("p t (h k) -> p t h k", h=HEADS)

            def wide(v):
                return v.unsqueeze(3).to_broadcast([P, T, HEADS, NE + 1])

            st.mark(dve.tensor_tensor(by_head(total[:, :, :]), by_head(edge[:, :, 0:Q]), wide(e2[:, 0, :, :]), ALU.mult))
            st.link(dve.tensor_tensor(by_head(part[:, :, :]), by_head(rows[:, :, 0:Q]), wide(e2[:, 1, :, :]), ALU.mult))
            st.link(dve.tensor_tensor(total[:, :, :], total[:, :, :], part[:, :, :], ALU.add))
            st.link(dve.tensor_scalar(inverse[:, :, :], by_head(total[:, :, :])[:, :, :, 0], 1e-16, None, ALU.add))
            st.link(dve.reciprocal(inverse[:, :, :], inverse[:, :, :]))
            st.link(dve.tensor_tensor(by_head(agg[:, :, :]), by_head(total[:, :, :])[:, :, :, 1:NE + 1],
                                      inverse[:, :, :].unsqueeze(3).to_broadcast([P, T, HEADS, NE]), ALU.mult))
            dve.wait_ge(vec_in, 48)

            def vector(n):
                return vec[:, n, :].unsqueeze(1).to_broadcast([P, T, F])

            st.link(dve.tensor_tensor(agg[:, :, :], agg[:, :, :], vector(0), ALU.add))
            norm.vector(dve, st, agg[:, :, :], agg[:, :, :], 0, normed)
            st.link(dve.tensor_tensor(agg[:, :, :], agg[:, :, :], vector(1), ALU.mult))
            st.link(dve.tensor_tensor(agg[:, :, :], agg[:, :, :], vector(2), ALU.add))
            st.link(dve.tensor_reduce(scores[:, :, :], agg[:, :, :].rearrange("p t (h k) -> p t k h", h=HEADS), X, ALU.add))
            st.link(dve.tensor_scalar(scores[:, :, :], scores[:, :, :], 1.0 / HEADS, None, ALU.mult))
            masks, tops = top_two(dve, st, a, "best", scores[:, :, :], T, NE)
            two_weights(dve, st, a, "best", gate[:, :, :], tops, masks, gap2, gap2_exp, gap2_ready, gap2_exp_ready)
            for b in range(B):
                tiles = slice(b * TB, (b + 1) * TB)
                st.link(dve.tensor_tensor(weighted[:, :, :].rearrange("p t (e c) -> p t e c", e=NE),
                                          eo[:, tiles, :].rearrange("p t (e c) -> p t e c", e=NE),
                                          gate[:, tiles, :].unsqueeze(3).to_broadcast([P, TB, NE, C]), ALU.mult))
                st.link(dve.tensor_reduce(summed[:, :, :], weighted[:, :, :].rearrange("p t (e c) -> p t c e", e=NE),
                                          X, ALU.add))
                dve.tensor_tensor(x_sb[:, tiles, :], x_sb[:, tiles, :], summed[:, :, :], ALU.add).then_inc(result, 1)
                dve.wait_ge(result, b + 1)

        @block.scalar
        def _(act):
            act.wait_ge(gaps_ready, 1)
            act.wait_ge(steps, marks["at"] + 4)
            act.activation(e2[:, :, :, :], gap[:, :, :, :], ACT.Exp).then_inc(exps_ready, 1)
            norm.scalar(act, 0)
            act.wait_ge(gap2_ready, 1)
            act.activation(gap2_exp[:, :], gap2[:, :], ACT.Exp).then_inc(gap2_exp_ready, 1)

        @block.gpsimd
        def _(pool):
            pool.wait_ge(steps, marks["at"])
            for t in range(T):
                gather(pool, edge[:, t, :], edge_rows_dram, at[:, t:t + 1], edge_in, bound=E - 1)

        @block.sync
        def _(sp):
            for n, v in enumerate((b_gat, ln_gamma, ln_beta)):
                sp.dma_start(vec[:, n, :], v.partition_broadcast(P)).then_inc(vec_in, 16)
            for b in range(B):
                sp.wait_ge(result, b + 1)
                sp.dma_start(out_dram[b, :, :, :].rearrange("(t r) w c -> (r w) t c", t=TB), x_sb[:, b * TB:(b + 1) * TB, :])\
                    .then_inc(stored, 16)
            sp.wait_ge(stored, 16 * B)


def build(nc, x, gamma, gate_w, gate_b, w1, w2, w3, kernel_w, W_gat, att_src, att_dst, b_gat, ln_gamma, ln_beta,
          W1, b1, W2, b2, edge_index, out):
    keys_dram = nc.dram_tensor("keys_dram", (E,), F32).ap()
    pivots_dram = nc.dram_tensor("pivots_dram", (E // BLK,), F32).ap()
    ends_dram = nc.dram_tensor("ends_dram", (N + 1,), F32).ap()
    table = nc.dram_tensor("table", (N, ROW), F32).ap()
    a_dst_dram = nc.dram_tensor("a_dst_dram", (N, HEADS), F32).ap()
    edge_ad_dram = nc.dram_tensor("edge_ad_dram", (E, HEADS), F32).ap()
    edge_rows_dram = nc.dram_tensor("edge_rows_dram", (E, ROW), F32).ap()
    with ExitStack() as ctx:
        a = Arena(nc, ctx, "all")
        ident = a.sb("ident", [P, P])
        p_sign = a.sb("p_sign", [P, 2])
        x_sb = a.sb("x_sb", [P, T, C])
        blocks_i = a.sb("blocks_i", [P, 1], I32)
        chunk_f = a.sb("chunk_f", [P, 1])
        first_dst = a.sb("first_dst", [P, 1])
        last_dst = a.sb("last_dst", [P, 1])
        state = a.sb("state", [P, ROW])
        ends_f = a.sb("ends_f", [P, T])
        starts_f = a.sb("starts_f", [P, T])
        ad_sb = a.sb("ad_sb", [P, T, HEADS])
        rows = a.sb("rows", [P, T, ROW])
        constants(nc, ident, p_sign)
        sort_edges(nc, edge_index, ident, p_sign, keys_dram, pivots_dram,
                   [v.rearrange("n k -> (n k)") for v in (edge_ad_dram, edge_rows_dram)])
        search(nc, keys_dram, pivots_dram, ends_dram, blocks_i, ends_f, starts_f)
        with ExitStack() as middle:
            m = Arena(nc, middle, "middle")
            yT = m.sb("yT", [C, N])
            dispatch = m.sb("dispatch", [P, T, w1.shape[0]])
            attention(nc, x, gamma, x_sb, yT, ident)
            gates(nc, gate_w, gate_b, yT, dispatch)
            experts(nc, w1, w2, w3, x_sb, yT, dispatch)
        eo = a.sb("eo", [P, T, NE * C])
        with ExitStack() as middle:
            m = Arena(nc, middle, "features")
            h_sb = m.sb("h_sb", [P, T, HEADS * NE])
            as_sb = m.sb("as_sb", [P, T, HEADS])
            convolve(nc, kernel_w, W_gat, att_src, att_dst, W1, b1, W2, b2, x_sb, eo, h_sb, as_sb, ad_sb, ident)
            write_table(nc, h_sb, as_sb, ad_sb, rows, table, a_dst_dram)
        spread(nc, keys_dram, ends_f, starts_f, ad_sb, a_dst_dram, edge_ad_dram, blocks_i, chunk_f, first_dst)
        edge_loop(nc, keys_dram, table, edge_ad_dram, edge_rows_dram, blocks_i, chunk_f, last_dst, state)
        join_chunks(nc, ends_dram, edge_rows_dram, ident, chunk_f, blocks_i, first_dst, last_dst, state)
        route(nc, b_gat, ln_gamma, ln_beta, edge_rows_dram, ends_f, starts_f, rows, ad_sb, x_sb, eo, out)


_INS = ["x", "L0_conv_gamma", "L0_ffn_gate_w", "L0_ffn_gate_b", "L0_ffn_w1", "L0_ffn_w2", "L0_ffn_w3",
        "L1_conv_kernel", "L1_ffn_W_gat", "L1_ffn_att_src", "L1_ffn_att_dst", "L1_ffn_b_gat", "L1_ffn_ln_gamma",
        "L1_ffn_ln_beta", "L1_ffn_W1", "L1_ffn_b1", "L1_ffn_W2", "L1_ffn_b2", "L1_ffn_edge_index"]
_OUTS = [((B, 32, 32, C), "float32")]


def kernel(**inputs):
    import numpy as _np
    import concourse.bacc as _bacc
    from concourse import mybir as _mybir
    from concourse.bass_utils import run_bass_kernel_spmd as _run
    nc = _bacc.Bacc("TRN2", target_bir_lowering=False, num_devices=1)
    arrays, args = {}, []
    for name in _INS:
        a = _np.ascontiguousarray(inputs[name])
        arrays[f"in_{name}_dram"] = a
        args.append(nc.dram_tensor(f"in_{name}_dram", a.shape, _mybir.dt.from_np(a.dtype), kind="ExternalInput").ap())
    for i, (shape, dtype) in enumerate(_OUTS):
        dt = _mybir.dt.from_np(_np.dtype(dtype))
        args.append(nc.dram_tensor(f"out_{i}_dram", shape, dt, kind="ExternalOutput").ap())
    build(nc, *args)
    r = _run(nc, [arrays], core_ids=[0])
    got = tuple(r.results[0][f"out_{i}_dram"] for i in range(len(_OUTS)))
    return got if len(got) > 1 else got[0]
```

```python
from contextlib import ExitStack

import concourse.bass as bass
from concourse import mybir

F32 = mybir.dt.float32
BF16 = mybir.dt.bfloat16
I32 = mybir.dt.int32
U32 = mybir.dt.uint32
ALU = mybir.AluOpType
ACT = mybir.ActivationFunctionType
X = mybir.AxisListType.X

P = 128
B, HW_, C = 8, 1024, 64
N = B * HW_
T = N // P
E = 262144
EC = E // P
SRC_BITS = 13
KEY_ONE = 1 << 28
FIELDS = 1 << 15
BLK = 64
ROW = 24
HEADS, NE = 4, 4
Q = HEADS * (NE + 1)
FAR = -3.0e38
NONE = -1.0e30


class Steps:

    def __init__(self, engine, sem):
        self.engine, self.sem, self.n = engine, sem, 0

    def mark(self, ins):
        ins.then_inc(self.sem, 1)
        self.n += 1
        return self.n

    def link(self, ins):
        self.mark(ins)
        self.engine.wait_ge(self.sem, self.n)


class Arena:

    def __init__(self, nc, ctx, phase):
        self.nc, self.ctx, self.phase = nc, ctx, phase

    def sb(self, name, shape, dt=F32):
        return self.ctx.enter_context(self.nc.sbuf_tensor(f"{self.phase}_{name}", shape, dt))

    def ps(self, name, shape):
        return self.ctx.enter_context(self.nc.psum_tensor(f"{self.phase}_{name}", shape, F32))

    def sem(self, name):
        return self.nc.alloc_semaphore(f"{self.phase}_{name}")


def constants(nc, ident, p_sign):
    with ExitStack() as ctx:
        a = Arena(nc, ctx, "constants")
        part = a.sb("part", [P, 1], I32)
        bit = a.sb("bit", [P, 1])
        made = a.sem("constants_made")
        signs = a.sem("signs_made")
        block = ctx.enter_context(nc.Block())

        @block.gpsimd
        def _(pool):
            st = Steps(pool, made)
            st.link(pool.memset(ident[:, :], 0.0))
            st.link(pool.affine_select(out=ident[:, :], in_=ident[:, :], compare_op=ALU.not_equal, fill=1.0,
                                       base=0, pattern=[[-1, P]], channel_multiplier=1))
            st.link(pool.iota(part[:, :], pattern=[[0, 1]], base=0, channel_multiplier=1))

        @block.vector
        def _(dve):
            dve.wait_ge(made, 3)
            st = Steps(dve, signs)
            st.link(dve.tensor_scalar(part[:, :], part[:, :], 1, None, ALU.bitwise_and))
            st.link(dve.tensor_copy(bit[:, :], part[:, :]))
            st.mark(dve.tensor_scalar(p_sign[:, 0:1], bit[:, :], -2.0, 1.0, ALU.mult, ALU.add))
            st.link(dve.tensor_scalar(p_sign[:, 1:2], bit[:, :], 2.0, -1.0, ALU.mult, ALU.add))


def sort_edges(nc, edge_index, ident, p_sign, sorted_keys, pivots, cleared):
    with ExitStack() as ctx:
        a = Arena(nc, ctx, "sort_edges")
        src_i = a.sb("src_i", [P, EC], I32)
        dst_i = a.sb("dst_i", [P, EC], I32)
        keys = [a.sb("keys_a", [P, EC]), a.sb("keys_b", [P, EC])]
        turned = a.ps("turned", [P, EC])
        loaded = a.sem("edges_loaded")
        sorting = a.sem("sort_steps")
        turns = a.sem("banks_turned")
        copies = a.sem("banks_copied")
        stored = a.sem("keys_stored")
        zeros = a.sb("zeros", [P, 4096])
        zeros_made = a.sem("zeros_made")
        clearing = a.sem("clearing")
        BANK = 512
        NB = EC // BANK
        plan = {"turn_at": [], "done": 0}

        def halves(buf, j):
            v = buf[:, :].rearrange("p (b h d) -> p b h d", h=2, d=1 << j)
            return v[:, :, 0, :], v[:, :, 1, :]

        block = ctx.enter_context(nc.Block())

        @block.vector
        def _(dve):
            st = Steps(dve, sorting)
            cur = 0

            def exchange(j):
                nonlocal cur
                lo, hi = halves(keys[cur], j)
                to_lo, to_hi = halves(keys[1 - cur], j)
                st.mark(dve.tensor_tensor(to_lo, lo, hi, ALU.min))
                st.link(dve.tensor_tensor(to_hi, lo, hi, ALU.max))
                cur = 1 - cur

            def exchange_first(j, last=False):
                nonlocal cur
                if last:
                    lo, hi = halves(keys[cur], j)
                    to_lo, to_hi = halves(keys[1 - cur], j)
                    st.mark(dve.scalar_tensor_tensor(to_lo, hi, -1.0, lo, ALU.mult, ALU.min))
                    st.link(dve.scalar_tensor_tensor(to_hi, hi, -1.0, lo, ALU.mult, ALU.max))
                else:
                    v = keys[cur][:, :].rearrange("p (b r h d) -> p b r h d", r=2, h=2, d=1 << j)
                    w = keys[1 - cur][:, :].rearrange("p (b r h d) -> p b r h d", r=2, h=2, d=1 << j)
                    for r in range(2):
                        lo, hi = v[:, :, r, 0, :], v[:, :, r, 1, :]
                        flip, keep = (hi, lo) if r == 0 else (lo, hi)
                        st.mark(dve.scalar_tensor_tensor(w[:, :, r, 0, :], flip, -1.0, keep, ALU.mult, ALU.min))
                        ins = dve.scalar_tensor_tensor(w[:, :, r, 1, :], flip, -1.0, keep, ALU.mult, ALU.max)
                        st.mark(ins)
                    dve.wait_ge(sorting, st.n)
                cur = 1 - cur

            def turn():
                nonlocal cur
                plan["turn_at"].append((st.n, cur))
                cur = 1 - cur
                dve.wait_ge(copies, NB * len(plan["turn_at"]))

            dve.wait_ge(loaded, 32)
            st.mark(dve.tensor_scalar(src_i[:, :], src_i[:, :], float(N - 1), None, ALU.min))
            st.link(dve.tensor_scalar(dst_i[:, :], dst_i[:, :], float(N), None, ALU.min))
            last_src, dropped = keys[0][:, :].bitcast(I32), keys[1][:, :].bitcast(I32)
            st.mark(dve.tensor_scalar(last_src, src_i[:, :], float(N - 1), float(N), ALU.is_ge, ALU.mult))
            st.link(dve.tensor_scalar(dropped, dst_i[:, :], float(N), float(N), ALU.is_ge, ALU.mult))
            st.link(dve.tensor_tensor(dst_i[:, :], dst_i[:, :], last_src, ALU.add))
            st.link(dve.tensor_tensor(dst_i[:, :], dst_i[:, :], dropped, ALU.add))
            st.link(dve.scalar_tensor_tensor(src_i[:, :], dst_i[:, :], SRC_BITS, src_i[:, :],
                                             ALU.logical_shift_left, ALU.bitwise_or))
            key_i = keys[0][:, :].bitcast(I32)
            st.link(dve.tensor_scalar(key_i, src_i[:, :], KEY_ONE, None, ALU.bitwise_or))
            odd = keys[0][:, 1::2]
            st.link(dve.tensor_scalar(odd, odd, -1.0, None, ALU.mult))
            for k in range(1, 19):
                if k == 11:
                    lo, hi = halves(keys[cur], 10)
                    st.mark(dve.tensor_scalar(lo, lo, p_sign[:, 0:1], None, ALU.mult))
                    st.link(dve.tensor_scalar(hi, hi, p_sign[:, 1:2], None, ALU.mult))
                    exchange(10)
                elif k > 11:
                    turn()
                    exchange_first(k - 12, last=k == 18)
                    for j in range(k - 13, -1, -1):
                        exchange(j)
                    turn()
                    exchange(10)
                else:
                    exchange_first(k - 1)
                for j in range(min(k - 1, 10) - 1, -1, -1):
                    exchange(j)
            plan["done"] = (st.n, cur)

        @block.tensor
        def _(pe):
            for n, (step, cur) in enumerate(plan["turn_at"]):
                pe.wait_ge(sorting, step)
                if n:
                    pe.wait_ge(copies, NB * n)
                for b in range(NB):
                    for t in range(b * 4, b * 4 + 4):
                        ins = pe.transpose(turned[:, t * P:(t + 1) * P], keys[cur][:, t * P:(t + 1) * P], ident[:, :])
                    ins.then_inc(turns, 1)

        @block.scalar
        def _(act):
            for n, (step, cur) in enumerate(plan["turn_at"]):
                for b in range(NB):
                    act.wait_ge(turns, NB * n + b + 1)
                    act.activation(keys[1 - cur][:, b * BANK:(b + 1) * BANK], turned[:, b * BANK:(b + 1) * BANK],
                                   ACT.Copy).then_inc(copies, 1)

        @block.gpsimd
        def _(pool):
            pool.memset(zeros[:, :], 0.0).then_inc(zeros_made, 1)

        @block.sync
        def _(sp):
            sp.dma_start(src_i[:, :], edge_index[0, :].rearrange("(p c) -> p c", p=P)).then_inc(loaded, 16)
            sp.dma_start(dst_i[:, :], edge_index[1, :].rearrange("(p c) -> p c", p=P)).then_inc(loaded, 16)
            sp.wait_ge(zeros_made, 1)
            for flat in cleared:
                for piece in range(flat.shape[0] // (P * 4096)):
                    sp.dma_start(flat[piece * P * 4096:(piece + 1) * P * 4096].rearrange("(p c) -> p c", p=P), zeros[:, :])\
                        .then_inc(clearing, 16)
            sp.wait_ge(clearing, 16 * sum(flat.shape[0] // (P * 4096) for flat in cleared))
            n, cur = plan["done"]
            sp.wait_ge(sorting, n)
            sp.dma_start(sorted_keys.rearrange("(p c) -> p c", p=P), keys[cur][:, :]).then_inc(stored, 16)
            sp.dma_start(pivots.rearrange("(p c) -> p c", p=P), keys[cur][:, BLK - 1::BLK],
                         allow_slow_non_contiguous=True).then_inc(stored, 16)
            sp.wait_ge(stored, 32)
def gather(pool, to, rows, index, done, bound=None):
    where = bass.IndirectOffsetOnAxis(ap=index, axis=0)
    if bound is None:
        pool.indirect_dma_start(to, None, rows, where).then_inc(done, 16)
    else:
        pool.indirect_dma_start(to, None, rows, where, bounds_check=bound, oob_is_err=False).then_inc(done, 16)


class Search:

    L = 64

    def __init__(self, nc, a, name, base, before, keys_dram, pivots_dram, ends_dram, ends_f, starts_f):
        L = self.L
        self.nc, self.base, self.before, self.ends_dram = nc, base, before, ends_dram
        self.tables = (pivots_dram, keys_dram)
        self.ends_f, self.starts_f = ends_f, starts_f
        self.node = a.sb(name + "_node", [P, T], I32)
        self.bound = a.sb(name + "_bound", [P, T], I32)
        self.tops = a.sb(name + "_tops", [P, L])
        self.found = a.sb(name + "_found", [P, T, L])
        self.less = a.sb(name + "_less", [P, T, L])
        self.counts = [a.sb(f"{name}_count{n}", [P, T]) for n in range(3)]
        self.at = a.sb(name + "_at", [P, T])
        self.index = [a.sb(f"{name}_index{n}", [P, T], U32) for n in range(2)]
        self.made = a.sem(name + "_nodes_made")
        self.tops_in = a.sem(name + "_tops_in")
        self.steps = a.sem(name + "_steps")
        self.level = a.sem(name + "_index_ready")
        self.rows_in = [a.sem(f"{name}_rows_in{n}") for n in range(2)]
        self.ends_ready = a.sem(name + "_ends_ready")
        self.stored = a.sem(name + "_ends_stored")
        self.reloaded = a.sem(name + "_ends_reloaded")

    def load_tops(self, sp):
        with self.nc.allow_non_contiguous_dma(reason="a value per row"):
            tops = self.tables[0].rearrange("(i c) -> c i", c=self.L)[self.L - 1, :]
            sp.dma_start(self.tops[:, :], tops.partition_broadcast(P)).then_inc(self.tops_in, 16)

    def gathers(self, pool):
        pool.iota(self.node[:, :], pattern=[[P, T]], base=self.base + 1, channel_multiplier=1).then_inc(self.made, 1)
        for n, table in enumerate(self.tables):
            pool.wait_ge(self.level, n + 1)
            for t in range(T):
                gather(pool, self.found[:, t, :], table.rearrange("(r c) -> r c", c=self.L),
                       self.index[n][:, t:t + 1], self.rows_in[n])

    def count(self, dve, n):
        L, less, counts, at = self.L, self.less, self.counts, self.at
        if n == 0:
            self.st = Steps(dve, self.steps)
        st = self.st
        if n == 0:
            dve.wait_ge(self.made, 1)
            st.link(dve.tensor_scalar(self.bound[:, :], self.node[:, :], SRC_BITS, KEY_ONE, ALU.logical_shift_left,
                                      ALU.bitwise_or))
            dve.wait_ge(self.tops_in, 16)
            values = self.tops[:, :].unsqueeze(1).to_broadcast([P, T, L])
        else:
            dve.wait_ge(self.rows_in[n - 1], 16 * T)
            values = self.found[:, :, :]
        st.link(dve.tensor_tensor(less[:, :, :], values, per_channel(self.bound[:, :].bitcast(F32), L), ALU.is_lt))
        st.link(dve.tensor_reduce(counts[n][:, :], less[:, :, :], X, ALU.add))
        if n == 0:
            st.link(dve.tensor_scalar(at[:, :], counts[0][:, :], L - 1.0, None, ALU.min))
        elif n == 1:
            st.link(dve.tensor_scalar(counts[1][:, :], counts[1][:, :], L - 1.0, None, ALU.min))
            st.link(dve.scalar_tensor_tensor(at[:, :], at[:, :], float(L), counts[1][:, :], ALU.mult, ALU.add))
        if n < 2:
            dve.tensor_copy(self.index[n][:, :], at[:, :]).then_inc(self.level, 1)
        else:
            dve.scalar_tensor_tensor(self.ends_f[:, :], at[:, :], float(L), counts[2][:, :], ALU.mult, ALU.add)\
                .then_inc(self.ends_ready, 1)

    def shift(self, sp):
        ends_dram = self.ends_dram
        with self.nc.allow_non_contiguous_dma(reason="a value per node"):
            sp.wait_ge(self.ends_ready, 1)
            sp.dma_start(ends_dram[1:N + 1].rearrange("(t p) -> p t", p=P), self.ends_f[:, :]).then_inc(self.stored, 16)
            sp.dma_start(ends_dram[0:1].rearrange("(a b) -> a b", a=1), self.before).then_inc(self.stored, 16)
            sp.wait_ge(self.stored, 32)
            sp.dma_start(self.starts_f[:, :], ends_dram[0:N].rearrange("(t p) -> p t", p=P)).then_inc(self.reloaded, 16)
            sp.wait_ge(self.reloaded, 16)




def per_channel(v, n):
    return v.unsqueeze(2).to_broadcast([v.shape[0], v.shape[1], n])


class Norm:

    def __init__(self, a, name, groups, width, eps):
        self.groups, self.width, self.eps = groups, width, eps
        self.squares = a.sb(name + "_squares", [P, groups, width])
        self.mean = a.sb(name + "_mean", [P, groups])
        self.var = a.sb(name + "_var", [P, groups])
        self.root = a.sb(name + "_root", [P, groups])
        self.rstd = a.sb(name + "_rstd", [P, groups])
        self.var_ready = a.sem(name + "_var_ready")
        self.root_ready = a.sem(name + "_root_ready")

    def vector(self, dve, st, y, x, nth, y_ready):
        w = self.width
        st.link(dve.tensor_reduce(self.mean[:, :], x, X, ALU.add))
        st.link(dve.tensor_scalar(self.mean[:, :], self.mean[:, :], -1.0 / w, None, ALU.mult))
        st.link(dve.tensor_tensor(y, x, per_channel(self.mean[:, :], w), ALU.add))
        st.link(dve.tensor_tensor(self.squares[:, :, :], y, y, ALU.mult))
        st.link(dve.tensor_reduce(self.var[:, :], self.squares[:, :, :], X, ALU.add))
        dve.tensor_scalar(self.var[:, :], self.var[:, :], 1.0 / w, self.eps, ALU.mult, ALU.add)\
            .then_inc(self.var_ready, 1)
        dve.wait_ge(self.root_ready, nth + 1)
        st.link(dve.reciprocal(self.rstd[:, :], self.root[:, :]))
        dve.tensor_tensor(y, y, per_channel(self.rstd[:, :], w), ALU.mult).then_inc(y_ready, 1)
        dve.wait_ge(y_ready, nth + 1)

    def scalar(self, act, nth):
        act.wait_ge(self.var_ready, nth + 1)
        act.activation(self.root[:, :], self.var[:, :], ACT.Sqrt).then_inc(self.root_ready, 1)


def wait_apart(engine, sem, value, spare):
    register, met, least = spare
    engine.reg_mov(register, value)
    engine.wait_ge(met, least)
    engine.wait_ge(sem, register)


class LoopSteps:

    def __init__(self, engine, sem, i, per):
        self.engine, self.sem, self.i, self.per, self.n = engine, sem, i, per, 0

    def mark(self, ins):
        ins.then_inc(self.sem, 1)
        self.n += 1

    def link(self, ins):
        self.mark(ins)
        self.engine.wait_ge(self.sem, self.i * self.per + self.n)

    def link_apart(self, ins, spare):
        self.mark(ins)
        wait_apart(self.engine, self.sem, self.i * self.per + self.n, spare)

    def end(self):
        assert self.n == self.per, (self.n, self.per)


def top_two(dve, st, a, name, values, G, K):
    order = a.sb(name + "_order", [P, K])
    pick = a.sb(name + "_pick", [P, G, K])
    rest = a.sb(name + "_rest", [P, G, K])
    best = a.sb(name + "_best", [P, G])
    masks = [a.sb(name + f"_mask{n}", [P, G, K]) for n in range(2)]
    tops = [a.sb(name + f"_top{n}", [P, G]) for n in range(2)]
    rank = order[:, :].unsqueeze(1).to_broadcast([P, G, K])
    for k in range(K):
        st.mark(dve.memset(order[:, k:k + 1], float(K - k)))
    for n in range(2):
        now = values if n == 0 else rest[:, :, :]
        st.link(dve.tensor_reduce(tops[n][:, :], now, X, ALU.max))
        st.link(dve.tensor_tensor(pick[:, :, :], now, per_channel(tops[n][:, :], K), ALU.is_equal))
        st.link(dve.tensor_tensor(pick[:, :, :], pick[:, :, :], rank, ALU.mult))
        st.link(dve.tensor_reduce(best[:, :], pick[:, :, :], X, ALU.max))
        st.link(dve.tensor_tensor(masks[n][:, :, :], rank, per_channel(best[:, :], K), ALU.is_equal))
        if n == 0:
            st.link(dve.scalar_tensor_tensor(rest[:, :, :], masks[0][:, :, :], FAR, values, ALU.mult, ALU.add))
    return masks, tops


def two_weights(dve, st, a, name, out, tops, masks, gap, gap_exp, gap_ready, exp_ready):
    G, K = out.shape[1], out.shape[2]
    w = [a.sb(name + f"_w{n}", [P, G]) for n in range(2)]
    dve.tensor_tensor(gap[:, :], tops[1][:, :], tops[0][:, :], ALU.subtract).then_inc(gap_ready, 1)
    dve.wait_ge(exp_ready, 1)
    st.link(dve.tensor_scalar(w[1][:, :], gap_exp[:, :], 1.0, None, ALU.add))
    st.link(dve.reciprocal(w[0][:, :], w[1][:, :]))
    st.link(dve.tensor_tensor(w[1][:, :], w[0][:, :], gap_exp[:, :], ALU.mult))
    st.mark(dve.tensor_tensor(masks[0][:, :, :], masks[0][:, :, :], per_channel(w[0][:, :], K), ALU.mult))
    st.link(dve.tensor_tensor(masks[1][:, :, :], masks[1][:, :, :], per_channel(w[1][:, :], K), ALU.mult))
    st.link(dve.tensor_tensor(out, masks[0][:, :, :], masks[1][:, :, :], ALU.add))


TB = T // B


def split_weights(dve, st, w, remainder, same, cross):
    st.link(dve.tensor_copy(same[0], w))
    st.mark(dve.tensor_copy(cross[C:2 * C], w[C:2 * C]))
    st.link(dve.tensor_tensor(remainder, w, same[0], ALU.subtract))
    st.link(dve.tensor_copy(same[1], remainder))
    st.link(dve.tensor_tensor(cross[0:C], remainder[0:C], same[1][0:C], ALU.subtract))


def attention(nc, x, gamma, x_sb, stacks, ident, keys, pivots, ends_dram, kept, blocks_i, ends_f, starts_f):
    with ExitStack() as ctx:
        a = Arena(nc, ctx, "attention")
        zero = a.sb("zero", [1, 1])
        kept_up = a.sb("kept_up", [P, 1])
        kept_i = a.sb("kept_i", [P, 1], I32)
        zero_made = a.sem("zero_made")
        kept_in = a.sem("kept_in")
        kept_steps = a.sem("kept_steps")
        find = Search(nc, a, "edges", 0, zero[:, :], keys, pivots, ends_dram, ends_f, starts_f)
        y = a.sb("y", [P, TB, C])
        y1 = a.sb("y1", [P, TB, C])
        parts = a.sb("parts", [P, TB, 3, C])
        rough = a.sb("rough", [P, TB, C], BF16)
        aT = a.sb("aT", [C, TB * P])
        gam = a.sb("gam", [P, 1])
        top = a.sb("top", [C, 1])
        probs = a.sb("probs", [C, C])
        total = a.sb("total", [C, 1])
        part = a.sb("part", [C, 1])
        gram = a.ps("gram", [C, 512])
        mix = a.ps("mix", [P, TB * C])
        turned = a.ps("turned", [C, TB * P])
        turned1 = [a.ps(f"turned1_{n}", [P, TB * P]) for n in range(2)]
        n0 = Norm(a, "n0", TB, C, 1e-6)
        n1 = Norm(a, "n1", TB, C, 1e-5)
        x_in = a.sem("x_in")
        gam_in = a.sem("gam_in")
        steps = a.sem("dve_steps")
        y_ready = a.sem("y_ready")
        y_turned = a.sem("y_turned")
        aT_ready = a.sem("aT_ready")
        gram_ready = a.sem("gram_ready")
        shift_ready = a.sem("shift_ready")
        exp_ready = a.sem("exp_ready")
        probs_ready = a.sem("probs_ready")
        mix_ready = a.sem("mix_ready")
        normed = a.sem("normed")
        y1_ready = a.sem("y1_ready")
        y1_turned = a.sem("y1_turned")
        y1_copied = a.sem("y1_copied")
        block = ctx.enter_context(nc.Block())

        @block.sync
        def _(sp):
            sp.dma_start(gam[:, :], gamma.to_broadcast([P, 1])).then_inc(gam_in, 16)
            with nc.allow_non_contiguous_dma(reason="256 B rows"):
                sp.dma_start(x_sb[:, :, :], x.rearrange("b (t r) w c -> (r w) (b t) c", t=TB)).then_inc(x_in, 16)
            find.load_tops(sp)
            sp.wait_ge(zero_made, 1)
            find.shift(sp)
            sp.dma_start(kept[:, :], ends_dram[N:N + 1].partition_broadcast(P)).then_inc(kept_in, 16)

        @block.gpsimd
        def _(pool):
            find.gathers(pool)

        @block.vector
        def _(dve):
            dve.wait_ge(gam_in, 16)
            dve.wait_ge(x_in, 16)
            spare = dve.alloc_register(f"dve_spare_{a.phase}"), x_in, 16

            def image(b):
                st = LoopSteps(dve, steps, b, 21)
                xb = x_sb[:, bass.ds(b * TB, TB), :]
                n0.vector(dve, st, y[:, :, :], xb, b, y_ready)
                st.link(dve.tensor_tensor(xb, xb, y[:, :, :], ALU.add))
                dve.wait_ge(gram_ready, b + 1)
                dve.tensor_reduce(top[:, :], gram[:, 0:C], X, ALU.max, negate=True).then_inc(shift_ready, 1)
                dve.wait_ge(exp_ready, b + 1)
                st.link(dve.reciprocal(part[:, :], total[:, :]))
                dve.tensor_scalar(probs[:, :], probs[:, :], part[:, 0:1], None, ALU.mult).then_inc(probs_ready, 1)
                dve.wait_ge(mix_ready, b + 1)
                st.link_apart(dve.scalar_tensor_tensor(xb, mix[:, :].rearrange("p (t c) -> p t c", t=TB), gam[:, 0:1],
                                                       xb, ALU.mult, ALU.add), spare)
                n1.vector(dve, st, y1[:, :, :], xb, b, normed)
                st.link(dve.tensor_copy(rough[:, :, :], y1[:, :, :]))
                st.mark(dve.tensor_copy(parts[:, :, 1, :], rough[:, :, :]))
                st.link(dve.tensor_tensor(y1[:, :, :], y1[:, :, :], rough[:, :, :], ALU.subtract))
                st.link(dve.tensor_copy(rough[:, :, :], y1[:, :, :]))
                st.mark(dve.tensor_copy(parts[:, :, 0, :], rough[:, :, :]))
                st.link(dve.tensor_tensor(y1[:, :, :], y1[:, :, :], rough[:, :, :], ALU.subtract))
                dve.tensor_copy(parts[:, :, 2, :], y1[:, :, :]).then_inc(y1_ready, 1)
                dve.wait_ge(y1_turned, 2 * b + 2)
                st.end()

            dve.memset(zero[:, :], 0.0).then_inc(zero_made, 1)
            find.count(dve, 0)
            with dve.Fori(0, B // 2) as b:
                image(b)
            find.count(dve, 1)
            with dve.Fori(B // 2, B) as b:
                image(b)
            find.count(dve, 2)
            dve.wait_ge(kept_in, 16)
            st = Steps(dve, kept_steps)
            st.link(dve.tensor_scalar(kept_up[:, :], kept[:, :], 1.0, float(P * BLK - 1), ALU.max, ALU.add))
            st.link(dve.tensor_copy(kept_i[:, :], kept_up[:, :]))
            st.link(dve.tensor_scalar(blocks_i[:, :], kept_i[:, :], 13, None, ALU.logical_shift_right))

        @block.scalar
        def _(act):
            with act.Fori(0, B) as b:
                n0.scalar(act, b)
                act.wait_ge(y_turned, b + 1)
                act.activation(aT[:, :], turned[:, :], ACT.Copy).then_inc(aT_ready, 1)
                act.wait_ge(shift_ready, b + 1)
                act.activation(probs[:, :], gram[:, 0:C], ACT.Exp, bias=top[:, 0:1], accum_out=total[:, :])\
                    .then_inc(exp_ready, 1)
                n1.scalar(act, b)
                for n in range(2):
                    act.wait_ge(y1_turned, 2 * b + n + 1)
                    act.activation(stacks[n][:, bass.ds(b * TB * P, TB * P)], turned1[n][:, :], ACT.Copy)\
                        .then_inc(y1_copied, 1)

        @block.tensor
        def _(pe):
            spare = pe.alloc_register(f"pe_spare_{a.phase}"), gam_in, 16
            with pe.Fori(0, B) as b:
                pe.wait_ge(y_ready, b + 1)
                for t in range(TB):
                    ins = pe.matmul(gram[:, 0:C], y[:, t, :], y[:, t, :], start=(t == 0), stop=(t == TB - 1))
                ins.then_inc(gram_ready, 1)
                for t in range(TB):
                    ins = pe.transpose(turned[:, t * P:(t + 1) * P], y[:, t, :], ident[:, :])
                ins.then_inc(y_turned, 1)
                pe.wait_ge(aT_ready, b + 1)
                pe.wait_ge(probs_ready, b + 1)
                for t in range(TB):
                    ins = pe.matmul(mix[:, t * C:(t + 1) * C], aT[:, t * P:(t + 1) * P], probs[:, :],
                                    start=True, stop=True)
                ins.then_inc(mix_ready, 1)
                wait_apart(pe, y1_ready, b + 1, spare)
                for n in range(2):
                    for t in range(TB):
                        stack = parts[:, t, n:n + 2, :].rearrange("p n c -> p (n c)")
                        ins = pe.transpose(turned1[n][:, t * P:(t + 1) * P], stack, ident[:, :])
                    ins.then_inc(y1_turned, 1)


def gates(nc, gate_w, gate_b, stacks, weightsT, ident):
    K = gate_w.shape[1]
    with ExitStack() as ctx:
        a = Arena(nc, ctx, "gates")
        gw = a.sb("gw", [P, K])
        left = a.sb("left", [P, K])
        gws = [a.sb(f"gw_part{n}", [P, K], BF16) for n in range(3)]
        gb = a.sb("gb", [P, K])
        logits = a.sb("logits", [P, T, K])
        gap, gap_exp = a.sb("gap", [P, T]), a.sb("gap_exp", [P, T])
        dispatch = a.sb("dispatch", [P, T, K])
        rough = a.sb("rough", [P, T, K], BF16)
        parts = a.sb("parts", [P, T, 3, K])
        logit_ps = a.ps("logit_ps", [P, 2, 512])
        turned = a.ps("turned", [3 * K, 4, 512])
        loaded = a.sem("gate_in")
        split = a.sem("gate_split")
        logits_ready = a.sem("logits_ready")
        steps = a.sem("gate_steps")
        gap_ready = a.sem("gap_ready")
        gap_exp_ready = a.sem("gap_exp_ready")
        parts_ready = a.sem("parts_ready")
        bank_turned = a.sem("bank_turned")
        bank_copied = a.sem("bank_copied")
        block = ctx.enter_context(nc.Block())

        @block.sync
        def _(sp):
            sp.dma_start(gw[0:C, :], gate_w).then_inc(loaded, 16)
            sp.dma_start(gw[C:P, :], gate_w).then_inc(loaded, 16)
            sp.dma_start(gb[:, :], gate_b.partition_broadcast(P)).then_inc(loaded, 16)

        @block.tensor
        def _(pe):
            pe.wait_ge(split, 5)
            for t in range(T):
                for n in range(3):
                    ins = pe.matmul(logit_ps[:, t // 32, (t % 32) * K:(t % 32 + 1) * K],
                                    stacks[n // 2][:, t * P:(t + 1) * P], gws[n][:, :], start=(n == 0), stop=(n == 2))
            ins.then_inc(logits_ready, 1)
            pe.wait_ge(parts_ready, 1)
            for q in range(T // 4):
                if q >= 4:
                    pe.wait_ge(bank_copied, q - 3)
                for t in range(4 * q, 4 * q + 4):
                    ins = pe.transpose(turned[:, q % 4, (t % 4) * P:(t % 4 + 1) * P],
                                       parts[:, t, :, :].rearrange("p n k -> p (n k)"), ident[:, :])
                ins.then_inc(bank_turned, 1)

        @block.vector
        def _(dve):
            dve.wait_ge(loaded, 48)
            st = Steps(dve, split)
            split_weights(dve, st, gw[:, :], left[:, :], [gws[0][:, :], gws[1][:, :]], gws[2][:, :])
            st = Steps(dve, steps)
            dve.wait_ge(logits_ready, 1)
            bias = gb[:, :].unsqueeze(1).to_broadcast([P, 32, K])
            for n in range(2):
                st.mark(dve.tensor_tensor(logits[:, 32 * n:32 * n + 32, :],
                                          logit_ps[:, n, :].rearrange("p (t k) -> p t k", k=K), bias, ALU.add))
            dve.wait_ge(steps, st.n)
            masks, tops = top_two(dve, st, a, "gate", logits[:, :, :], T, K)
            two_weights(dve, st, a, "gate", dispatch[:, :, :], tops, masks, gap, gap_exp, gap_ready, gap_exp_ready)
            for n in range(2):
                st.link(dve.tensor_copy(rough[:, :, :], dispatch[:, :, :]))
                st.mark(dve.tensor_copy(parts[:, :, n, :], rough[:, :, :]))
                st.link(dve.tensor_tensor(dispatch[:, :, :], dispatch[:, :, :], rough[:, :, :], ALU.subtract))
            dve.tensor_copy(parts[:, :, 2, :], dispatch[:, :, :]).then_inc(parts_ready, 1)

        @block.scalar
        def _(act):
            act.wait_ge(gap_ready, 1)
            act.activation(gap_exp[:, :], gap[:, :], ACT.Exp).then_inc(gap_exp_ready, 1)
            for q in range(T // 4):
                act.wait_ge(bank_turned, q + 1)
                act.activation(weightsT[:, q * 512:(q + 1) * 512], turned[:, q % 4, :], ACT.Copy).then_inc(bank_copied, 1)


def experts(nc, w1, w2, w3, x_sb, stacks, weightsT, ident):
    K, H = w1.shape[0], w1.shape[2]
    G = 4 * P
    GROUPS = N // G
    LAG = 2
    with ExitStack() as ctx:
        a = Arena(nc, ctx, "experts")
        w = [a.sb(f"w{n}", [P, K * H]) for n in range(2)]
        left = a.sb("left", [P, K * H])
        ws = [[a.sb(f"w{m}_part{n}", [P, K * H], BF16) for n in range(3)] for m in range(2)]
        u3 = a.sb("u3", [H, K, C])
        pick = a.sb("pick", [3 * K, K])
        select = a.sb("select", [3 * K, K, H], BF16)
        add_halves = a.sb("add_halves", [P, C])
        gated = a.sb("gated", [H, 2, G])
        product = a.sb("product", [H, 2, G])
        hidden = a.sb("hidden", [H, 4, G])
        sums = a.sb("sums", [P, G])
        h1 = a.ps("h1", [H, 2, G])
        h2 = a.ps("h2", [H, 2, G])
        spread_w = a.ps("spread_w", [H, 2, G])
        acc = a.ps("acc", [P, G])
        back = a.ps("back", [P, G])
        loaded = a.sem("weights_in")
        made = a.sem("weights_split")
        h1_ready = a.sem("h1_ready")
        h2_ready = a.sem("h2_ready")
        h1_read = a.sem("h1_read")
        h2_read = a.sem("h2_read")
        hidden_ready = a.sem("hidden_ready")
        hidden_read = a.sem("hidden_read")
        acc_read = a.sem("acc_read")
        back_ready = a.sem("back_ready")
        added = a.sem("added")
        block = ctx.enter_context(nc.Block())

        @block.sync
        def _(sp):
            for n, source in enumerate((w1, w2)):
                for half in range(2):
                    sp.dma_start(w[n][half * C:(half + 1) * C, :].rearrange("c (e h) -> c e h", e=K),
                                 source.rearrange("e c h -> c e h")).then_inc(loaded, 16)
            sp.dma_start(u3[:, :, :], w3.rearrange("e h c -> h e c")).then_inc(loaded, 16)

        @block.tensor
        def _(pe):
            pe.wait_ge(loaded, 80)
            pe.wait_ge(made, 15)
            spare = pe.alloc_register(f"pe_spare_{a.phase}"), loaded, 80

            def out_product(n, e):
                wait_apart(pe, hidden_ready, n + 3, spare)
                half = (e % 2) * C
                pe.matmul(acc[half:half + C, :], u3[:, e, :], hidden[:, e % 4, :], start=(e < 2), stop=(e >= K - 2))\
                    .then_inc(hidden_read, 1)

            def turn_back(g):
                wait_apart(pe, acc_read, g + 2, spare)
                pe.wait_ge(added, g + 1)
                for q in range(4):
                    ins = pe.matmul(back[:, q * C:(q + 1) * C], sums[:, q * P:(q + 1) * P], add_halves[:, :],
                                    start=True, stop=True)
                ins.then_inc(back_ready, 1)

            def group(g, first):
                tokens = [s[:, bass.ds(g * G, G)] for s in stacks]
                for e in range(K):
                    n = g * K + e
                    wait_apart(pe, h1_read, n + 1, spare)
                    for part in range(3):
                        ins = pe.matmul(h1[:, e % 2, :], ws[0][part][:, e * H:(e + 1) * H], tokens[part // 2],
                                        start=(part == 0), stop=(part == 2))
                    ins.then_inc(h1_ready, 1)
                    wait_apart(pe, hidden_ready, n + 1, spare)
                    pe.matmul(spread_w[:, e % 2, :], select[:, e, :], weightsT[:, bass.ds(g * G, G)],
                              start=True, stop=True)
                    if e == LAG:
                        wait_apart(pe, acc_read, g + 1, spare)
                    for part in range(3):
                        ins = pe.matmul(h2[:, e % 2, :], ws[1][part][:, e * H:(e + 1) * H], tokens[part // 2],
                                        start=(part == 0), stop=(part == 2))
                    ins.then_inc(h2_ready, 1)
                    if e >= LAG or not first:
                        out_product(n - LAG, (e - LAG) % K)
                    if e == LAG + 1 and not first:
                        turn_back(g - 1)

            group(0, True)
            with pe.Fori(1, GROUPS) as g:
                group(g, False)
            for e in range(K - LAG, K):
                out_product((GROUPS - 1) * K + e, e)
            turn_back(GROUPS - 1)

        @block.scalar
        def _(act):
            act.wait_ge(made, 15)

            def copy_sums(g):
                act.wait_ge(back_ready, g + 1)
                act.wait_ge(hidden_read, g * K + K + 4)
                act.activation(sums[:, :], acc[:, :], ACT.Copy).then_inc(acc_read, 1)

            def group(g, first):
                for e in range(K):
                    n = g * K + e
                    act.wait_ge(h1_ready, n + 1)
                    act.wait_ge(h2_read, n + 1)
                    act.activation(gated[:, e % 2, :], h1[:, e % 2, :], ACT.Silu).then_inc(h1_read, 1)
                    if e == LAG - 1 and not first:
                        copy_sums(g - 1)

            group(0, True)
            with act.Fori(1, GROUPS) as g:
                group(g, False)
            copy_sums(GROUPS - 1)

        @block.vector
        def _(dve):
            for sem, free in ((h1_read, 2), (h2_read, 2), (hidden_ready, 2), (hidden_read, 4), (acc_read, 1),
                              (back_ready, 1), (added, 1)):
                dve.sem_inc(sem, free)
            st = Steps(dve, made)
            st.mark(dve.tensor_copy(add_halves[0:C, :], ident[0:C, 0:C]))
            st.mark(dve.tensor_copy(add_halves[C:P, :], ident[C:P, C:P]))
            st.link(dve.tensor_tensor(pick[:, :], ident[0:3 * K, 0:K], ident[0:3 * K, K:2 * K], ALU.add))
            st.link(dve.tensor_tensor(pick[:, :], pick[:, :], ident[0:3 * K, 2 * K:3 * K], ALU.add))
            st.mark(dve.tensor_copy(select[:, :, :], per_channel(pick[:, :], H)))
            dve.wait_ge(loaded, 80)
            for n in range(2):
                split_weights(dve, st, w[n][:, :], left[:, :], [ws[n][0][:, :], ws[n][1][:, :]], ws[n][2][:, :])
            assert st.n == 15
            spare = dve.alloc_register(f"dve_spare_{a.phase}"), loaded, 80

            def add_back(g):
                wait_apart(dve, back_ready, g + 2, spare)
                tiles = x_sb[:, bass.ds(g * 4, 4), :]
                dve.tensor_tensor(tiles, tiles, back[:, 0:4 * C].rearrange("p (q c) -> p q c", q=4), ALU.add)\
                    .then_inc(added, 1)

            def group(g, first):
                for e in range(K):
                    n = g * K + e
                    dve.wait_ge(h1_read, n + 3)
                    dve.wait_ge(h2_ready, n + 1)
                    dve.tensor_tensor(product[:, e % 2, :], gated[:, e % 2, :], h2[:, e % 2, :], ALU.mult)\
                        .then_inc(h2_read, 1)
                    dve.wait_ge(h2_read, n + 3)
                    dve.wait_ge(hidden_read, n + 1)
                    dve.tensor_tensor(hidden[:, e % 4, :], product[:, e % 2, :], spread_w[:, e % 2, :], ALU.mult)\
                        .then_inc(hidden_ready, 1)
                    if e == LAG + 1 and not first:
                        add_back(g - 1)

            group(0, True)
            with dve.Fori(1, GROUPS) as g:
                group(g, False)
            add_back(GROUPS - 1)


def convolve(nc, kernel_w, W_gat, att_src, att_dst, W1, b1, W2, b2, x_sb, eo, h_sb, as_sb, ad_sb, ident,
             keys, pivots, ends_dram, kept, ends_f, starts_f):
    S = 32
    PAD = S + 2
    K, H = W1.shape[0], W1.shape[2]
    with ExitStack() as ctx:
        a = Arena(nc, ctx, "convolve")
        find = Search(nc, a, "last_src", N, kept[0:1, :], keys, pivots, ends_dram, ends_f, starts_f)
        y = a.sb("y", [P, TB, C])
        y4 = a.sb("y4", [P, TB, C])
        padded = a.sb("padded", [C, 3, PAD, S])
        y4T = a.sb("y4T", [C, TB * P])
        cw = a.sb("cw", [C, 9, C])
        wg = a.sb("wg", [C, HEADS * NE])
        att = a.sb("att", [P, 2, HEADS * NE])
        u1 = a.sb("u1", [C, K, H])
        ub1 = a.sb("ub1", [H, K])
        u2 = a.sb("u2", [H, K, C])
        ub2 = a.sb("ub2", [P, K * C])
        hidden = a.sb("hidden", [H, K, TB * P])
        products = a.sb("products", [P, TB, HEADS * NE])
        n2 = Norm(a, "n2", TB, C, 1e-6)
        n3 = Norm(a, "n3", TB, C, 1e-5)
        turned = a.ps("turned", [C, TB * P])
        conv = a.ps("conv", [P, TB * C])
        feats = a.ps("feats", [P, 512])
        h1 = a.ps("h1", [H, 2, 512])
        outs = a.ps("outs", [P, 2, 512])
        loaded = a.sem("weights_in")
        signed = a.sem("signs_ready")
        steps = a.sem("dve_steps")
        y_ready = a.sem("y_ready")
        y_turned = a.sem("y_turned")
        padded_ready = a.sem("padded_ready")
        conv_ready = a.sem("conv_ready")
        y4_ready = a.sem("y4_ready")
        y4_turned = a.sem("y4_turned")
        y4T_ready = a.sem("y4T_ready")
        feats_ready = a.sem("feats_ready")
        h1_ready = a.sem("h1_ready")
        hidden_ready = a.sem("hidden_ready")
        outs_ready = a.sem("outs_ready")
        outs_free = a.sem("outs_free")
        block = ctx.enter_context(nc.Block())

        @block.gpsimd
        def _(pool):
            find.gathers(pool)

        @block.sync
        def _(sp):
            find.load_tops(sp)
            sp.dma_start(cw[:, :, :], kernel_w.rearrange("a b c d -> c (a b) d")).then_inc(loaded, 16)
            sp.dma_start(wg[:, :], W_gat).then_inc(loaded, 16)
            sp.dma_start(att[:, 0, :], att_src.rearrange("h k -> (h k)").partition_broadcast(P)).then_inc(loaded, 16)
            sp.dma_start(att[:, 1, :], att_dst.rearrange("h k -> (h k)").partition_broadcast(P)).then_inc(loaded, 16)
            sp.dma_start(u1[:, :, :], W1.rearrange("e c h -> c e h")).then_inc(loaded, 16)
            with nc.allow_non_contiguous_dma(reason="small bias"):
                sp.dma_start(ub1[:, :], b1.rearrange("e h -> h e")).then_inc(loaded, 16)
            sp.dma_start(u2[:, :, :], W2.rearrange("e h c -> h e c")).then_inc(loaded, 16)
            sp.dma_start(ub2[:, :], b2.rearrange("e c -> (e c)").partition_broadcast(P)).then_inc(loaded, 16)
            find.shift(sp)

        @block.vector
        def _(dve):
            dve.wait_ge(loaded, 128)
            st = Steps(dve, signed)
            st.link(dve.tensor_scalar(cw[:, :, :], cw[:, :, :], 0.0, None, ALU.is_ge))
            st.link(dve.tensor_scalar(cw[:, :, :], cw[:, :, :], 2.0, -1.0, ALU.mult, ALU.add))
            st.link(dve.memset(padded[:, :, :, :], 0.0))
            dve.sem_inc(outs_free, 2)
            spare = dve.alloc_register(f"dve_spare_{a.phase}"), signed, 3

            def image(b):
                st = LoopSteps(dve, steps, b, 18)
                xb = x_sb[:, bass.ds(b * TB, TB), :]
                n2.vector(dve, st, y[:, :, :], xb, b, y_ready)
                dve.wait_ge(conv_ready, b + 1)
                st.link_apart(dve.tensor_tensor(xb, xb, conv[:, :].rearrange("p (t c) -> p t c", t=TB), ALU.add), spare)
                n3.vector(dve, st, y4[:, :, :], xb, b, y4_ready)
                dve.wait_ge(feats_ready, b + 1)
                h = h_sb[:, bass.ds(b * TB, TB), :]
                st.link(dve.tensor_copy(h, feats[:, 0:TB * HEADS * NE].rearrange("p (t k) -> p t k", t=TB)))
                for n, to in enumerate((as_sb, ad_sb)):
                    st.link(dve.tensor_tensor(products[:, :, :], h,
                                              att[:, n, :].unsqueeze(1).to_broadcast([P, TB, HEADS * NE]), ALU.mult))
                    st.link(dve.tensor_reduce(to[:, bass.ds(b * TB, TB), :],
                                              products[:, :, :].rearrange("p t (h k) -> p t h k", k=NE), X, ALU.add))
                for n in range(TB // 2):
                    dve.wait_ge(outs_ready, b * (TB // 2) + n + 1)
                    dve.tensor_tensor(eo[:, bass.ds(b * TB + 2 * n, 2), :],
                                      outs[:, n % 2, :].rearrange("p (t k) -> p t k", t=2),
                                      ub2[:, :].unsqueeze(1).to_broadcast([P, 2, K * C]), ALU.add)\
                        .then_inc(outs_free, 1)
                st.end()

            find.count(dve, 0)
            with dve.Fori(0, B // 2) as b:
                image(b)
            find.count(dve, 1)
            with dve.Fori(B // 2, B) as b:
                image(b)
            find.count(dve, 2)

        @block.scalar
        def _(act):
            act.wait_ge(signed, 3)
            with act.Fori(0, B) as b:
                n2.scalar(act, b)
                act.wait_ge(y_turned, b + 1)
                image = turned[:, :].rearrange("c (r w) -> c r w", w=S)
                for w in range(3):
                    left, right = max(1 - w, 0), min(S, S + 1 - w)
                    act.activation(padded[:, w, 1:S + 1, left:right], image[:, :, left + w - 1:right + w - 1],
                                   ACT.Copy).then_inc(padded_ready, 1)
                n3.scalar(act, b)
                act.wait_ge(y4_turned, b + 1)
                act.activation(y4T[:, :], turned[:, :], ACT.Copy).then_inc(y4T_ready, 1)
                for e in range(K):
                    for s in range(2):
                        act.wait_ge(h1_ready, b * 2 * K + 2 * e + s + 1)
                        act.activation(hidden[:, e, s * 512:(s + 1) * 512], h1[:, s, :], ACT.Gelu, bias=ub1[:, e:e + 1])\
                            .then_inc(hidden_ready, 1)

        @block.tensor
        def _(pe):
            pe.wait_ge(signed, 3)
            spare = pe.alloc_register(f"pe_spare_{a.phase}"), signed, 3
            with pe.Fori(0, B) as b:
                wait_apart(pe, y_ready, b + 1, spare)
                for t in range(TB):
                    ins = pe.transpose(turned[:, t * P:(t + 1) * P], y[:, t, :], ident[:, :])
                ins.then_inc(y_turned, 1)
                pe.wait_ge(padded_ready, 3 * b + 3)
                for t in range(TB):
                    for tap in range(9):
                        r, w = 4 * t + tap // 3, tap % 3
                        ins = pe.matmul(conv[:, t * C:(t + 1) * C], padded[:, w, r:r + 4, :], cw[:, tap, :],
                                        start=(tap == 0), stop=(tap == 8))
                ins.then_inc(conv_ready, 1)
                wait_apart(pe, y4_ready, b + 1, spare)
                for t in range(TB):
                    ins = pe.transpose(turned[:, t * P:(t + 1) * P], y4[:, t, :], ident[:, :])
                ins.then_inc(y4_turned, 1)
                pe.wait_ge(y4T_ready, b + 1)
                for t in range(TB):
                    ins = pe.matmul(feats[:, t * HEADS * NE:(t + 1) * HEADS * NE], y4T[:, t * P:(t + 1) * P], wg[:, :],
                                    start=True, stop=True)
                ins.then_inc(feats_ready, 1)
                for e in range(K):
                    for s in range(2):
                        if e:
                            pe.wait_ge(hidden_ready, b * 2 * K + 2 * e + s - 1)
                        pe.matmul(h1[:, s, :], u1[:, e, :], y4T[:, s * 512:(s + 1) * 512], start=True, stop=True)\
                            .then_inc(h1_ready, 1)
                pe.wait_ge(hidden_ready, (b + 1) * 2 * K)
                for n in range(TB // 2):
                    pe.wait_ge(outs_free, b * (TB // 2) + n + 1)
                    for t in range(2 * n, 2 * n + 2):
                        for e in range(K):
                            at = (t % 2) * K * C + e * C
                            ins = pe.matmul(outs[:, n % 2, at:at + C], hidden[:, e, t * P:(t + 1) * P], u2[:, e, :],
                                            start=True, stop=True)
                    ins.then_inc(outs_ready, 1)


def write_table(nc, h_sb, as_sb, ad_sb, rows, table, a_dst):
    with ExitStack() as ctx:
        a = Arena(nc, ctx, "write_table")
        made = a.sem("rows_made")
        stored = a.sem("rows_stored")
        block = ctx.enter_context(nc.Block())

        @block.vector
        def _(dve):
            st = Steps(dve, made)
            st.link(dve.memset(rows[:, :, :], 1.0))
            for h in range(HEADS):
                st.mark(dve.tensor_copy(rows[:, :, h * 5 + 1:h * 5 + 5], h_sb[:, :, h * NE:(h + 1) * NE]))
            st.link(dve.tensor_copy(rows[:, :, Q:ROW], as_sb[:, :, :]))

        @block.sync
        def _(sp):
            sp.wait_ge(made, 6)
            sp.dma_start(table.rearrange("(t p) k -> p t k", p=P), rows[:, :, :]).then_inc(stored, 16)
            sp.dma_start(a_dst.rearrange("(t p) k -> p t k", p=P), ad_sb[:, :, :]).then_inc(stored, 16)
            sp.wait_ge(stored, 32)


def spread(nc, keys_dram, ends_f, starts_f, ad_sb, a_dst_dram, edge_ad_dram, blocks_i, chunk_f, first_dst):
    with ExitStack() as ctx:
        a = Arena(nc, ctx, "spread")
        empty = a.sb("empty", [P, T])
        to_f = a.sb("to_f", [P, T])
        to = a.sb("to", [P, T], U32)
        part = a.sb("part", [P, 1], I32)
        part_f = a.sb("part_f", [P, 1])
        blocks_f = a.sb("blocks_f", [P, 1])
        chunk_i = a.sb("chunk_i", [P, 1], U32)
        keys = a.sb("keys", [P, BLK], I32)
        dst = a.sb("dst", [P, 1], I32)
        known = a.sb("known", [P, 1])
        first_i = a.sb("first_i", [P, 1], U32)
        first_ad = a.sb("first_ad", [P, HEADS])
        cut_f = a.sb("cut_f", [P, 1])
        cut_i = a.sb("cut_i", [P, 1], U32)
        steps = a.sem("spread_steps")
        made = a.sem("made")
        keys_in = a.sem("keys_in")
        ad_in = a.sem("ad_in")
        written = a.sem("edge_ad_written")
        block = ctx.enter_context(nc.Block())

        @block.vector
        def _(dve):
            st = Steps(dve, steps)
            st.link(dve.tensor_tensor(empty[:, :], starts_f[:, :], ends_f[:, :], ALU.is_equal))
            st.link(dve.scalar_tensor_tensor(to_f[:, :], empty[:, :], float(2 * E), starts_f[:, :], ALU.mult, ALU.add))
            st.link(dve.tensor_copy(to[:, :], to_f[:, :]))
            dve.wait_ge(made, 1)
            st.mark(dve.tensor_copy(part_f[:, :], part[:, :]))
            st.link(dve.tensor_copy(blocks_f[:, :], blocks_i[:, :]))
            st.link(dve.tensor_tensor(chunk_f[:, :], part_f[:, :], blocks_f[:, :], ALU.mult))
            st.link(dve.tensor_copy(chunk_i[:, :], chunk_f[:, :]))
            dve.wait_ge(keys_in, 16)
            st.link(dve.tensor_scalar(dst[:, :], keys[:, 0:1], SRC_BITS, FIELDS - 1, ALU.logical_shift_right,
                                      ALU.bitwise_and))
            st.link(dve.tensor_copy(first_dst[:, :], dst[:, :]))
            st.link(dve.tensor_scalar(known[:, :], first_dst[:, :], N - 1.0, None, ALU.min))
            st.link(dve.tensor_copy(first_i[:, :], known[:, :]))
            st.link(dve.tensor_scalar(cut_f[:, :], chunk_f[:, :], float(BLK), None, ALU.mult))
            st.link(dve.tensor_copy(cut_i[:, :], cut_f[:, :]))

        @block.gpsimd
        def _(pool):
            pool.iota(part[:, :], pattern=[[0, 1]], base=0, channel_multiplier=1).then_inc(made, 1)
            pool.wait_ge(steps, 3)
            for t in range(T):
                pool.indirect_dma_start(edge_ad_dram, bass.IndirectOffsetOnAxis(ap=to[:, t:t + 1], axis=0),
                                        ad_sb[:, t, :], None, bounds_check=E - 1, oob_is_err=False)\
                    .then_inc(written, 16)
            pool.wait_ge(steps, 7)
            gather(pool, keys[:, :].bitcast(F32), keys_dram.rearrange("(r c) -> r c", c=BLK), chunk_i[:, :], keys_in)
            pool.wait_ge(steps, 13)
            gather(pool, first_ad[:, :], a_dst_dram, first_i[:, :], ad_in)
            pool.wait_ge(ad_in, 16)
            pool.wait_ge(written, 16 * T)
            pool.indirect_dma_start(edge_ad_dram, bass.IndirectOffsetOnAxis(ap=cut_i[:, :], axis=0),
                                    first_ad[:, :], None).then_inc(written, 16)
            pool.wait_ge(written, 16 * (T + 1))


def edge_loop(nc, keys_dram, table, edge_ad_dram, edge_rows_dram, blocks_i, chunk_f, last_dst, state):
    W = BLK // 2
    W1 = W + 1
    with ExitStack() as ctx:
        a = Arena(nc, ctx, "edges")

        def slots(name, shape, dt=F32):
            return [a.sb(f"{name}{s}", shape, dt) for s in range(2)]

        def slot_sems(name):
            return [a.sem(f"{name}{s}") for s in range(2)]

        keys = slots("keys", [P, W], I32)
        dst = a.sb("dst", [P, W], I32)
        src = slots("src", [P, W], I32)
        dst_f = slots("dst_f", [P, W1])
        keep = slots("keep", [P, HEADS, W1])
        fresh = slots("fresh", [P, HEADS, W1])
        key_f = slots("key_f", [P, 1])
        key_i = slots("key_i", [P, 1], U32)
        out_f = slots("out_f", [P, 1])
        out_i = slots("out_i", [P, 1], U32)
        ad_i = slots("ad_i", [P, 1], U32)
        rows = slots("rows", [P, W, ROW])
        ad = slots("ad", [P, W, HEADS])
        out = slots("out", [P, W, ROW])
        starts = a.sb("starts", [P, HEADS, W1])
        held = a.sb("held", [P, HEADS, W1])
        raw = a.sb("raw", [P, HEADS, W])
        score = a.sb("score", [P, HEADS, W1])
        tops = a.sb("tops", [P, HEADS, W1])
        before = a.sb("before", [P, HEADS, W])
        gaps = a.sb("gaps", [P, 2, HEADS, W])
        weight = a.sb("weight", [P, HEADS, W])
        decay = a.sb("decay", [P, Q, W1])
        terms = a.sb("terms", [P, Q, W1])
        sums = a.sb("sums", [P, Q, W1])
        key_i_ready = slot_sems("key_i_ready")
        keys_in = slot_sems("keys_in")
        ad_in = slot_sems("ad_in")
        src_ready = slot_sems("src_ready")
        rows_in = slot_sems("rows_in")
        summed = slot_sems("summed")
        copied = slot_sems("copied")
        stored = slot_sems("stored")
        steps = a.sem("edge_steps")
        first = a.sem("first_steps")
        gaps_ready = a.sem("gaps_ready")
        weights_ready = a.sem("weights_ready")
        block = ctx.enter_context(nc.Block())
        key_rows = keys_dram.rearrange("(r c) -> r c", c=W)
        ad_rows = edge_ad_dram.rearrange("(r c) k -> r (c k)", c=W)
        out_rows = edge_rows_dram.rearrange("(r c) k -> r (c k)", c=W)
        LAST = E // W - 1

        def flat(v):
            return v[:, :, :].rearrange("p h w -> p (h w)")

        def wide(v):
            return v.unsqueeze(1).to_broadcast([P, HEADS, W])

        def prepare(dve, st, s):
            st.link(dve.tensor_scalar(key_f[s][:, :], key_f[s][:, :], 2.0, None, ALU.add))
            dve.tensor_copy(key_i[s][:, :], key_f[s][:, :]).then_inc(key_i_ready[s], 1)
            st.link(dve.tensor_scalar(dst[:, :], keys[s][:, :], SRC_BITS, FIELDS - 1, ALU.logical_shift_right,
                                      ALU.bitwise_and))
            dve.tensor_scalar(src[s][:, :], keys[s][:, :], N - 1, None, ALU.bitwise_and).then_inc(src_ready[s], 1)
            st.mark(dve.tensor_copy(dst_f[s][:, 0:1], dst_f[1 - s][:, W:W1]))
            st.link(dve.tensor_copy(dst_f[s][:, 1:W1], dst[:, :]))
            st.link(dve.tensor_tensor(keep[s][:, :, 1:W1], wide(dst_f[s][:, 1:W1]), wide(dst_f[s][:, 0:W]),
                                      ALU.is_equal))
            st.link(dve.tensor_scalar(fresh[s][:, :, 1:W1], keep[s][:, :, 1:W1], 1.0, -FAR, ALU.subtract, ALU.mult))

        @block.gpsimd
        def _(pool):
            blocks = pool.value_load(blocks_i[0:1, 0:1], min_val=1, max_val=EC // BLK)
            last = pool.alloc_register("pool_last_block")
            pool.reg_mov(last, LAST)
            pool.wait_ge(first, 22)
            for s in range(2):
                gather(pool, keys[s][:, :].bitcast(F32), key_rows, key_i[s][:, :], keys_in[s], bound=last)
            gather(pool, ad[0][:, :, :].rearrange("p c k -> p (c k)"), ad_rows, ad_i[0][:, :], ad_in[0], bound=last)
            spare = pool.alloc_register("pool_spare"), first, 22
            with pool.Fori(0, blocks) as i:
                for s in range(2):
                    o = 1 - s
                    wait_apart(pool, src_ready[s], i + 1, spare)
                    pool.wait_ge(key_i_ready[s], i + 1)
                    pool.wait_ge(summed[s], i)
                    gather(pool, keys[s][:, :].bitcast(F32), key_rows, key_i[s][:, :], keys_in[s], bound=last)
                    for c in range(W):
                        gather(pool, rows[s][:, c, :], table, src[s][:, c:c + 1].bitcast(U32), rows_in[s])
                    wait_apart(pool, copied[o], i + s, spare)
                    pool.indirect_dma_start(out_rows, bass.IndirectOffsetOnAxis(ap=out_i[o][:, :], axis=0),
                                            out[o][:, :, :].rearrange("p c k -> p (c k)"), None,
                                            bounds_check=last, oob_is_err=False).then_inc(stored[o], 16)
                    wait_apart(pool, summed[o], i + s, spare)
                    gather(pool, ad[o][:, :, :].rearrange("p c k -> p (c k)"), ad_rows, ad_i[o][:, :], ad_in[o],
                           bound=last)
            wait_apart(pool, copied[1], blocks, spare)
            pool.indirect_dma_start(out_rows, bass.IndirectOffsetOnAxis(ap=out_i[1][:, :], axis=0),
                                    out[1][:, :, :].rearrange("p c k -> p (c k)"), None,
                                    bounds_check=last, oob_is_err=False).then_inc(stored[1], 16)
            for s in range(2):
                pool.wait_ge(stored[s], blocks * 16 + 16 * s)
                pool.wait_ge(keys_in[s], blocks * 16 + 16)
                pool.wait_ge(ad_in[s], blocks * 16 + 16 * (1 - s))

        @block.vector
        def _(dve):
            blocks = dve.value_load(blocks_i[0:1, 0:1], min_val=1, max_val=EC // BLK)
            st = Steps(dve, first)
            for s in range(2):
                st.mark(dve.memset(keep[s][:, :, 0:1], 0.0))
                st.mark(dve.memset(fresh[s][:, :, 0:1], FAR))
                st.mark(dve.memset(ad[s][:, :, :], 0.0))
                st.mark(dve.memset(out[s][:, :, :], 0.0))
                st.mark(dve.memset(keys[s][:, :], 0))
                st.mark(dve.tensor_scalar(key_f[s][:, :], chunk_f[:, :], 2.0, float(s), ALU.mult, ALU.add))
                st.link(dve.tensor_scalar(out_f[s][:, :], chunk_f[:, :], 2.0, float(s), ALU.mult, ALU.add))
                st.mark(dve.tensor_copy(key_i[s][:, :], key_f[s][:, :]))
                st.mark(dve.tensor_copy(ad_i[s][:, :], out_f[s][:, :]))
            st.link(dve.memset(starts[:, :, :], 0.0))
            st.link(dve.memset(dst_f[1][:, W:W1], float(2 * E)))
            st.link(dve.tensor_copy(out_i[1][:, :], dst_f[1][:, W:W1]))
            st.link(dve.memset(dst_f[1][:, W:W1], -1.0))
            assert st.n == 22
            st.mark(dve.memset(decay[:, :, 0:1], 0.0))
            st.mark(dve.memset(held[:, :, W:W1], 0.0))
            st.mark(dve.memset(tops[:, :, W:W1], NONE))
            st.link(dve.memset(sums[:, :, W:W1], 0.0))
            for s in range(2):
                dve.wait_ge(keys_in[s], 16)
                prepare(dve, st, s)
            spare = dve.alloc_register("dve_spare_edges"), first, 22
            with dve.Fori(0, blocks) as i:
                st = LoopSteps(dve, steps, i, 42)
                for s in range(2):
                    o = 1 - s
                    dve.wait_ge(ad_in[s], i * 16 + 16)
                    st.mark(dve.tensor_copy(starts[:, :, 0:1], held[:, :, W:W1]))
                    st.link(dve.tensor_copy(starts[:, :, 1:W1], ad[s][:, :, :].rearrange("p w h -> p h w")))
                    st.link(dve.tensor_tensor_scan(flat(held), flat(keep[s]), flat(starts), 0.0, ALU.mult, ALU.add))
                    dve.wait_ge(rows_in[s], i * (16 * W) + 16 * W)
                    st.link(dve.tensor_tensor(raw[:, :, :], rows[s][:, :, Q:ROW].rearrange("p w h -> p h w"),
                                              held[:, :, 1:W1], ALU.add))
                    st.mark(dve.tensor_copy(score[:, :, 0:1], tops[:, :, W:W1]))
                    st.link(dve.scalar_tensor_tensor(score[:, :, 1:W1], raw[:, :, :], 0.2, raw[:, :, :],
                                                     ALU.mult, ALU.max))
                    dve.wait_ge(copied[o], i + s)
                    st.link(dve.tensor_tensor_scan(flat(tops), flat(fresh[s]), flat(score), 0.0, ALU.add, ALU.max))
                    st.mark(dve.tensor_tensor(gaps[:, 1, :, :], score[:, :, 1:W1], tops[:, :, 1:W1], ALU.subtract))
                    st.link(dve.tensor_tensor(before[:, :, :], tops[:, :, 0:W], fresh[s][:, :, 1:W1], ALU.add))
                    dve.tensor_tensor(gaps[:, 0, :, :], before[:, :, :], tops[:, :, 1:W1], ALU.subtract)\
                        .then_inc(gaps_ready, 1)
                    dve.wait_ge(stored[s], i * 16 + 16 * s)
                    st.mark(dve.tensor_copy(out_i[s][:, :], out_f[s][:, :]))
                    st.mark(dve.tensor_copy(last_dst[:, :], dst_f[s][:, W:W1]))
                    st.link(dve.tensor_copy(terms[:, :, 0:1], sums[:, :, W:W1]))
                    st.link(dve.tensor_scalar(out_f[s][:, :], out_f[s][:, :], 2.0, None, ALU.add))
                    st.mark(dve.tensor_copy(ad_i[s][:, :], out_f[s][:, :]))
                    dve.wait_ge(weights_ready, i * 2 + s + 1)
                    per_head = terms[:, :, 1:W1].rearrange("p (h k) w -> p h k w", h=HEADS)
                    st.link(dve.tensor_tensor(per_head, rows[s][:, :, 0:Q].rearrange("p w (h k) -> p h k w", h=HEADS),
                                              weight[:, :, :].unsqueeze(2).to_broadcast([P, HEADS, NE + 1, W]),
                                              ALU.mult))
                    dve.tensor_tensor_scan(flat(sums), flat(decay), flat(terms), 0.0, ALU.mult, ALU.add)\
                        .then_inc(summed[s], 1)
                    dve.wait_ge(keys_in[s], i * 16 + 32)
                    prepare(dve, st, s)
                st.end()
            dve.wait_ge(summed[1], blocks)
            dve.tensor_copy(state[:, 0:Q], sums[:, :, W]).then_inc(first, 1)
            dve.tensor_copy(state[:, Q:ROW], tops[:, :, W]).then_inc(first, 1)

        @block.scalar
        def _(act):
            blocks = act.value_load(blocks_i[0:1, 0:1], min_val=1, max_val=EC // BLK)
            with act.Fori(0, blocks) as i:
                for s in range(2):
                    act.wait_ge(gaps_ready, i * 2 + s + 1)
                    act.activation(weight[:, :, :], gaps[:, 1, :, :], ACT.Exp)
                    act.activation(decay[:, :, 1:W1].rearrange("p (h k) w -> p h k w", h=HEADS),
                                   gaps[:, 0, :, :].unsqueeze(2).to_broadcast([P, HEADS, NE + 1, W]), ACT.Exp)\
                        .then_inc(weights_ready, 1)
                    act.wait_ge(summed[s], i + 1)
                    act.activation(out[s][:, :, 0:Q], sums[:, :, 1:W1].rearrange("p q w -> p w q"), ACT.Copy)
                    act.activation(out[s][:, :, Q:ROW], tops[:, :, 1:W1].rearrange("p h w -> p w h"), ACT.Copy)\
                        .then_inc(copied[s], 1)


def join_chunks(nc, ends_dram, edge_rows_dram, ident, chunk_f, blocks_i, first_dst, last_dst, state):
    W1 = P + 1
    with ExitStack() as ctx:
        a = Arena(nc, ctx, "join")
        cols = a.sb("cols", [P, 4, Q])
        row = a.sb("row", [Q, 4, P])
        same = a.sb("same", [Q, P])
        pens = a.sb("pens", [Q, P])
        joined = a.sb("joined", [Q, P])
        none = a.sb("none", [Q, P])
        tops = a.sb("tops", [Q, P])
        gaps = a.sb("gaps", [Q, 2, P])
        exps = a.sb("exps", [Q, 2, P])
        terms = a.sb("terms", [Q, P])
        sums = a.sb("sums", [Q, P])
        carry = a.sb("carry", [Q, 2, P])
        back = a.sb("back", [P, 2, Q])
        node_f = a.sb("node_f", [P, 1])
        node_i = a.sb("node_i", [P, 1], U32)
        end_f = a.sb("end_f", [P, 1])
        limit = a.sb("limit", [P, 1])
        blocks_f = a.sb("blocks_f", [P, 1])
        beyond = a.sb("beyond", [P, 1])
        last_i = a.sb("last_i", [P, 1], U32)
        old = a.sb("old", [P, ROW])
        new = a.sb("new", [P, ROW])
        gap2 = a.sb("gap2", [P, 2, HEADS])
        exp2 = a.sb("exp2", [P, 2, HEADS])
        part2 = a.sb("part2", [P, 2, Q])
        turned = a.ps("turned", [Q, 4 * P])
        returned = a.ps("returned", [P, 2 * Q])
        steps = a.sem("join_steps")
        cols_turned = a.sem("cols_turned")
        gaps_ready = a.sem("gaps_ready")
        exps_ready = a.sem("exps_ready")
        carry_turned = a.sem("carry_turned")
        end_in = a.sem("end_in")
        old_in = a.sem("old_in")
        gap2_ready = a.sem("gap2_ready")
        exp2_ready = a.sem("exp2_ready")
        fixed = a.sem("rows_fixed")
        marks = {}
        block = ctx.enter_context(nc.Block())

        @block.vector
        def _(dve):
            st = Steps(dve, steps)
            per_head = cols[:, 1, :].rearrange("p (h k) -> p h k", h=HEADS)
            st.mark(dve.tensor_copy(cols[:, 0, :], state[:, 0:Q]))
            st.mark(dve.tensor_copy(per_head, per_channel(state[:, Q:ROW], NE + 1)))
            st.mark(dve.tensor_copy(cols[:, 2, :], last_dst[:, :].to_broadcast([P, Q])))
            st.link(dve.tensor_copy(cols[:, 3, :], first_dst[:, :].to_broadcast([P, Q])))
            marks["cols"] = st.n
            st.link(dve.tensor_scalar(node_f[:, :], first_dst[:, :], 1.0, float(N), ALU.add, ALU.min))
            st.link(dve.tensor_copy(node_i[:, :], node_f[:, :]))
            marks["node"] = st.n
            st.mark(dve.memset(old[:, :], 0.0))
            st.link(dve.tensor_copy(blocks_f[:, :], blocks_i[:, :]))
            st.link(dve.tensor_tensor(limit[:, :], chunk_f[:, :], blocks_f[:, :], ALU.add))
            st.link(dve.tensor_scalar(limit[:, :], limit[:, :], float(BLK), None, ALU.mult))
            dve.wait_ge(end_in, 16)
            st.link(dve.tensor_tensor(beyond[:, :], end_f[:, :], limit[:, :], ALU.is_gt))
            st.link(dve.scalar_tensor_tensor(beyond[:, :], first_dst[:, :], float(N), beyond[:, :], ALU.is_ge, ALU.add))
            st.link(dve.tensor_scalar(end_f[:, :], end_f[:, :], 1.0, None, ALU.subtract))
            st.link(dve.scalar_tensor_tensor(end_f[:, :], beyond[:, :], float(2 * E), end_f[:, :], ALU.mult, ALU.add))
            st.link(dve.tensor_copy(last_i[:, :], end_f[:, :]))
            marks["last"] = st.n
            dve.wait_ge(cols_turned, 1)
            st.link(dve.tensor_copy(row[:, :, :], turned[:, :].rearrange("q (n p) -> q n p", n=4)))
            st.mark(dve.memset(same[:, 0:1], 0.0))
            st.mark(dve.memset(joined[:, 0:1], 0.0))
            st.mark(dve.tensor_tensor(same[:, 1:P], row[:, 2, 1:P], row[:, 2, 0:P - 1], ALU.is_equal))
            st.link(dve.tensor_tensor(joined[:, 1:P], row[:, 3, 1:P], row[:, 2, 0:P - 1], ALU.is_equal))
            st.link(dve.tensor_scalar(pens[:, :], same[:, :], 1.0, -FAR, ALU.subtract, ALU.mult))
            st.link(dve.tensor_tensor_scan(tops[:, :], pens[:, :], row[:, 1, :], 0.0, ALU.add, ALU.max))
            st.mark(dve.tensor_tensor(gaps[:, 1, :], row[:, 1, :], tops[:, :], ALU.subtract))
            st.mark(dve.memset(gaps[:, 0, 0:1], FAR))
            st.link(dve.tensor_tensor(gaps[:, 0, 1:P], tops[:, 0:P - 1], pens[:, 1:P], ALU.add))
            dve.tensor_tensor(gaps[:, 0, 1:P], gaps[:, 0, 1:P], tops[:, 1:P], ALU.subtract).then_inc(gaps_ready, 1)
            dve.wait_ge(exps_ready, 1)
            st.link(dve.tensor_tensor(terms[:, :], row[:, 0, :], exps[:, 1, :], ALU.mult))
            st.link(dve.tensor_tensor_scan(sums[:, :], exps[:, 0, :], terms[:, :], 0.0, ALU.mult, ALU.add))
            st.link(dve.memset(carry[:, :, :], 0.0))
            st.mark(dve.tensor_tensor(carry[:, 0, 1:P], sums[:, 0:P - 1], joined[:, 1:P], ALU.mult))
            st.link(dve.tensor_tensor(carry[:, 1, 1:P], tops[:, 0:P - 1], joined[:, 1:P], ALU.mult))
            st.link(dve.tensor_scalar(none[:, :], joined[:, :], 1.0, -NONE, ALU.subtract, ALU.mult))
            st.link(dve.tensor_tensor(carry[:, 1, :], carry[:, 1, :], none[:, :], ALU.add))
            marks["carry"] = st.n
            dve.wait_ge(carry_turned, 1)
            st.link(dve.tensor_copy(back[:, :, :], returned[:, :].rearrange("p (n q) -> p n q", n=2)))
            dve.wait_ge(old_in, 16)
            carried = back[:, 1, 0:Q:NE + 1]
            st.link(dve.tensor_tensor(new[:, Q:ROW], old[:, Q:ROW], carried, ALU.max))
            st.mark(dve.tensor_tensor(gap2[:, 0, :], old[:, Q:ROW], new[:, Q:ROW], ALU.subtract))
            dve.tensor_tensor(gap2[:, 1, :], carried, new[:, Q:ROW], ALU.subtract).then_inc(gap2_ready, 1)
            dve.wait_ge(steps, st.n)
            dve.wait_ge(exp2_ready, 1)
            for n, sums_n in enumerate((old[:, 0:Q], back[:, 0, :])):
                st.link(dve.tensor_tensor(part2[:, n, :].rearrange("p (h k) -> p h k", h=HEADS),
                                          sums_n.rearrange("p (h k) -> p h k", h=HEADS),
                                          per_channel(exp2[:, n, :], NE + 1), ALU.mult))
            st.link(dve.tensor_tensor(new[:, 0:Q], part2[:, 0, :], part2[:, 1, :], ALU.add))
            marks["new"] = st.n

        @block.tensor
        def _(pe):
            pe.wait_ge(steps, marks["cols"])
            for n in range(4):
                ins = pe.transpose(turned[:, n * P:(n + 1) * P], cols[:, n, :], ident[:, :])
            ins.then_inc(cols_turned, 1)
            pe.wait_ge(steps, marks["carry"])
            for n in range(2):
                ins = pe.transpose(returned[:, n * Q:(n + 1) * Q], carry[:, n, :], ident[0:Q, 0:Q])
            ins.then_inc(carry_turned, 1)

        @block.scalar
        def _(act):
            act.wait_ge(gaps_ready, 1)
            act.wait_ge(steps, marks["last"])
            act.activation(exps[:, :, :], gaps[:, :, :], ACT.Exp).then_inc(exps_ready, 1)
            act.wait_ge(gap2_ready, 1)
            act.activation(exp2[:, :, :], gap2[:, :, :], ACT.Exp).then_inc(exp2_ready, 1)

        @block.gpsimd
        def _(pool):
            pool.wait_ge(steps, marks["node"])
            gather(pool, end_f[:, :], ends_dram.rearrange("(n a) -> n a", a=1), node_i[:, :], end_in)
            pool.wait_ge(steps, marks["last"])
            gather(pool, old[:, :], edge_rows_dram, last_i[:, :], old_in, bound=E - 1)
            pool.wait_ge(steps, marks["new"])
            pool.indirect_dma_start(edge_rows_dram, bass.IndirectOffsetOnAxis(ap=last_i[:, :], axis=0), new[:, :], None,
                                    bounds_check=E - 1, oob_is_err=False).then_inc(fixed, 16)
            pool.wait_ge(fixed, 16)


def route(nc, b_gat, ln_gamma, ln_beta, edge_rows_dram, table, ends_f, starts_f, last_ends, last_starts, rows,
          ad_sb, x_sb, eo, out_dram):
    F = HEADS * NE
    with ExitStack() as ctx:
        a = Arena(nc, ctx, "route")
        edge = a.sb("edge", [P, T, ROW])
        empty = a.sb("empty", [P, T])
        at_f = a.sb("at_f", [P, T])
        at = a.sb("at", [P, T], U32)
        vec = a.sb("vec", [P, 3, F])
        mine = a.sb("mine", [P, T, HEADS])
        top = a.sb("top", [P, T, HEADS])
        last_row = a.sb("last_row", [P, ROW])
        times = a.sb("times", [P, T])
        absent = a.sb("absent", [P, T])
        shared = a.sb("shared", [P, T, HEADS])
        gap = a.sb("gap", [P, 3, T, HEADS])
        e2 = a.sb("e2", [P, 3, T, HEADS])
        part = a.sb("part", [P, T, Q])
        part3 = a.sb("part3", [P, T, Q])
        total = a.sb("total", [P, T, Q])
        inverse = a.sb("inverse", [P, T, HEADS])
        agg = a.sb("agg", [P, T, F])
        scores = a.sb("scores", [P, T, NE])
        gate = a.sb("gate", [P, T, NE])
        gap2, gap2_exp = a.sb("gap2", [P, T]), a.sb("gap2_exp", [P, T])
        weighted = a.sb("weighted", [P, TB, NE * C])
        summed = a.sb("summed", [P, TB, C])
        norm = Norm(a, "norm", T, F, 1e-5)
        vec_in = a.sem("vec_in")
        last_in = a.sem("last_in")
        steps = a.sem("route_steps")
        edge_in = a.sem("edge_in")
        gaps_ready = a.sem("gaps_ready")
        exps_ready = a.sem("exps_ready")
        normed = a.sem("normed")
        gap2_ready = a.sem("gap2_ready")
        gap2_exp_ready = a.sem("gap2_exp_ready")
        result = a.sem("result_ready")
        stored = a.sem("result_stored")
        marks = {}
        block = ctx.enter_context(nc.Block())

        @block.vector
        def _(dve):
            st = Steps(dve, steps)
            st.mark(dve.memset(edge[:, :, 0:Q], 0.0))
            st.mark(dve.memset(edge[:, :, Q:ROW], NONE))
            st.mark(dve.tensor_tensor(empty[:, :], starts_f[:, :], ends_f[:, :], ALU.is_equal))
            st.link(dve.tensor_scalar(at_f[:, :], ends_f[:, :], 1.0, None, ALU.subtract))
            st.link(dve.scalar_tensor_tensor(at_f[:, :], empty[:, :], float(2 * E), at_f[:, :], ALU.mult, ALU.add))
            st.link(dve.tensor_scalar(at_f[:, :], at_f[:, :], 0.0, None, ALU.max))
            st.link(dve.tensor_copy(at[:, :], at_f[:, :]))
            marks["at"] = st.n
            st.link(dve.tensor_tensor(mine[:, :, :], rows[:, :, Q:ROW], ad_sb[:, :, :], ALU.add))
            st.link(dve.scalar_tensor_tensor(mine[:, :, :], mine[:, :, :], 0.2, mine[:, :, :], ALU.mult, ALU.max))
            dve.wait_ge(last_in, 16)
            st.link(dve.tensor_tensor(times[:, :], last_ends[:, :], last_starts[:, :], ALU.subtract))
            st.mark(dve.tensor_scalar(absent[:, :], times[:, :], 0.0, NONE, ALU.is_le, ALU.mult))
            st.link(dve.tensor_tensor(shared[:, :, :], last_row[:, Q:ROW].unsqueeze(1).to_broadcast([P, T, HEADS]),
                                      ad_sb[:, :, :], ALU.add))
            st.link(dve.scalar_tensor_tensor(shared[:, :, :], shared[:, :, :], 0.2, shared[:, :, :], ALU.mult, ALU.max))
            st.link(dve.tensor_tensor(shared[:, :, :], shared[:, :, :], per_channel(absent[:, :], HEADS), ALU.add))
            st.link(dve.tensor_tensor(top[:, :, :], mine[:, :, :], shared[:, :, :], ALU.max))
            dve.wait_ge(edge_in, 16 * T)
            st.link(dve.tensor_tensor(top[:, :, :], top[:, :, :], edge[:, :, Q:ROW], ALU.max))
            st.mark(dve.tensor_tensor(gap[:, 2, :, :], shared[:, :, :], top[:, :, :], ALU.subtract))
            st.mark(dve.tensor_tensor(gap[:, 0, :, :], edge[:, :, Q:ROW], top[:, :, :], ALU.subtract))
            marks["gaps"] = st.n
            dve.tensor_tensor(gap[:, 1, :, :], mine[:, :, :], top[:, :, :], ALU.subtract).then_inc(gaps_ready, 1)
            dve.wait_ge(exps_ready, 1)

            def by_head(v):
                return v.rearrange("p t (h k) -> p t h k", h=HEADS)

            def wide(v):
                return v.unsqueeze(3).to_broadcast([P, T, HEADS, NE + 1])

            st.mark(dve.tensor_tensor(by_head(total[:, :, :]), by_head(edge[:, :, 0:Q]), wide(e2[:, 0, :, :]), ALU.mult))
            st.mark(dve.tensor_tensor(by_head(part[:, :, :]), by_head(rows[:, :, 0:Q]), wide(e2[:, 1, :, :]), ALU.mult))
            st.link(dve.tensor_tensor(e2[:, 2, :, :], e2[:, 2, :, :], per_channel(times[:, :], HEADS), ALU.mult))
            st.mark(dve.tensor_tensor(by_head(part3[:, :, :]), by_head(last_row[:, 0:Q].unsqueeze(1).to_broadcast([P, T, Q])),
                                      wide(e2[:, 2, :, :]), ALU.mult))
            st.link(dve.tensor_tensor(total[:, :, :], total[:, :, :], part[:, :, :], ALU.add))
            st.link(dve.tensor_tensor(total[:, :, :], total[:, :, :], part3[:, :, :], ALU.add))
            st.link(dve.tensor_scalar(inverse[:, :, :], by_head(total[:, :, :])[:, :, :, 0], 1e-16, None, ALU.add))
            st.link(dve.reciprocal(inverse[:, :, :], inverse[:, :, :]))
            st.link(dve.tensor_tensor(by_head(agg[:, :, :]), by_head(total[:, :, :])[:, :, :, 1:NE + 1],
                                      inverse[:, :, :].unsqueeze(3).to_broadcast([P, T, HEADS, NE]), ALU.mult))
            dve.wait_ge(vec_in, 48)

            def vector(n):
                return vec[:, n, :].unsqueeze(1).to_broadcast([P, T, F])

            st.link(dve.tensor_tensor(agg[:, :, :], agg[:, :, :], vector(0), ALU.add))
            norm.vector(dve, st, agg[:, :, :], agg[:, :, :], 0, normed)
            st.link(dve.tensor_tensor(agg[:, :, :], agg[:, :, :], vector(1), ALU.mult))
            st.link(dve.tensor_tensor(agg[:, :, :], agg[:, :, :], vector(2), ALU.add))
            st.link(dve.tensor_reduce(scores[:, :, :], agg[:, :, :].rearrange("p t (h k) -> p t k h", h=HEADS), X, ALU.add))
            st.link(dve.tensor_scalar(scores[:, :, :], scores[:, :, :], 1.0 / HEADS, None, ALU.mult))
            masks, tops = top_two(dve, st, a, "best", scores[:, :, :], T, NE)
            two_weights(dve, st, a, "best", gate[:, :, :], tops, masks, gap2, gap2_exp, gap2_ready, gap2_exp_ready)
            for b in range(B):
                tiles = slice(b * TB, (b + 1) * TB)
                st.link(dve.tensor_tensor(weighted[:, :, :].rearrange("p t (e c) -> p t e c", e=NE),
                                          eo[:, tiles, :].rearrange("p t (e c) -> p t e c", e=NE),
                                          gate[:, tiles, :].unsqueeze(3).to_broadcast([P, TB, NE, C]), ALU.mult))
                st.link(dve.tensor_reduce(summed[:, :, :], weighted[:, :, :].rearrange("p t (e c) -> p t c e", e=NE),
                                          X, ALU.add))
                dve.tensor_tensor(x_sb[:, tiles, :], x_sb[:, tiles, :], summed[:, :, :], ALU.add).then_inc(result, 1)
                dve.wait_ge(result, b + 1)

        @block.scalar
        def _(act):
            act.wait_ge(gaps_ready, 1)
            act.wait_ge(steps, marks["gaps"])
            act.activation(e2[:, :, :, :], gap[:, :, :, :], ACT.Exp).then_inc(exps_ready, 1)
            norm.scalar(act, 0)
            act.wait_ge(gap2_ready, 1)
            act.activation(gap2_exp[:, :], gap2[:, :], ACT.Exp).then_inc(gap2_exp_ready, 1)

        @block.gpsimd
        def _(pool):
            pool.wait_ge(steps, marks["at"])
            for t in range(T):
                gather(pool, edge[:, t, :], edge_rows_dram, at[:, t:t + 1], edge_in, bound=E - 1)

        @block.sync
        def _(sp):
            sp.dma_start(last_row[:, :], table[N - 1, :].partition_broadcast(P)).then_inc(last_in, 16)
            for n, v in enumerate((b_gat, ln_gamma, ln_beta)):
                sp.dma_start(vec[:, n, :], v.partition_broadcast(P)).then_inc(vec_in, 16)
            for b in range(B):
                sp.wait_ge(result, b + 1)
                sp.dma_start(out_dram[b, :, :, :].rearrange("(t r) w c -> (r w) t c", t=TB), x_sb[:, b * TB:(b + 1) * TB, :])\
                    .then_inc(stored, 16)
            sp.wait_ge(stored, 16 * B)


def build(nc, x, gamma, gate_w, gate_b, w1, w2, w3, kernel_w, W_gat, att_src, att_dst, b_gat, ln_gamma, ln_beta,
          W1, b1, W2, b2, edge_index, out):
    keys_dram = nc.dram_tensor("keys_dram", (E,), F32).ap()
    pivots_dram = nc.dram_tensor("pivots_dram", (E // BLK,), F32).ap()
    ends_dram = nc.dram_tensor("ends_dram", (N + 1,), F32).ap()
    last_src_dram = nc.dram_tensor("last_src_dram", (N + 1,), F32).ap()
    table = nc.dram_tensor("table", (N, ROW), F32).ap()
    a_dst_dram = nc.dram_tensor("a_dst_dram", (N, HEADS), F32).ap()
    edge_ad_dram = nc.dram_tensor("edge_ad_dram", (E, HEADS), F32).ap()
    edge_rows_dram = nc.dram_tensor("edge_rows_dram", (E, ROW), F32).ap()
    with ExitStack() as ctx:
        a = Arena(nc, ctx, "all")
        ident = a.sb("ident", [P, P])
        p_sign = a.sb("p_sign", [P, 2])
        x_sb = a.sb("x_sb", [P, T, C])
        blocks_i = a.sb("blocks_i", [P, 1], I32)
        chunk_f = a.sb("chunk_f", [P, 1])
        first_dst = a.sb("first_dst", [P, 1])
        last_dst = a.sb("last_dst", [P, 1])
        state = a.sb("state", [P, ROW])
        ends_f = a.sb("ends_f", [P, T])
        starts_f = a.sb("starts_f", [P, T])
        kept = a.sb("kept", [P, 1])
        last_ends, last_starts = a.sb("last_ends", [P, T]), a.sb("last_starts", [P, T])
        ad_sb = a.sb("ad_sb", [P, T, HEADS])
        rows = a.sb("rows", [P, T, ROW])
        constants(nc, ident, p_sign)
        sort_edges(nc, edge_index, ident, p_sign, keys_dram, pivots_dram,
                   [v.rearrange("n k -> (n k)") for v in (edge_ad_dram, edge_rows_dram)])
        with ExitStack() as middle:
            m = Arena(nc, middle, "middle")
            stacks = [m.sb(f"stack{n}", [P, N], BF16) for n in range(2)]
            weightsT = m.sb("weightsT", [48, N], BF16)
            attention(nc, x, gamma, x_sb, stacks, ident, keys_dram, pivots_dram, ends_dram, kept, blocks_i,
                      ends_f, starts_f)
            gates(nc, gate_w, gate_b, stacks, weightsT, ident)
            experts(nc, w1, w2, w3, x_sb, stacks, weightsT, ident)
        eo = a.sb("eo", [P, T, NE * C])
        with ExitStack() as middle:
            m = Arena(nc, middle, "features")
            h_sb = m.sb("h_sb", [P, T, HEADS * NE])
            as_sb = m.sb("as_sb", [P, T, HEADS])
            convolve(nc, kernel_w, W_gat, att_src, att_dst, W1, b1, W2, b2, x_sb, eo, h_sb, as_sb, ad_sb,
                     ident, keys_dram, pivots_dram, last_src_dram, kept, last_ends, last_starts)
            write_table(nc, h_sb, as_sb, ad_sb, rows, table, a_dst_dram)
        spread(nc, keys_dram, ends_f, starts_f, ad_sb, a_dst_dram, edge_ad_dram, blocks_i, chunk_f, first_dst)
        edge_loop(nc, keys_dram, table, edge_ad_dram, edge_rows_dram, blocks_i, chunk_f, last_dst, state)
        join_chunks(nc, ends_dram, edge_rows_dram, ident, chunk_f, blocks_i, first_dst, last_dst, state)
        route(nc, b_gat, ln_gamma, ln_beta, edge_rows_dram, table, ends_f, starts_f, last_ends, last_starts, rows, ad_sb,
              x_sb, eo, out)


_INS = ["x", "L0_conv_gamma", "L0_ffn_gate_w", "L0_ffn_gate_b", "L0_ffn_w1", "L0_ffn_w2", "L0_ffn_w3",
        "L1_conv_kernel", "L1_ffn_W_gat", "L1_ffn_att_src", "L1_ffn_att_dst", "L1_ffn_b_gat", "L1_ffn_ln_gamma",
        "L1_ffn_ln_beta", "L1_ffn_W1", "L1_ffn_b1", "L1_ffn_W2", "L1_ffn_b2", "L1_ffn_edge_index"]
_OUTS = [((B, 32, 32, C), "float32")]


def kernel(**inputs):
    import numpy as _np
    import concourse.bacc as _bacc
    from concourse import mybir as _mybir
    from concourse.bass_utils import run_bass_kernel_spmd as _run
    nc = _bacc.Bacc("TRN2", target_bir_lowering=False, num_devices=1)
    arrays, args = {}, []
    for name in _INS:
        a = _np.ascontiguousarray(inputs[name])
        arrays[f"in_{name}_dram"] = a
        args.append(nc.dram_tensor(f"in_{name}_dram", a.shape, _mybir.dt.from_np(a.dtype), kind="ExternalInput").ap())
    for i, (shape, dtype) in enumerate(_OUTS):
        dt = _mybir.dt.from_np(_np.dtype(dtype))
        args.append(nc.dram_tensor(f"out_{i}_dram", shape, dt, kind="ExternalOutput").ap())
    build(nc, *args)
    r = _run(nc, [arrays], core_ids=[0])
    got = tuple(r.results[0][f"out_{i}_dram"] for i in range(len(_OUTS)))
    return got if len(got) > 1 else got[0]
```

```python
from contextlib import ExitStack

import concourse.bass as bass
from concourse import mybir

F32 = mybir.dt.float32
BF16 = mybir.dt.bfloat16
I32 = mybir.dt.int32
U32 = mybir.dt.uint32
ALU = mybir.AluOpType
ACT = mybir.ActivationFunctionType
X = mybir.AxisListType.X

P = 128
B, HW_, C = 8, 1024, 64
N = B * HW_
T = N // P
E = 262144
EC = E // P
SRC_BITS = 13
KEY_ONE = 1 << 28
FIELDS = 1 << 15
BLK = 64
ROW = 24
HEADS, NE = 4, 4
Q = HEADS * (NE + 1)
FAR = -3.0e38
NONE = -1.0e30


class Steps:

    def __init__(self, engine, sem):
        self.engine, self.sem, self.n = engine, sem, 0

    def mark(self, ins):
        ins.then_inc(self.sem, 1)
        self.n += 1
        return self.n

    def link(self, ins):
        self.mark(ins)
        self.engine.wait_ge(self.sem, self.n)


class Arena:

    def __init__(self, nc, ctx, phase):
        self.nc, self.ctx, self.phase = nc, ctx, phase

    def sb(self, name, shape, dt=F32):
        return self.ctx.enter_context(self.nc.sbuf_tensor(f"{self.phase}_{name}", shape, dt))

    def ps(self, name, shape):
        return self.ctx.enter_context(self.nc.psum_tensor(f"{self.phase}_{name}", shape, F32))

    def sem(self, name):
        return self.nc.alloc_semaphore(f"{self.phase}_{name}")


def wait_apart(engine, sem, value, spare):
    register, met, least = spare
    engine.reg_mov(register, value)
    engine.wait_ge(met, least)
    engine.wait_ge(sem, register)


def constants(nc, edge_index, ident, p_sign, keys, zeros, x, x_sb, x_in):
    with ExitStack() as ctx:
        a = Arena(nc, ctx, "constants")
        part = a.sb("part", [P, 1], I32)
        bit = a.sb("bit", [P, 1])
        src_i = a.sb("src_i", [P, EC], I32)
        loaded = a.sem("edges_loaded")
        made = a.sem("constants_made")
        signs = a.sem("signs_made")
        steps = a.sem("key_steps")
        dst_i, last_src, dropped = (keys[n][:, :].bitcast(I32) for n in (2, 0, 1))
        block = ctx.enter_context(nc.Block())

        @block.gpsimd
        def _(pool):
            st = Steps(pool, made)
            st.link(pool.memset(ident[:, :], 0.0))
            st.link(pool.affine_select(out=ident[:, :], in_=ident[:, :], compare_op=ALU.not_equal, fill=1.0,
                                       base=0, pattern=[[-1, P]], channel_multiplier=1))
            st.link(pool.iota(part[:, :], pattern=[[0, 1]], base=0, channel_multiplier=1))
            st.link(pool.memset(zeros[:, :], 0.0))

        @block.vector
        def _(dve):
            dve.wait_ge(made, 3)
            st = Steps(dve, signs)
            st.link(dve.tensor_scalar(part[:, :], part[:, :], 1, None, ALU.bitwise_and))
            st.link(dve.tensor_copy(bit[:, :], part[:, :]))
            st.mark(dve.tensor_scalar(p_sign[:, 0:1], bit[:, :], -2.0, 1.0, ALU.mult, ALU.add))
            st.link(dve.tensor_scalar(p_sign[:, 1:2], bit[:, :], 2.0, -1.0, ALU.mult, ALU.add))
            st = Steps(dve, steps)
            dve.wait_ge(loaded, 32)
            st.mark(dve.tensor_scalar(src_i[:, :], src_i[:, :], float(N - 1), None, ALU.min))
            st.link(dve.tensor_scalar(dst_i, dst_i, float(N), None, ALU.min))
            st.mark(dve.tensor_scalar(last_src, src_i[:, :], float(N - 1), float(N), ALU.is_ge, ALU.mult))
            st.link(dve.tensor_scalar(dropped, dst_i, float(N), float(N), ALU.is_ge, ALU.mult))
            st.link(dve.tensor_tensor(dst_i, dst_i, last_src, ALU.add))
            st.link(dve.tensor_tensor(dst_i, dst_i, dropped, ALU.add))
            st.link(dve.scalar_tensor_tensor(src_i[:, :], dst_i, SRC_BITS, src_i[:, :],
                                             ALU.logical_shift_left, ALU.bitwise_or))
            st.link(dve.tensor_scalar(keys[0][:, :].bitcast(I32), src_i[:, :], KEY_ONE, None, ALU.bitwise_or))
            odd = keys[0][:, 1::2]
            st.link(dve.tensor_scalar(odd, odd, -1.0, None, ALU.mult))

        @block.sync
        def _(sp):
            sp.dma_start(src_i[:, :], edge_index[0, :].rearrange("(p c) -> p c", p=P)).then_inc(loaded, 16)
            sp.dma_start(dst_i, edge_index[1, :].rearrange("(p c) -> p c", p=P)).then_inc(loaded, 16)

        @block.scalar
        def _(act):
            with nc.allow_non_contiguous_dma(reason="256 B rows"):
                act.dma_start(x_sb[:, :, :], x.rearrange("b (t r) w c -> (r w) (b t) c", t=T // B)).then_inc(x_in, 16)


class Sort:

    ROUND = 4 * P
    ROUNDS = EC // ROUND
    STAGES = range(12, 19)

    def __init__(self, a, keys, p_sign):
        self.keys, self.p_sign, self.cur = keys, p_sign, 0
        self.steps = a.sem("sort_steps")
        self.wanted = a.sem("turn_wanted")
        self.turned = a.sem("round_turned")
        self.copied = a.sem("round_copied")
        self.turns = 0
        self.stage, self.exchanged = 1, 0

    def start(self, dve):
        self.st = Steps(dve, self.steps)

    def halves(self, buf, j):
        v = self.keys[buf][:, :].rearrange("p (b h d) -> p b h d", h=2, d=1 << j)
        return v[:, :, 0, :], v[:, :, 1, :]

    def wait_written(self, dve):
        if self.st.n:
            dve.wait_ge(self.steps, self.st.n)

    def exchange(self, dve, half, j, to):
        if half == 0:
            self.wait_written(dve)
        source, target = self.halves(self.cur, j), self.halves(to, j)
        self.st.mark(dve.tensor_tensor(target[half], source[0], source[1], (ALU.min, ALU.max)[half]))
        if half == 1:
            self.cur = to

    def exchange_first(self, dve, half, j, to, last=False):
        st = self.st
        if half == 0:
            self.wait_written(dve)
        if last:
            (lo, hi), target = self.halves(self.cur, j), self.halves(to, j)
            st.mark(dve.scalar_tensor_tensor(target[half], hi, -1.0, lo, ALU.mult, (ALU.min, ALU.max)[half]))
        else:
            v, w = (self.keys[n][:, :].rearrange("p (b r h d) -> p b r h d", r=2, h=2, d=1 << j)
                    for n in (self.cur, to))
            lo, hi = v[:, :, half, 0, :], v[:, :, half, 1, :]
            flip, keep = (hi, lo) if half == 0 else (lo, hi)
            st.mark(dve.scalar_tensor_tensor(w[:, :, half, 0, :], flip, -1.0, keep, ALU.mult, ALU.min))
            st.mark(dve.scalar_tensor_tensor(w[:, :, half, 1, :], flip, -1.0, keep, ALU.mult, ALU.max))
        if half == 1:
            self.cur = to

    def early(self, dve, count=1):
        for _ in range(count):
            if self.stage < self.STAGES[0]:
                self.within(dve, self.stage, self.exchanged)
                self.exchanged += 1
                if self.exchanged == self.stage:
                    self.stage, self.exchanged = self.stage + 1, 0

    def within(self, dve, k, m):
        if m == 0 and k == 11:
            self.wait_written(dve)
            lo, hi = self.halves(self.cur, 10)
            self.st.mark(dve.tensor_scalar(lo, lo, self.p_sign[:, 0:1], None, ALU.mult))
            self.st.mark(dve.tensor_scalar(hi, hi, self.p_sign[:, 1:2], None, ALU.mult))
        to = 1 - self.cur
        for half in range(2):
            if m == 0 and k < 11:
                self.exchange_first(dve, half, k - 1, to)
            else:
                self.exchange(dve, half, k - 1 - m, to)

    def want_turn(self, dve):
        assert self.cur == 0
        self.turns += 1
        self.wait_written(dve)
        dve.sem_inc(self.wanted, 1)

    def wait_turned(self, dve):
        dve.wait_ge(self.copied, 1 + self.ROUNDS * self.turns)
        self.cur = 1

    def across(self, dve, k, h):
        n, m, half = k - 11, h // 2, h % 2
        to = 1 - self.cur if n % 2 or m < n - 2 else (2 if m == n - 2 else 0)
        if m == 0:
            self.exchange_first(dve, half, k - 12, to, last=k == 18)
        else:
            self.exchange(dve, half, n - 1 - m, to)

    def below(self, dve, h):
        self.exchange(dve, h % 2, 10 - h // 2, 1 - self.cur)

    def turn_round(self, pe, bank, ident, stage, back, r, spare):
        if r == 0:
            wait_apart(pe, self.wanted, stage * 2 + back + 1, spare)
        before = (stage * 2 + back) * self.ROUNDS + r
        wait_apart(pe, self.copied, before + 1, spare)
        for t in range(4):
            at = r * self.ROUND + t * P
            ins = pe.transpose(bank[:, t * P:(t + 1) * P], self.keys[0][:, at:at + P], ident[:, :])
        ins.then_inc(self.turned, 1)

    def copy_round(self, act, bank, stage, back, r):
        act.wait_ge(self.turned, (stage * 2 + back) * self.ROUNDS + r + 1)
        act.activation(self.keys[1][:, r * self.ROUND:(r + 1) * self.ROUND], bank, ACT.Copy).then_inc(self.copied, 1)
def gather(pool, to, rows, index, done, bound=None):
    where = bass.IndirectOffsetOnAxis(ap=index, axis=0)
    if bound is None:
        pool.indirect_dma_start(to, None, rows, where).then_inc(done, 16)
    else:
        pool.indirect_dma_start(to, None, rows, where, bounds_check=bound, oob_is_err=False).then_inc(done, 16)


class Search:

    L = 64

    def __init__(self, nc, a, name, base, before, keys_dram, pivots_dram, ends_dram, ends_f, starts_f,
                 less, found=None):
        L = self.L
        self.nc, self.base, self.before, self.ends_dram = nc, base, before, ends_dram
        self.tables = (pivots_dram, keys_dram)
        self.ends_f, self.starts_f = ends_f, starts_f
        self.node = a.sb(name + "_node", [P, T], I32)
        self.bound = a.sb(name + "_bound", [P, T], I32)
        self.tops = a.sb(name + "_tops", [P, L])
        self.found = a.sb(name + "_found", [P, T, L]) if found is None else found
        self.less = less
        self.counts = [a.sb(f"{name}_count{n}", [P, T]) for n in range(3)]
        self.at = a.sb(name + "_at", [P, T])
        self.index = [a.sb(f"{name}_index{n}", [P, T], U32) for n in range(2)]
        self.made = a.sem(name + "_nodes_made")
        self.tops_in = a.sem(name + "_tops_in")
        self.steps = a.sem(name + "_steps")
        self.level = a.sem(name + "_index_ready")
        self.rows_in = [a.sem(f"{name}_rows_in{n}") for n in range(2)]
        self.ends_ready = a.sem(name + "_ends_ready")
        self.stored = a.sem(name + "_ends_stored")
        self.reloaded = a.sem(name + "_ends_reloaded")

    def load_tops(self, sp):
        with self.nc.allow_non_contiguous_dma(reason="a value per row"):
            tops = self.tables[0].rearrange("(i c) -> c i", c=self.L)[self.L - 1, :]
            sp.dma_start(self.tops[:, :], tops.partition_broadcast(P)).then_inc(self.tops_in, 16)

    def number(self, pool):
        pool.iota(self.node[:, :], pattern=[[P, T]], base=self.base + 1, channel_multiplier=1).then_inc(self.made, 1)

    def gathers(self, pool, n, first=0, last=T):
        pool.wait_ge(self.level, n + 1)
        for t in range(first, last):
            gather(pool, self.found[:, t, :], self.tables[n].rearrange("(r c) -> r c", c=self.L),
                   self.index[n][:, t:t + 1], self.rows_in[n])

    def count(self, dve, n):
        L, less, counts, at = self.L, self.less, self.counts, self.at
        if n == 0:
            self.st = Steps(dve, self.steps)
        st = self.st
        if n == 0:
            dve.wait_ge(self.made, 1)
            st.link(dve.tensor_scalar(self.bound[:, :], self.node[:, :], SRC_BITS, KEY_ONE, ALU.logical_shift_left,
                                      ALU.bitwise_or))
            dve.wait_ge(self.tops_in, 16)
            values = self.tops[:, :].unsqueeze(1).to_broadcast([P, T, L])
        else:
            dve.wait_ge(self.rows_in[n - 1], 16 * T)
            values = self.found[:, :, :]
        st.link(dve.tensor_tensor(less[:, :, :], values, per_channel(self.bound[:, :].bitcast(F32), L), ALU.is_lt))
        st.link(dve.tensor_reduce(counts[n][:, :], less[:, :, :], X, ALU.add))
        if n == 0:
            st.link(dve.tensor_scalar(at[:, :], counts[0][:, :], L - 1.0, None, ALU.min))
        elif n == 1:
            st.link(dve.tensor_scalar(counts[1][:, :], counts[1][:, :], L - 1.0, None, ALU.min))
            st.link(dve.scalar_tensor_tensor(at[:, :], at[:, :], float(L), counts[1][:, :], ALU.mult, ALU.add))
        if n < 2:
            dve.tensor_copy(self.index[n][:, :], at[:, :]).then_inc(self.level, 1)
        else:
            dve.scalar_tensor_tensor(self.ends_f[:, :], at[:, :], float(L), counts[2][:, :], ALU.mult, ALU.add)\
                .then_inc(self.ends_ready, 1)

    def shift(self, sp):
        ends_dram = self.ends_dram
        with self.nc.allow_non_contiguous_dma(reason="a value per node"):
            sp.wait_ge(self.ends_ready, 1)
            sp.dma_start(ends_dram[1:N + 1].rearrange("(t p) -> p t", p=P), self.ends_f[:, :]).then_inc(self.stored, 16)
            sp.dma_start(ends_dram[0:1].rearrange("(a b) -> a b", a=1), self.before).then_inc(self.stored, 16)
            sp.wait_ge(self.stored, 32)
            sp.dma_start(self.starts_f[:, :], ends_dram[0:N].rearrange("(t p) -> p t", p=P)).then_inc(self.reloaded, 16)
            sp.wait_ge(self.reloaded, 16)




def per_channel(v, n):
    return v.unsqueeze(2).to_broadcast([v.shape[0], v.shape[1], n])


class Norm:

    def __init__(self, a, name, groups, width, eps):
        self.groups, self.width, self.eps = groups, width, eps
        self.squares = a.sb(name + "_squares", [P, groups, width])
        self.mean = a.sb(name + "_mean", [P, groups])
        self.var = a.sb(name + "_var", [P, groups])
        self.root = a.sb(name + "_root", [P, groups])
        self.rstd = a.sb(name + "_rstd", [P, groups])
        self.var_ready = a.sem(name + "_var_ready")
        self.root_ready = a.sem(name + "_root_ready")

    def vector(self, dve, st, y, x, nth, y_ready, meanwhile=None):
        w = self.width
        st.link(dve.tensor_reduce(self.mean[:, :], x, X, ALU.add))
        st.link(dve.tensor_scalar(self.mean[:, :], self.mean[:, :], -1.0 / w, None, ALU.mult))
        st.link(dve.tensor_tensor(y, x, per_channel(self.mean[:, :], w), ALU.add))
        st.link(dve.tensor_tensor(self.squares[:, :, :], y, y, ALU.mult))
        st.link(dve.tensor_reduce(self.var[:, :], self.squares[:, :, :], X, ALU.add))
        dve.tensor_scalar(self.var[:, :], self.var[:, :], 1.0 / w, self.eps, ALU.mult, ALU.add)\
            .then_inc(self.var_ready, 1)
        if meanwhile is not None:
            meanwhile()
        dve.wait_ge(self.root_ready, nth + 1)
        st.link(dve.reciprocal(self.rstd[:, :], self.root[:, :]))
        dve.tensor_tensor(y, y, per_channel(self.rstd[:, :], w), ALU.mult).then_inc(y_ready, 1)
        dve.wait_ge(y_ready, nth + 1)

    def scalar(self, act, nth):
        act.wait_ge(self.var_ready, nth + 1)
        act.activation(self.root[:, :], self.var[:, :], ACT.Sqrt).then_inc(self.root_ready, 1)


class LoopSteps:

    def __init__(self, engine, sem, i, per):
        self.engine, self.sem, self.i, self.per, self.n = engine, sem, i, per, 0

    def mark(self, ins):
        ins.then_inc(self.sem, 1)
        self.n += 1

    def link(self, ins):
        self.mark(ins)
        self.engine.wait_ge(self.sem, self.i * self.per + self.n)

    def link_apart(self, ins, spare):
        self.mark(ins)
        wait_apart(self.engine, self.sem, self.i * self.per + self.n, spare)

    def end(self):
        assert self.n == self.per, (self.n, self.per)


def top_two(dve, st, a, name, values, G, K):
    order = a.sb(name + "_order", [P, K])
    pick = a.sb(name + "_pick", [P, G, K])
    rest = a.sb(name + "_rest", [P, G, K])
    best = a.sb(name + "_best", [P, G])
    masks = [a.sb(name + f"_mask{n}", [P, G, K]) for n in range(2)]
    tops = [a.sb(name + f"_top{n}", [P, G]) for n in range(2)]
    rank = order[:, :].unsqueeze(1).to_broadcast([P, G, K])
    for k in range(K):
        st.mark(dve.memset(order[:, k:k + 1], float(K - k)))
    for n in range(2):
        now = values if n == 0 else rest[:, :, :]
        st.link(dve.tensor_reduce(tops[n][:, :], now, X, ALU.max))
        st.link(dve.tensor_tensor(pick[:, :, :], now, per_channel(tops[n][:, :], K), ALU.is_equal))
        st.link(dve.tensor_tensor(pick[:, :, :], pick[:, :, :], rank, ALU.mult))
        st.link(dve.tensor_reduce(best[:, :], pick[:, :, :], X, ALU.max))
        st.link(dve.tensor_tensor(masks[n][:, :, :], rank, per_channel(best[:, :], K), ALU.is_equal))
        if n == 0:
            st.link(dve.scalar_tensor_tensor(rest[:, :, :], masks[0][:, :, :], FAR, values, ALU.mult, ALU.add))
    return masks, tops


def two_weights(dve, st, a, name, out, tops, masks, gap, gap_exp, gap_ready, exp_ready, nth=0):
    G, K = out.shape[1], out.shape[2]
    w = [a.sb(name + f"_w{n}", [P, G]) for n in range(2)]
    dve.tensor_tensor(gap[:, :], tops[1][:, :], tops[0][:, :], ALU.subtract).then_inc(gap_ready, 1)
    dve.wait_ge(exp_ready, nth + 1)
    st.link(dve.tensor_scalar(w[1][:, :], gap_exp[:, :], 1.0, None, ALU.add))
    st.link(dve.reciprocal(w[0][:, :], w[1][:, :]))
    st.link(dve.tensor_tensor(w[1][:, :], w[0][:, :], gap_exp[:, :], ALU.mult))
    st.mark(dve.tensor_tensor(masks[0][:, :, :], masks[0][:, :, :], per_channel(w[0][:, :], K), ALU.mult))
    st.link(dve.tensor_tensor(masks[1][:, :, :], masks[1][:, :, :], per_channel(w[1][:, :], K), ALU.mult))
    st.link(dve.tensor_tensor(out, masks[0][:, :, :], masks[1][:, :, :], ALU.add))


TB = T // B
EARLY_TILES = 20


def split_rows(dve, st, y, rough, parts, ready):
    for n in (1, 0):
        st.link(dve.tensor_copy(rough[:, :, :], y[:, :, :]))
        st.mark(dve.tensor_copy(parts[:, :, n, :], rough[:, :, :]))
        st.link(dve.tensor_tensor(y[:, :, :], y[:, :, :], rough[:, :, :], ALU.subtract))
    dve.tensor_copy(parts[:, :, 2, :], y[:, :, :]).then_inc(ready, 1)


def split_weights(dve, st, w, remainder, same, cross):
    st.link(dve.tensor_copy(same[0], w))
    st.link(dve.tensor_copy(cross[C:2 * C], w[C:2 * C]))
    st.link(dve.tensor_tensor(remainder, w, same[0], ALU.subtract))
    st.link(dve.tensor_copy(same[1], remainder))
    st.link(dve.tensor_tensor(cross[0:C], remainder[0:C], same[1][0:C], ALU.subtract))


class SplitWeights:

    def __init__(self, a, w1, w2):
        self.sources = (w1, w2)
        self.K, self.H = w1.shape[0], w1.shape[2]
        width = self.K * self.H
        self.w = [a.sb(f"w{n}", [P, width]) for n in range(2)]
        self.left = a.sb("left", [P, width])
        self.ws = [[a.sb(f"w{m}_part{n}", [P, width], BF16) for n in range(3)] for m in range(2)]
        self.loaded = a.sem("weights_in")
        self.parted = a.sem("weights_split")

    def load(self, act):
        for n, source in enumerate(self.sources):
            for half in range(2):
                act.dma_start(self.w[n][half * C:(half + 1) * C, :].rearrange("c (e h) -> c e h", e=self.K),
                              source.rearrange("e c h -> c e h")).then_inc(self.loaded, 16)

    def split(self, pool):
        pool.wait_ge(self.loaded, 64)
        st = Steps(pool, self.parted)
        for w, parts in zip(self.w, self.ws):
            split_weights(pool, st, w[:, :], self.left[:, :], [parts[0][:, :], parts[1][:, :]], parts[2][:, :])


def attention(nc, gamma, x_sb, x_in, stacks, ident, sort, weights):
    with ExitStack() as ctx:
        a = Arena(nc, ctx, "attention")
        y = a.sb("y", [P, TB, C])
        y1 = a.sb("y1", [P, TB, C])
        parts = a.sb("parts", [P, TB, 3, C])
        rough = a.sb("rough", [P, TB, C], BF16)
        aT = a.sb("aT", [C, TB * P])
        gam = a.sb("gam", [P, 1])
        top = a.sb("top", [C, 1])
        probs = a.sb("probs", [C, C])
        total = a.sb("total", [C, 1])
        part = a.sb("part", [C, 1])
        gram = a.ps("gram", [C, 512])
        mix = a.ps("mix", [P, TB * C])
        turned = a.ps("turned", [C, TB * P])
        turned1 = [a.ps(f"turned1_{n}", [P, TB * P]) for n in range(2)]
        n0 = Norm(a, "n0", TB, C, 1e-6)
        n1 = Norm(a, "n1", TB, C, 1e-5)
        gam_in = a.sem("gam_in")
        steps = a.sem("dve_steps")
        y_ready = a.sem("y_ready")
        y_turned = a.sem("y_turned")
        aT_ready = a.sem("aT_ready")
        gram_ready = a.sem("gram_ready")
        shift_ready = a.sem("shift_ready")
        exp_ready = a.sem("exp_ready")
        probs_ready = a.sem("probs_ready")
        mix_ready = a.sem("mix_ready")
        normed = a.sem("normed")
        y1_ready = a.sem("y1_ready")
        y1_turned = a.sem("y1_turned")
        y1_copied = a.sem("y1_copied")
        block = ctx.enter_context(nc.Block())

        @block.sync
        def _(sp):
            sp.dma_start(gam[:, :], gamma.to_broadcast([P, 1])).then_inc(gam_in, 16)
            weights.load(sp)

        @block.gpsimd
        def _(pool):
            weights.split(pool)

        @block.vector
        def _(dve):
            dve.wait_ge(gam_in, 16)
            dve.wait_ge(x_in, 16)
            sort.start(dve)
            for b in range(B):
                st = LoopSteps(dve, steps, b, 21)
                xb = x_sb[:, b * TB:(b + 1) * TB, :]
                n0.vector(dve, st, y[:, :, :], xb, b, y_ready, lambda: sort.early(dve))
                st.link(dve.tensor_tensor(xb, xb, y[:, :, :], ALU.add))
                sort.early(dve)
                dve.wait_ge(gram_ready, b + 1)
                dve.tensor_reduce(top[:, :], gram[:, 0:C], X, ALU.max, negate=True).then_inc(shift_ready, 1)
                sort.early(dve)
                dve.wait_ge(exp_ready, b + 1)
                st.link(dve.reciprocal(part[:, :], total[:, :]))
                dve.tensor_scalar(probs[:, :], probs[:, :], part[:, 0:1], None, ALU.mult).then_inc(probs_ready, 1)
                sort.early(dve)
                dve.wait_ge(mix_ready, b + 1)
                st.link(dve.scalar_tensor_tensor(xb, mix[:, :].rearrange("p (t c) -> p t c", t=TB), gam[:, 0:1],
                                                 xb, ALU.mult, ALU.add))
                n1.vector(dve, st, y1[:, :, :], xb, b, normed, lambda: sort.early(dve))
                split_rows(dve, st, y1, rough, parts, y1_ready)
                sort.early(dve, 2)
                dve.wait_ge(y1_turned, 2 * b + 2)
                st.end()

        @block.scalar
        def _(act):
            with act.Fori(0, B) as b:
                n0.scalar(act, b)
                act.wait_ge(y_turned, b + 1)
                act.activation(aT[:, :], turned[:, :], ACT.Copy).then_inc(aT_ready, 1)
                act.wait_ge(shift_ready, b + 1)
                act.activation(probs[:, :], gram[:, 0:C], ACT.Exp, bias=top[:, 0:1], accum_out=total[:, :])\
                    .then_inc(exp_ready, 1)
                n1.scalar(act, b)
                for n in range(2):
                    act.wait_ge(y1_turned, 2 * b + n + 1)
                    act.activation(stacks[n][:, bass.ds(b * TB * P, TB * P)], turned1[n][:, :], ACT.Copy)\
                        .then_inc(y1_copied, 1)

        @block.tensor
        def _(pe):
            spare = pe.alloc_register(f"pe_spare_{a.phase}"), gam_in, 16
            with pe.Fori(0, B) as b:
                pe.wait_ge(y_ready, b + 1)
                for t in range(TB):
                    ins = pe.matmul(gram[:, 0:C], y[:, t, :], y[:, t, :], start=(t == 0), stop=(t == TB - 1))
                ins.then_inc(gram_ready, 1)
                for t in range(TB):
                    ins = pe.transpose(turned[:, t * P:(t + 1) * P], y[:, t, :], ident[:, :])
                ins.then_inc(y_turned, 1)
                pe.wait_ge(aT_ready, b + 1)
                pe.wait_ge(probs_ready, b + 1)
                for t in range(TB):
                    ins = pe.matmul(mix[:, t * C:(t + 1) * C], aT[:, t * P:(t + 1) * P], probs[:, :],
                                    start=True, stop=True)
                ins.then_inc(mix_ready, 1)
                wait_apart(pe, y1_ready, b + 1, spare)
                for n in range(2):
                    for t in range(TB):
                        stack = parts[:, t, n:n + 2, :].rearrange("p n c -> p (n c)")
                        ins = pe.transpose(turned1[n][:, t * P:(t + 1) * P], stack, ident[:, :])
                    ins.then_inc(y1_turned, 1)


def gates(nc, gate_w, gate_b, stacks, weightsT, ident, sort):
    K = gate_w.shape[1]
    with ExitStack() as ctx:
        a = Arena(nc, ctx, "gates")
        gw = a.sb("gw", [P, K])
        left = a.sb("left", [P, K])
        gws = [a.sb(f"gw_part{n}", [P, K], BF16) for n in range(3)]
        gb = a.sb("gb", [P, K])
        logits = a.sb("logits", [P, T, K])
        gap, gap_exp = a.sb("gap", [P, T]), a.sb("gap_exp", [P, T])
        dispatch = a.sb("dispatch", [P, T, K])
        rough = a.sb("rough", [P, T, K], BF16)
        parts = a.sb("parts", [P, T, 3, K])
        logit_ps = a.ps("logit_ps", [P, 2, 512])
        turned = a.ps("turned", [3 * K, 4, 512])
        loaded = a.sem("gate_in")
        split = a.sem("gate_split")
        logits_ready = a.sem("logits_ready")
        steps = a.sem("gate_steps")
        gap_ready = a.sem("gap_ready")
        gap_exp_ready = a.sem("gap_exp_ready")
        parts_ready = a.sem("parts_ready")
        bank_turned = a.sem("bank_turned")
        bank_copied = a.sem("bank_copied")
        block = ctx.enter_context(nc.Block())

        @block.sync
        def _(sp):
            sp.dma_start(gw[0:C, :], gate_w).then_inc(loaded, 16)
            sp.dma_start(gw[C:P, :], gate_w).then_inc(loaded, 16)
            sp.dma_start(gb[:, :], gate_b.partition_broadcast(P)).then_inc(loaded, 16)

        @block.tensor
        def _(pe):
            pe.wait_ge(split, 5)
            for t in range(T):
                for n in range(3):
                    ins = pe.matmul(logit_ps[:, t // 32, (t % 32) * K:(t % 32 + 1) * K],
                                    stacks[n // 2][:, t * P:(t + 1) * P], gws[n][:, :], start=(n == 0), stop=(n == 2))
            ins.then_inc(logits_ready, 1)
            pe.wait_ge(parts_ready, 1)
            for q in range(T // 4):
                if q >= 4:
                    pe.wait_ge(bank_copied, q - 3)
                for t in range(4 * q, 4 * q + 4):
                    ins = pe.transpose(turned[:, q % 4, (t % 4) * P:(t % 4 + 1) * P],
                                       parts[:, t, :, :].rearrange("p n k -> p (n k)"), ident[:, :])
                ins.then_inc(bank_turned, 1)

        @block.vector
        def _(dve):
            dve.wait_ge(loaded, 48)
            st = Steps(dve, split)
            split_weights(dve, st, gw[:, :], left[:, :], [gws[0][:, :], gws[1][:, :]], gws[2][:, :])
            st = Steps(dve, steps)
            sort.early(dve, 4)
            dve.wait_ge(logits_ready, 1)
            bias = gb[:, :].unsqueeze(1).to_broadcast([P, 32, K])
            for n in range(2):
                st.mark(dve.tensor_tensor(logits[:, 32 * n:32 * n + 32, :],
                                          logit_ps[:, n, :].rearrange("p (t k) -> p t k", k=K), bias, ALU.add))
            dve.wait_ge(steps, st.n)
            masks, tops = top_two(dve, st, a, "gate", logits[:, :, :], T, K)
            two_weights(dve, st, a, "gate", dispatch[:, :, :], tops, masks, gap, gap_exp, gap_ready, gap_exp_ready)
            for n in range(2):
                st.link(dve.tensor_copy(rough[:, :, :], dispatch[:, :, :]))
                st.mark(dve.tensor_copy(parts[:, :, n, :], rough[:, :, :]))
                st.link(dve.tensor_tensor(dispatch[:, :, :], dispatch[:, :, :], rough[:, :, :], ALU.subtract))
            dve.tensor_copy(parts[:, :, 2, :], dispatch[:, :, :]).then_inc(parts_ready, 1)
            sort.early(dve, 6)

        @block.scalar
        def _(act):
            act.wait_ge(gap_ready, 1)
            act.activation(gap_exp[:, :], gap[:, :], ACT.Exp).then_inc(gap_exp_ready, 1)
            for q in range(T // 4):
                act.wait_ge(bank_turned, q + 1)
                act.activation(weightsT[:, q * 512:(q + 1) * 512], turned[:, q % 4, :], ACT.Copy).then_inc(bank_copied, 1)


def experts(nc, weights, w3, x_sb, stacks, weightsT, ident, sort, keys, pivots, zeros, cleared):
    K, H, ws = weights.K, weights.H, weights.ws
    G = 4 * P
    GROUPS = N // G
    LAG = 2
    TURN_AT = (5, 14)
    ACROSS, BELOW = (7, 6), (16, 21)
    assert GROUPS == 2 + 2 * len(sort.STAGES)
    with ExitStack() as ctx:
        a = Arena(nc, ctx, "experts")
        u3 = a.sb("u3", [H, K, C])
        pick = a.sb("pick", [3 * K, K])
        select = a.sb("select", [3 * K, K, H], BF16)
        add_halves = a.sb("add_halves", [P, C])
        gated = a.sb("gated", [H, 2, G])
        product = a.sb("product", [H, 2, G])
        hidden = a.sb("hidden", [H, 4, G])
        sums = a.sb("sums", [P, G])
        h1 = a.ps("h1", [H, 2, G])
        h2 = a.ps("h2", [H, 2, G])
        spread_w = a.ps("spread_w", [H, 2, G])
        acc = a.ps("acc", [P, G])
        back = a.ps("back", [P, G])
        loaded = a.sem("weights_in")
        keys_stored = a.sem("keys_stored")
        clearing = a.sem("clearing")
        made = a.sem("weights_split")
        h1_ready = a.sem("h1_ready")
        h2_ready = a.sem("h2_ready")
        h1_read = a.sem("h1_read")
        h2_read = a.sem("h2_read")
        hidden_ready = a.sem("hidden_ready")
        hidden_read = a.sem("hidden_read")
        acc_read = a.sem("acc_read")
        back_ready = a.sem("back_ready")
        added = a.sem("added")
        block = ctx.enter_context(nc.Block())

        @block.tensor
        def _(pe):
            pe.wait_ge(loaded, 16)
            pe.wait_ge(made, 5)
            spare = pe.alloc_register(f"pe_spare_{a.phase}"), loaded, 16

            def out_product(n, e):
                wait_apart(pe, hidden_ready, n + 3, spare)
                half = (e % 2) * C
                pe.matmul(acc[half:half + C, :], u3[:, e, :], hidden[:, e % 4, :], start=(e < 2), stop=(e >= K - 2))\
                    .then_inc(hidden_read, 1)

            def turn_back(g, turns):
                wait_apart(pe, sort.copied, turns * sort.ROUNDS + 1, spare)
                wait_apart(pe, acc_read, g + 2, spare)
                pe.wait_ge(added, g + 1)
                for q in range(4):
                    ins = pe.matmul(back[:, q * C:(q + 1) * C], sums[:, q * P:(q + 1) * P], add_halves[:, :],
                                    start=True, stop=True)
                ins.then_inc(back_ready, 1)

            def rounds(stage, e, half):
                for back_turn, at in enumerate(TURN_AT):
                    if stage is not None and at <= e < at + sort.ROUNDS // 2:
                        sort.turn_round(pe, back, ident, stage, back_turn, 2 * (e - at) + half, spare)

            def group(g, first, turns=0, stage=None):
                tokens = [s[:, bass.ds(g * G, G)] for s in stacks]
                for e in range(K):
                    n = g * K + e
                    wait_apart(pe, h1_read, n + 1, spare)
                    for part in range(3):
                        ins = pe.matmul(h1[:, e % 2, :], ws[0][part][:, e * H:(e + 1) * H], tokens[part // 2],
                                        start=(part == 0), stop=(part == 2))
                    ins.then_inc(h1_ready, 1)
                    rounds(stage, e, 0)
                    wait_apart(pe, hidden_ready, n + 1, spare)
                    pe.matmul(spread_w[:, e % 2, :], select[:, e, :], weightsT[:, bass.ds(g * G, G)],
                              start=True, stop=True)
                    if e == LAG:
                        wait_apart(pe, acc_read, g + 1, spare)
                    for part in range(3):
                        ins = pe.matmul(h2[:, e % 2, :], ws[1][part][:, e * H:(e + 1) * H], tokens[part // 2],
                                        start=(part == 0), stop=(part == 2))
                    ins.then_inc(h2_ready, 1)
                    rounds(stage, e, 1)
                    if e >= LAG or not first:
                        out_product(n - LAG, (e - LAG) % K)
                    if e == LAG + 1 and not first:
                        turn_back(g - 1, turns)

            group(0, True)
            group(1, False)
            with pe.Fori(0, len(sort.STAGES)) as s:
                group(2 * s + 2, False, 2 * s, s)
                group(2 * s + 3, False, 2 * s + 2)
            for e in range(K - LAG, K):
                out_product((GROUPS - 1) * K + e, e)
            turn_back(GROUPS - 1, 2 * len(sort.STAGES))

        @block.scalar
        def _(act):
            act.wait_ge(made, 5)

            def copy_sums(g):
                act.wait_ge(back_ready, g + 1)
                act.wait_ge(hidden_read, g * K + K + 4)
                act.activation(sums[:, :], acc[:, :], ACT.Copy).then_inc(acc_read, 1)

            def group(g, first, stage=None):
                for e in range(K):
                    n = g * K + e
                    act.wait_ge(h1_ready, n + 1)
                    act.wait_ge(h2_read, n + 1)
                    act.activation(gated[:, e % 2, :], h1[:, e % 2, :], ACT.Silu).then_inc(h1_read, 1)
                    for back_turn, at in enumerate(TURN_AT):
                        if stage is not None and at <= e < at + sort.ROUNDS // 2:
                            for r in range(2 * (e - at), 2 * (e - at) + 2):
                                sort.copy_round(act, back[:, :], stage, back_turn, r)
                    if e == LAG - 1 and not first:
                        copy_sums(g - 1)

            group(0, True)
            group(1, False)
            with act.Fori(0, len(sort.STAGES)) as s:
                group(2 * s + 2, False, s)
                group(2 * s + 3, False)
            copy_sums(GROUPS - 1)

        @block.vector
        def _(dve):
            for sem, free in ((h1_read, 2), (h2_read, 2), (hidden_ready, 2), (hidden_read, 4), (acc_read, 1),
                              (back_ready, 1), (added, 1), (sort.copied, 1)):
                dve.sem_inc(sem, free)
            st = Steps(dve, made)
            st.mark(dve.tensor_copy(add_halves[0:C, :], ident[0:C, 0:C]))
            st.mark(dve.tensor_copy(add_halves[C:P, :], ident[C:P, C:P]))
            st.link(dve.tensor_tensor(pick[:, :], ident[0:3 * K, 0:K], ident[0:3 * K, K:2 * K], ALU.add))
            st.link(dve.tensor_tensor(pick[:, :], pick[:, :], ident[0:3 * K, 2 * K:3 * K], ALU.add))
            st.mark(dve.tensor_copy(select[:, :, :], per_channel(pick[:, :], H)))
            dve.wait_ge(made, st.n)
            assert st.n == 5
            spare = dve.alloc_register(f"dve_spare_{a.phase}"), loaded, 16

            def add_back(g):
                wait_apart(dve, back_ready, g + 2, spare)
                tiles = x_sb[:, bass.ds(g * 4, 4), :]
                dve.tensor_tensor(tiles, tiles, back[:, 0:4 * C].rearrange("p (q c) -> p q c", q=4), ALU.add)\
                    .then_inc(added, 1)

            def multiply(g, e):
                n = g * K + e
                dve.wait_ge(h1_read, n + 3)
                dve.wait_ge(h2_ready, n + 1)
                dve.tensor_tensor(product[:, e % 2, :], gated[:, e % 2, :], h2[:, e % 2, :], ALU.mult)\
                    .then_inc(h2_read, 1)

            def weigh(g, e):
                n = g * K + e
                dve.wait_ge(h2_read, n + 3)
                dve.wait_ge(hidden_read, n + 1)
                dve.tensor_tensor(hidden[:, e % 4, :], product[:, e % 2, :], spread_w[:, e % 2, :], ALU.mult)\
                    .then_inc(hidden_ready, 1)
                if e == LAG + 1 and g > 0:
                    add_back(g - 1)

            assert sort.stage == sort.STAGES[0]
            for g in range(2):
                for e in range(K):
                    multiply(g, e)
                    weigh(g, e)

            def share(i, window, halves):
                first, steps = window
                ends = [min(max(n - first, 0), steps) * halves // steps for n in (i, i + 1)]
                return range(*ends)

            for s, k in enumerate(sort.STAGES):
                for i in range(2 * K):
                    multiply(2 * s + 2 + i // K, i % K)
                    if i == BELOW[0]:
                        sort.wait_turned(dve)
                    if s > 0:
                        for h in share(i + 2 * K, BELOW, 22):
                            sort.below(dve, h)
                    if i == ACROSS[0]:
                        sort.wait_turned(dve)
                    halves = [*share(i, ACROSS, 2 * (k - 11))]
                    for h in halves[:1]:
                        sort.across(dve, k, h)
                    for h in share(i, BELOW, 22):
                        sort.below(dve, h)
                    weigh(2 * s + 2 + i // K, i % K)
                    for h in halves[1:]:
                        sort.across(dve, k, h)
                    if i + 1 in TURN_AT:
                        dve.wait_ge(added, 2 * s + 3)
                        sort.want_turn(dve)
            for i in range(2 * K, sum(BELOW)):
                for h in share(i, BELOW, 22):
                    sort.below(dve, h)
            sort.wait_written(dve)
            dve.sem_inc(sort.wanted, 1)
            add_back(GROUPS - 1)

        @block.sync
        def _(sp):
            sp.dma_start(u3[:, :, :], w3.rearrange("e h c -> h e c")).then_inc(loaded, 16)
            width = zeros.shape[1]
            for flat in cleared:
                for piece in range(flat.shape[0] // (P * width)):
                    sp.dma_start(flat[piece * P * width:(piece + 1) * P * width].rearrange("(p c) -> p c", p=P), zeros[:, :])\
                        .then_inc(clearing, 16)
            sp.wait_ge(sort.wanted, 2 * len(sort.STAGES) + 1)
            sp.dma_start(keys.rearrange("(p c) -> p c", p=P), sort.keys[sort.cur][:, :]).then_inc(keys_stored, 16)
            sp.dma_start(pivots.rearrange("(p c) -> p c", p=P), sort.keys[sort.cur][:, BLK - 1::BLK],
                         allow_slow_non_contiguous=True).then_inc(keys_stored, 16)
            sp.wait_ge(keys_stored, 32)
            sp.wait_ge(clearing, 16 * sum(flat.shape[0] // (P * width) for flat in cleared))


class LastWeights:

    def __init__(self, a, W_gat, W1):
        self.W_gat, self.W1 = W_gat, W1
        self.K, self.H = W1.shape[0], W1.shape[2]
        F = HEADS * NE
        self.wg = a.sb("wg", [P, F])
        self.wgs = [a.sb(f"wg_part{n}", [P, F], BF16) for n in range(3)]
        self.u1 = a.sb("u1", [P, self.K * self.H])
        self.us = [a.sb(f"u1_part{n}", [P, self.K * self.H], BF16) for n in range(3)]
        self.left = a.sb("left", [P, self.K * self.H])
        self.loaded = a.sem("last_weights_in")
        self.parted = a.sem("last_weights_split")

    def load(self, sp):
        for half in range(2):
            sp.dma_start(self.wg[half * C:(half + 1) * C, :], self.W_gat).then_inc(self.loaded, 16)
            sp.dma_start(self.u1[half * C:(half + 1) * C, :].rearrange("c (e h) -> c e h", e=self.K),
                         self.W1.rearrange("e c h -> c e h")).then_inc(self.loaded, 16)

    def split(self, dve):
        dve.wait_ge(self.loaded, 64)
        st = Steps(dve, self.parted)
        for w, parts in ((self.wg, self.wgs), (self.u1, self.us)):
            split_weights(dve, st, w[:, :], self.left[:, 0:w.shape[1]], [parts[0][:, :], parts[1][:, :]], parts[2][:, :])


def convolve(nc, kernel_w, x_sb, stacks, ident, keys, pivots, ends_dram, kept, blocks_i, ends_f, starts_f,
             find_last, last_weights, room):
    S = 32
    PAD = S + 2
    with ExitStack() as ctx:
        a = Arena(nc, ctx, "convolve")
        zero = a.sb("zero", [1, 1])
        kept_up = a.sb("kept_up", [P, 1])
        kept_i = a.sb("kept_i", [P, 1], I32)
        zero_made = a.sem("zero_made")
        kept_in = a.sem("kept_in")
        kept_steps = a.sem("kept_steps")
        find = Search(nc, a, "edges", 0, zero[:, :], keys, pivots, ends_dram, ends_f, starts_f,
                      find_last.less, room)
        y = a.sb("y", [P, TB, C])
        parts = a.sb("parts", [P, TB, 3, C])
        y4 = a.sb("y4", [P, TB, C])
        parts4 = a.sb("parts4", [P, TB, 3, C])
        rough = a.sb("rough", [P, TB, C], BF16)
        padded = a.sb("padded", [P, 2, 3, PAD, S], BF16)
        cw = a.sb("cw", [P, 9 * C])
        signs = a.sb("signs", [P, 2, 9 * C], BF16)
        n2 = Norm(a, "n2", TB, C, 1e-6)
        n3 = Norm(a, "n3", TB, C, 1e-5)
        turned = [a.ps(f"turned{n}", [P, TB * P]) for n in range(2)]
        conv = a.ps("conv", [P, TB * C])
        loaded = a.sem("weights_in")
        signed = a.sem("signs_ready")
        steps2 = a.sem("n2_steps")
        steps3 = a.sem("n3_steps")
        normed2 = a.sem("normed2")
        normed3 = a.sem("normed3")
        y_ready = a.sem("y_ready")
        y_turned = a.sem("y_turned")
        padded_ready = a.sem("padded_ready")
        conv_ready = a.sem("conv_ready")
        y4_ready = a.sem("y4_ready")
        y4_turned = a.sem("y4_turned")
        y4_copied = a.sem("y4_copied")
        block = ctx.enter_context(nc.Block())

        @block.gpsimd
        def _(pool):
            find.number(pool)
            find_last.number(pool)
            find.gathers(pool, 0)
            find_last.gathers(pool, 0)
            find.gathers(pool, 1)
            find_last.gathers(pool, 1, 0, EARLY_TILES)

        @block.sync
        def _(sp):
            find.load_tops(sp)
            find_last.load_tops(sp)
            for half in range(2):
                sp.dma_start(cw[half * C:(half + 1) * C, :].rearrange("c (a d) -> c a d", d=C),
                             kernel_w.rearrange("a b c d -> c (a b) d")).then_inc(loaded, 16)
            last_weights.load(sp)
            sp.wait_ge(zero_made, 1)
            find.shift(sp)
            sp.dma_start(kept[:, :], ends_dram[N:N + 1].partition_broadcast(P)).then_inc(kept_in, 16)
            sp.wait_ge(kept_in, 16)

        @block.vector
        def _(dve):
            dve.sem_inc(y4_copied, 2)
            dve.sem_inc(y4_turned, 2)
            find.count(dve, 0)
            find_last.count(dve, 0)
            dve.wait_ge(loaded, 32)
            st = Steps(dve, signed)
            st.link(dve.tensor_scalar(cw[:, :], cw[:, :], 0.0, None, ALU.is_ge))
            st.mark(dve.tensor_scalar(signs[:, 0, :], cw[:, :], 2.0, -1.0, ALU.mult, ALU.add))
            st.mark(dve.tensor_scalar(signs[C:P, 1, :], cw[C:P, :], 2.0, -1.0, ALU.mult, ALU.add))
            st.mark(dve.memset(signs[0:C, 1, :], 0.0))
            st.link(dve.memset(padded[:, :, :, :, :], 0.0))
            spare = dve.alloc_register(f"dve_spare_{a.phase}"), signed, 5

            def before(b):
                st = LoopSteps(dve, steps2, b, 12)
                n2.vector(dve, st, y[:, :, :], x_sb[:, bass.ds(b * TB, TB), :], b, normed2)
                split_rows(dve, st, y, rough, parts, y_ready)
                st.end()

            def behind(b):
                st = LoopSteps(dve, steps3, b, 13)
                xb = x_sb[:, bass.ds(b * TB, TB), :]
                dve.wait_ge(conv_ready, b + 1)
                st.link_apart(dve.tensor_tensor(xb, xb, conv[:, :].rearrange("p (t c) -> p t c", t=TB), ALU.add), spare)
                n3.vector(dve, st, y4[:, :, :], xb, b, normed3)
                dve.wait_ge(y4_turned, 2 * b + 2)
                split_rows(dve, st, y4, rough, parts4, y4_ready)
                st.end()

            def image(b):
                dve.wait_ge(y_turned, 2 * b + 2)
                before(b + 1)
                dve.wait_ge(y_ready, b + 2)
                behind(b)

            dve.memset(zero[:, :], 0.0).then_inc(zero_made, 1)
            before(0)
            with dve.Fori(0, B // 2) as b:
                image(b)
            find.count(dve, 1)
            with dve.Fori(B // 2, B - 1) as b:
                image(b)
            dve.wait_ge(y_ready, B)
            behind(B - 1)
            find_last.count(dve, 1)
            last_weights.split(dve)
            find.count(dve, 2)
            dve.wait_ge(kept_in, 16)
            st = Steps(dve, kept_steps)
            st.link(dve.tensor_scalar(kept_up[:, :], kept[:, :], 1.0, float(P * BLK - 1), ALU.max, ALU.add))
            st.link(dve.tensor_copy(kept_i[:, :], kept_up[:, :]))
            st.link(dve.tensor_scalar(blocks_i[:, :], kept_i[:, :], 13, None, ALU.logical_shift_right))

        @block.scalar
        def _(act):
            act.wait_ge(signed, 5)

            def pad(b, first):
                if not first:
                    act.wait_ge(conv_ready, b)
                for n in range(2):
                    if n == 1 and not first:
                        n3.scalar(act, b - 1)
                    act.wait_ge(y_turned, 2 * b + n + 1)
                    image = turned[n][:, :].rearrange("c (r w) -> c r w", w=S)
                    for w in range(3):
                        left, right = max(1 - w, 0), min(S, S + 1 - w)
                        act.activation(padded[:, n, w, 1:S + 1, left:right], image[:, :, left + w - 1:right + w - 1],
                                       ACT.Copy).then_inc(padded_ready, 1)

            def stack(b):
                for n in range(2):
                    act.wait_ge(y4_turned, 2 * b + n + 3)
                    act.activation(stacks[n][:, bass.ds(b * TB * P, TB * P)], turned[n][:, :], ACT.Copy)\
                        .then_inc(y4_copied, 1)

            n2.scalar(act, 0)
            pad(0, True)
            with act.Fori(0, B - 1) as b:
                n2.scalar(act, b + 1)
                pad(b + 1, False)
                stack(b)
            n3.scalar(act, B - 1)
            stack(B - 1)

        @block.tensor
        def _(pe):
            pe.wait_ge(signed, 5)
            spare = pe.alloc_register(f"pe_spare_{a.phase}"), signed, 5

            def turn(source, ready, b, free, free_at, done):
                wait_apart(pe, ready, b + 1, spare)
                for n in range(2):
                    for t in range(TB):
                        if t == 0:
                            wait_apart(pe, free, free_at + n, spare)
                        stacked = source[:, t, n:n + 2, :].rearrange("p n c -> p (n c)")
                        ins = pe.transpose(turned[n][:, t * P:(t + 1) * P], stacked, ident[:, :])
                    ins.then_inc(done, 1)

            def convolution(b):
                wait_apart(pe, padded_ready, 6 * b + 6, spare)
                for t in range(TB):
                    for n in range(2):
                        for tap in range(9):
                            r, w = 4 * t + tap // 3, tap % 3
                            ins = pe.matmul(conv[:, t * C:(t + 1) * C], padded[:, n, w, r:r + 4, :],
                                            signs[:, n, tap * C:(tap + 1) * C],
                                            start=(n == 0 and tap == 0), stop=(n == 1 and tap == 8))
                ins.then_inc(conv_ready, 1)

            turn(parts, y_ready, 0, y4_copied, 1, y_turned)
            with pe.Fori(0, B - 1) as b:
                convolution(b)
                turn(parts, y_ready, b + 1, y4_copied, 2 * b + 1, y_turned)
                wait_apart(pe, padded_ready, 6 * b + 12, spare)
                turn(parts4, y4_ready, b, y4_copied, 2 * b + 1, y4_turned)
            convolution(B - 1)
            turn(parts4, y4_ready, B - 1, y4_copied, 2 * B - 1, y4_turned)


def publish(nc, last_weights, find_last, att_src, att_dst, b1, W2, b2, stacks, eo, ident, rows, ad_sb, table, a_dst_dram,
            keys_dram, ends_f, starts_f, edge_ad_dram, blocks_i, chunk_f, first_dst):
    K, H, wgs, us = last_weights.K, last_weights.H, last_weights.wgs, last_weights.us
    F = HEADS * NE
    G = 4 * P
    GROUPS = N // G
    LAG = 2
    with ExitStack() as ctx:
        a = Arena(nc, ctx, "publish")
        att = a.sb("att", [P, 2, F])
        ub1 = a.sb("ub1", [H, K])
        u2 = a.sb("u2", [H, K, C])
        ub2 = a.sb("ub2", [P, K * C])
        h_sb = a.sb("h_sb", [P, T, F])
        products = a.sb("products", [P, 2, T, F])
        as_sb = a.sb("as_sb", [P, T, HEADS])
        hidden = a.sb("hidden", [H, K, G])
        sums = a.sb("sums", [P, 2, G])
        empty = a.sb("empty", [P, T])
        to_f = a.sb("to_f", [P, T])
        to = a.sb("to", [P, T], U32)
        part = a.sb("part", [P, 1], I32)
        part_f = a.sb("part_f", [P, 1])
        blocks_f = a.sb("blocks_f", [P, 1])
        chunk_i = a.sb("chunk_i", [P, 1], U32)
        keys = a.sb("keys", [P, BLK], I32)
        dst = a.sb("dst", [P, 1], I32)
        known = a.sb("known", [P, 1])
        first_i = a.sb("first_i", [P, 1], U32)
        first_ad = a.sb("first_ad", [P, HEADS])
        cut_f = a.sb("cut_f", [P, 1])
        cut_i = a.sb("cut_i", [P, 1], U32)
        feats = a.ps("feats", [P, 2, 512])
        h1 = a.ps("h1", [H, 2, G])
        acc = a.ps("acc", [P, 2, G])
        back = a.ps("back", [P, 4, K * C])
        loaded = a.sem("weights_in")
        steps = a.sem("spread_steps")
        made = a.sem("made")
        keys_in = a.sem("keys_in")
        ad_in = a.sem("ad_in")
        written = a.sem("edge_ad_written")
        feats_ready = a.sem("feats_ready")
        node_steps = a.sem("node_steps")
        stored = a.sem("rows_stored")
        h1_ready = a.sem("h1_ready")
        h1_read = a.sem("h1_read")
        hidden_read = a.sem("hidden_read")
        acc_read = a.sem("acc_read")
        back_ready = a.sem("back_ready")
        added = a.sem("added")
        marks = {}
        block = ctx.enter_context(nc.Block())

        @block.vector
        def _(dve):
            for sem, free in ((h1_read, 2), (hidden_read, 4), (acc_read, 1), (back_ready, 1), (added, 1)):
                dve.sem_inc(sem, free)
            sp = Steps(dve, steps)
            sp.link(dve.tensor_tensor(empty[:, :], starts_f[:, :], ends_f[:, :], ALU.is_equal))
            sp.link(dve.scalar_tensor_tensor(to_f[:, :], empty[:, :], float(2 * E), starts_f[:, :], ALU.mult, ALU.add))
            sp.link(dve.tensor_copy(to[:, :], to_f[:, :]))
            marks["to"] = sp.n
            dve.wait_ge(made, 1)
            sp.mark(dve.tensor_copy(part_f[:, :], part[:, :]))
            sp.link(dve.tensor_copy(blocks_f[:, :], blocks_i[:, :]))
            sp.link(dve.tensor_tensor(chunk_f[:, :], part_f[:, :], blocks_f[:, :], ALU.mult))
            sp.link(dve.tensor_copy(chunk_i[:, :], chunk_f[:, :]))
            marks["chunk"] = sp.n
            nd = Steps(dve, node_steps)
            nd.link(dve.memset(rows[:, :, :], 1.0))
            dve.wait_ge(loaded, 80)
            dve.wait_ge(feats_ready, 1)
            for n in range(2):
                nd.mark(dve.tensor_copy(h_sb[:, n * 32:(n + 1) * 32, :], feats[:, n, :].rearrange("p (t k) -> p t k", k=F)))
            dve.wait_ge(node_steps, nd.n)
            for n in range(2):
                nd.link(dve.tensor_tensor(products[:, n, :, :], h_sb[:, :, :],
                                          att[:, n, :].unsqueeze(1).to_broadcast([P, T, F]), ALU.mult))
            for n, values in enumerate((as_sb, ad_sb)):
                nd.mark(dve.tensor_reduce(values[:, :, :], products[:, n, :, :].rearrange("p t (h k) -> p t h k", k=NE),
                                          X, ALU.add))
            nd.link(dve.tensor_copy(rows[:, :, 0:Q].rearrange("p t (h k) -> p t h k", k=NE + 1)[:, :, :, 1:NE + 1],
                                    h_sb[:, :, :].rearrange("p t (h k) -> p t h k", k=NE)))
            nd.link(dve.tensor_copy(rows[:, :, Q:ROW], as_sb[:, :, :]))
            marks["rows"] = nd.n
            dve.wait_ge(keys_in, 16)
            sp.link(dve.tensor_scalar(dst[:, :], keys[:, 0:1], SRC_BITS, FIELDS - 1, ALU.logical_shift_right,
                                      ALU.bitwise_and))
            sp.link(dve.tensor_copy(first_dst[:, :], dst[:, :]))
            sp.link(dve.tensor_scalar(known[:, :], first_dst[:, :], N - 1.0, None, ALU.min))
            sp.link(dve.tensor_copy(first_i[:, :], known[:, :]))
            sp.link(dve.tensor_scalar(cut_f[:, :], chunk_f[:, :], float(BLK), None, ALU.mult))
            sp.link(dve.tensor_copy(cut_i[:, :], cut_f[:, :]))
            marks["cut"] = sp.n
            spare = dve.alloc_register(f"dve_spare_{a.phase}"), loaded, 80

            def add_bias(g):
                wait_apart(dve, back_ready, g + 2, spare)
                dve.tensor_tensor(eo[:, bass.ds(g * 4, 4), :], back[:, :, :],
                                  ub2[:, :].unsqueeze(1).to_broadcast([P, 4, K * C]), ALU.add).then_inc(added, 1)

            with dve.Fori(0, GROUPS) as g:
                add_bias(g)
            find_last.count(dve, 2)

        @block.tensor
        def _(pe):
            for t in range(T):
                for n in range(3):
                    ins = pe.matmul(feats[:, t // 32, (t % 32) * F:(t % 32 + 1) * F],
                                    stacks[n // 2][:, t * P:(t + 1) * P], wgs[n][:, :], start=(n == 0), stop=(n == 2))
            ins.then_inc(feats_ready, 1)
            pe.wait_ge(loaded, 80)
            spare = pe.alloc_register(f"pe_spare_{a.phase}"), loaded, 80

            def out_product(n, e):
                wait_apart(pe, h1_read, n + 3, spare)
                half = (e % 2) * C
                pe.matmul(acc[half:half + C, e // 2, :], u2[:, e, :], hidden[:, e, :], start=True, stop=True)\
                    .then_inc(hidden_read, 1)

            def turn_back(g):
                wait_apart(pe, acc_read, g + 2, spare)
                pe.wait_ge(added, g + 1)
                for q in range(4):
                    for pair in range(2):
                        ins = pe.transpose(back[:, q, pair * P:(pair + 1) * P], sums[:, pair, q * P:(q + 1) * P],
                                           ident[:, :])
                ins.then_inc(back_ready, 1)

            def group(g, first):
                tokens = [s[:, bass.ds(g * G, G)] for s in stacks]
                for e in range(K):
                    n = g * K + e
                    wait_apart(pe, h1_read, n + 1, spare)
                    for m in range(3):
                        if m == 1 and e == LAG:
                            wait_apart(pe, acc_read, g + 1, spare)
                        ins = pe.matmul(h1[:, e % 2, :], us[m][:, e * H:(e + 1) * H], tokens[m // 2],
                                        start=(m == 0), stop=(m == 2))
                    ins.then_inc(h1_ready, 1)
                    if e >= LAG or not first:
                        out_product(n - LAG, (e - LAG) % K)
                    if e == K - 1 and not first:
                        turn_back(g - 1)

            group(0, True)
            with pe.Fori(1, GROUPS) as g:
                group(g, False)
            for e in range(K - LAG, K):
                out_product((GROUPS - 1) * K + e, e)
            turn_back(GROUPS - 1)

        @block.scalar
        def _(act):
            act.wait_ge(loaded, 80)

            def copy_sums(g):
                act.wait_ge(back_ready, g + 1)
                act.wait_ge(hidden_read, g * K + K + 4)
                act.activation(sums[:, :, :], acc[:, :, :], ACT.Copy).then_inc(acc_read, 1)

            def group(g, first):
                for e in range(K):
                    n = g * K + e
                    act.wait_ge(h1_ready, n + 1)
                    act.wait_ge(hidden_read, n + 1)
                    act.activation(hidden[:, e, :], h1[:, e % 2, :], ACT.Gelu, bias=ub1[:, e:e + 1]).then_inc(h1_read, 1)
                    if e == LAG - 1 and not first:
                        copy_sums(g - 1)

            group(0, True)
            with act.Fori(1, GROUPS) as g:
                group(g, False)
            copy_sums(GROUPS - 1)

        @block.gpsimd
        def _(pool):
            pool.iota(part[:, :], pattern=[[0, 1]], base=0, channel_multiplier=1).then_inc(made, 1)
            pool.wait_ge(steps, marks["chunk"])
            gather(pool, keys[:, :].bitcast(F32), keys_dram.rearrange("(r c) -> r c", c=BLK), chunk_i[:, :], keys_in)
            find_last.gathers(pool, 1, EARLY_TILES)
            pool.wait_ge(node_steps, marks["rows"])
            for t in range(T):
                pool.indirect_dma_start(edge_ad_dram, bass.IndirectOffsetOnAxis(ap=to[:, t:t + 1], axis=0),
                                        ad_sb[:, t, :], None, bounds_check=E - 1, oob_is_err=False)\
                    .then_inc(written, 16)
            pool.wait_ge(steps, marks["cut"])
            pool.wait_ge(stored, 32)
            gather(pool, first_ad[:, :], a_dst_dram, first_i[:, :], ad_in)
            pool.wait_ge(ad_in, 16)
            pool.wait_ge(written, 16 * T)
            pool.indirect_dma_start(edge_ad_dram, bass.IndirectOffsetOnAxis(ap=cut_i[:, :], axis=0),
                                    first_ad[:, :], None).then_inc(written, 16)
            pool.wait_ge(written, 16 * (T + 1))

        @block.sync
        def _(sp):
            for n, v in enumerate((att_src, att_dst)):
                sp.dma_start(att[:, n, :], v.rearrange("h k -> (h k)").partition_broadcast(P)).then_inc(loaded, 16)
            with nc.allow_non_contiguous_dma(reason="small bias"):
                sp.dma_start(ub1[:, :], b1.rearrange("e h -> h e")).then_inc(loaded, 16)
            sp.dma_start(u2[:, :, :], W2.rearrange("e h c -> h e c")).then_inc(loaded, 16)
            sp.dma_start(ub2[:, :], b2.rearrange("e c -> (e c)").partition_broadcast(P)).then_inc(loaded, 16)
            sp.wait_ge(node_steps, marks["rows"])
            sp.dma_start(table.rearrange("(t p) k -> p t k", p=P), rows[:, :, :]).then_inc(stored, 16)
            sp.dma_start(a_dst_dram.rearrange("(t p) k -> p t k", p=P), ad_sb[:, :, :]).then_inc(stored, 16)
            sp.wait_ge(stored, 32)
            find_last.shift(sp)


def edge_loop(nc, keys_dram, table, edge_ad_dram, edge_rows_dram, blocks_i, chunk_f, last_dst, state):
    W = BLK // 2
    W1 = W + 1
    with ExitStack() as ctx:
        a = Arena(nc, ctx, "edges")

        def slots(name, shape, dt=F32):
            return [a.sb(f"{name}{s}", shape, dt) for s in range(2)]

        def slot_sems(name):
            return [a.sem(f"{name}{s}") for s in range(2)]

        keys = slots("keys", [P, W], I32)
        dst = a.sb("dst", [P, W], I32)
        src = slots("src", [P, W], I32)
        dst_f = slots("dst_f", [P, W1])
        keep = slots("keep", [P, HEADS, W1])
        fresh = slots("fresh", [P, HEADS, W1])
        key_f = slots("key_f", [P, 1])
        key_i = slots("key_i", [P, 1], U32)
        out_f = slots("out_f", [P, 1])
        out_i = slots("out_i", [P, 1], U32)
        ad_i = slots("ad_i", [P, 1], U32)
        rows = slots("rows", [P, W, ROW])
        ad = slots("ad", [P, W, HEADS])
        out = slots("out", [P, W, ROW])
        starts = a.sb("starts", [P, HEADS, W1])
        held = a.sb("held", [P, HEADS, W1])
        raw = a.sb("raw", [P, HEADS, W])
        score = a.sb("score", [P, HEADS, W1])
        tops = a.sb("tops", [P, HEADS, W1])
        before = a.sb("before", [P, HEADS, W])
        gaps = a.sb("gaps", [P, 2, HEADS, W])
        weight = a.sb("weight", [P, HEADS, W])
        decay = a.sb("decay", [P, Q, W1])
        terms = a.sb("terms", [P, Q, W1])
        sums = a.sb("sums", [P, Q, W1])
        key_i_ready = slot_sems("key_i_ready")
        keys_in = slot_sems("keys_in")
        ad_in = slot_sems("ad_in")
        src_ready = slot_sems("src_ready")
        rows_in = slot_sems("rows_in")
        summed = slot_sems("summed")
        copied = slot_sems("copied")
        stored = slot_sems("stored")
        steps = a.sem("edge_steps")
        first = a.sem("first_steps")
        gaps_ready = a.sem("gaps_ready")
        weights_ready = a.sem("weights_ready")
        block = ctx.enter_context(nc.Block())
        key_rows = keys_dram.rearrange("(r c) -> r c", c=W)
        ad_rows = edge_ad_dram.rearrange("(r c) k -> r (c k)", c=W)
        out_rows = edge_rows_dram.rearrange("(r c) k -> r (c k)", c=W)
        LAST = E // W - 1

        def flat(v):
            return v[:, :, :].rearrange("p h w -> p (h w)")

        def wide(v):
            return v.unsqueeze(1).to_broadcast([P, HEADS, W])

        def prepare(dve, st, s):
            st.link(dve.tensor_scalar(key_f[s][:, :], key_f[s][:, :], 2.0, None, ALU.add))
            dve.tensor_copy(key_i[s][:, :], key_f[s][:, :]).then_inc(key_i_ready[s], 1)
            st.link(dve.tensor_scalar(dst[:, :], keys[s][:, :], SRC_BITS, FIELDS - 1, ALU.logical_shift_right,
                                      ALU.bitwise_and))
            dve.tensor_scalar(src[s][:, :], keys[s][:, :], N - 1, None, ALU.bitwise_and).then_inc(src_ready[s], 1)
            st.mark(dve.tensor_copy(dst_f[s][:, 0:1], dst_f[1 - s][:, W:W1]))
            st.link(dve.tensor_copy(dst_f[s][:, 1:W1], dst[:, :]))
            st.link(dve.tensor_tensor(keep[s][:, :, 1:W1], wide(dst_f[s][:, 1:W1]), wide(dst_f[s][:, 0:W]),
                                      ALU.is_equal))
            st.link(dve.tensor_scalar(fresh[s][:, :, 1:W1], keep[s][:, :, 1:W1], 1.0, -FAR, ALU.subtract, ALU.mult))

        @block.gpsimd
        def _(pool):
            blocks = pool.value_load(blocks_i[0:1, 0:1], min_val=1, max_val=EC // BLK)
            last = pool.alloc_register("pool_last_block")
            pool.reg_mov(last, LAST)
            pool.wait_ge(first, 22)
            for s in range(2):
                gather(pool, keys[s][:, :].bitcast(F32), key_rows, key_i[s][:, :], keys_in[s], bound=last)
            gather(pool, ad[0][:, :, :].rearrange("p c k -> p (c k)"), ad_rows, ad_i[0][:, :], ad_in[0], bound=last)
            spare = pool.alloc_register("pool_spare"), first, 22
            with pool.Fori(0, blocks) as i:
                for s in range(2):
                    o = 1 - s
                    wait_apart(pool, src_ready[s], i + 1, spare)
                    pool.wait_ge(key_i_ready[s], i + 1)
                    pool.wait_ge(summed[s], i)
                    gather(pool, keys[s][:, :].bitcast(F32), key_rows, key_i[s][:, :], keys_in[s], bound=last)
                    for c in range(W):
                        gather(pool, rows[s][:, c, :], table, src[s][:, c:c + 1].bitcast(U32), rows_in[s])
                    wait_apart(pool, copied[o], i + s, spare)
                    pool.indirect_dma_start(out_rows, bass.IndirectOffsetOnAxis(ap=out_i[o][:, :], axis=0),
                                            out[o][:, :, :].rearrange("p c k -> p (c k)"), None,
                                            bounds_check=last, oob_is_err=False).then_inc(stored[o], 16)
                    wait_apart(pool, summed[o], i + s, spare)
                    gather(pool, ad[o][:, :, :].rearrange("p c k -> p (c k)"), ad_rows, ad_i[o][:, :], ad_in[o],
                           bound=last)
            wait_apart(pool, copied[1], blocks, spare)
            pool.indirect_dma_start(out_rows, bass.IndirectOffsetOnAxis(ap=out_i[1][:, :], axis=0),
                                    out[1][:, :, :].rearrange("p c k -> p (c k)"), None,
                                    bounds_check=last, oob_is_err=False).then_inc(stored[1], 16)
            for s in range(2):
                pool.wait_ge(stored[s], blocks * 16 + 16 * s)
                pool.wait_ge(keys_in[s], blocks * 16 + 16)
                pool.wait_ge(ad_in[s], blocks * 16 + 16 * (1 - s))

        @block.vector
        def _(dve):
            blocks = dve.value_load(blocks_i[0:1, 0:1], min_val=1, max_val=EC // BLK)
            st = Steps(dve, first)
            for s in range(2):
                st.mark(dve.memset(keep[s][:, :, 0:1], 0.0))
                st.mark(dve.memset(fresh[s][:, :, 0:1], FAR))
                st.mark(dve.memset(ad[s][:, :, :], 0.0))
                st.mark(dve.memset(out[s][:, :, :], 0.0))
                st.mark(dve.memset(keys[s][:, :], 0))
                st.mark(dve.tensor_scalar(key_f[s][:, :], chunk_f[:, :], 2.0, float(s), ALU.mult, ALU.add))
                st.link(dve.tensor_scalar(out_f[s][:, :], chunk_f[:, :], 2.0, float(s), ALU.mult, ALU.add))
                st.mark(dve.tensor_copy(key_i[s][:, :], key_f[s][:, :]))
                st.mark(dve.tensor_copy(ad_i[s][:, :], out_f[s][:, :]))
            st.link(dve.memset(starts[:, :, :], 0.0))
            st.link(dve.memset(dst_f[1][:, W:W1], float(2 * E)))
            st.link(dve.tensor_copy(out_i[1][:, :], dst_f[1][:, W:W1]))
            st.link(dve.memset(dst_f[1][:, W:W1], -1.0))
            assert st.n == 22
            st.mark(dve.memset(decay[:, :, 0:1], 0.0))
            st.mark(dve.memset(held[:, :, W:W1], 0.0))
            st.mark(dve.memset(tops[:, :, W:W1], NONE))
            st.link(dve.memset(sums[:, :, W:W1], 0.0))
            for s in range(2):
                dve.wait_ge(keys_in[s], 16)
                prepare(dve, st, s)
            spare = dve.alloc_register("dve_spare_edges"), first, 22
            with dve.Fori(0, blocks) as i:
                st = LoopSteps(dve, steps, i, 42)
                for s in range(2):
                    o = 1 - s
                    dve.wait_ge(ad_in[s], i * 16 + 16)
                    st.mark(dve.tensor_copy(starts[:, :, 0:1], held[:, :, W:W1]))
                    st.link(dve.tensor_copy(starts[:, :, 1:W1], ad[s][:, :, :].rearrange("p w h -> p h w")))
                    st.link(dve.tensor_tensor_scan(flat(held), flat(keep[s]), flat(starts), 0.0, ALU.mult, ALU.add))
                    dve.wait_ge(rows_in[s], i * (16 * W) + 16 * W)
                    st.link(dve.tensor_tensor(raw[:, :, :], rows[s][:, :, Q:ROW].rearrange("p w h -> p h w"),
                                              held[:, :, 1:W1], ALU.add))
                    st.mark(dve.tensor_copy(score[:, :, 0:1], tops[:, :, W:W1]))
                    st.link(dve.scalar_tensor_tensor(score[:, :, 1:W1], raw[:, :, :], 0.2, raw[:, :, :],
                                                     ALU.mult, ALU.max))
                    dve.wait_ge(copied[o], i + s)
                    st.link(dve.tensor_tensor_scan(flat(tops), flat(fresh[s]), flat(score), 0.0, ALU.add, ALU.max))
                    st.mark(dve.tensor_tensor(gaps[:, 1, :, :], score[:, :, 1:W1], tops[:, :, 1:W1], ALU.subtract))
                    st.link(dve.tensor_tensor(before[:, :, :], tops[:, :, 0:W], fresh[s][:, :, 1:W1], ALU.add))
                    dve.tensor_tensor(gaps[:, 0, :, :], before[:, :, :], tops[:, :, 1:W1], ALU.subtract)\
                        .then_inc(gaps_ready, 1)
                    dve.wait_ge(stored[s], i * 16 + 16 * s)
                    st.mark(dve.tensor_copy(out_i[s][:, :], out_f[s][:, :]))
                    st.mark(dve.tensor_copy(last_dst[:, :], dst_f[s][:, W:W1]))
                    st.link(dve.tensor_copy(terms[:, :, 0:1], sums[:, :, W:W1]))
                    st.link(dve.tensor_scalar(out_f[s][:, :], out_f[s][:, :], 2.0, None, ALU.add))
                    st.mark(dve.tensor_copy(ad_i[s][:, :], out_f[s][:, :]))
                    dve.wait_ge(weights_ready, i * 2 + s + 1)
                    per_head = terms[:, :, 1:W1].rearrange("p (h k) w -> p h k w", h=HEADS)
                    st.link(dve.tensor_tensor(per_head, rows[s][:, :, 0:Q].rearrange("p w (h k) -> p h k w", h=HEADS),
                                              weight[:, :, :].unsqueeze(2).to_broadcast([P, HEADS, NE + 1, W]),
                                              ALU.mult))
                    dve.tensor_tensor_scan(flat(sums), flat(decay), flat(terms), 0.0, ALU.mult, ALU.add)\
                        .then_inc(summed[s], 1)
                    dve.wait_ge(keys_in[s], i * 16 + 32)
                    prepare(dve, st, s)
                st.end()
            dve.wait_ge(summed[1], blocks)
            dve.tensor_copy(state[:, 0:Q], sums[:, :, W]).then_inc(first, 1)
            dve.tensor_copy(state[:, Q:ROW], tops[:, :, W]).then_inc(first, 1)

        @block.scalar
        def _(act):
            blocks = act.value_load(blocks_i[0:1, 0:1], min_val=1, max_val=EC // BLK)
            with act.Fori(0, blocks) as i:
                for s in range(2):
                    act.wait_ge(gaps_ready, i * 2 + s + 1)
                    act.activation(weight[:, :, :], gaps[:, 1, :, :], ACT.Exp)
                    act.activation(decay[:, :, 1:W1].rearrange("p (h k) w -> p h k w", h=HEADS),
                                   gaps[:, 0, :, :].unsqueeze(2).to_broadcast([P, HEADS, NE + 1, W]), ACT.Exp)\
                        .then_inc(weights_ready, 1)
                    act.wait_ge(summed[s], i + 1)
                    act.activation(out[s][:, :, 0:Q], sums[:, :, 1:W1].rearrange("p q w -> p w q"), ACT.Copy)
                    act.activation(out[s][:, :, Q:ROW], tops[:, :, 1:W1].rearrange("p h w -> p w h"), ACT.Copy)\
                        .then_inc(copied[s], 1)


def join_chunks(nc, ends_dram, edge_rows_dram, ident, chunk_f, blocks_i, first_dst, last_dst, state):
    W1 = P + 1
    with ExitStack() as ctx:
        a = Arena(nc, ctx, "join")
        cols = a.sb("cols", [P, 4, Q])
        row = a.sb("row", [Q, 4, P])
        same = a.sb("same", [Q, P])
        pens = a.sb("pens", [Q, P])
        joined = a.sb("joined", [Q, P])
        none = a.sb("none", [Q, P])
        tops = a.sb("tops", [Q, P])
        gaps = a.sb("gaps", [Q, 2, P])
        exps = a.sb("exps", [Q, 2, P])
        terms = a.sb("terms", [Q, P])
        sums = a.sb("sums", [Q, P])
        carry = a.sb("carry", [Q, 2, P])
        back = a.sb("back", [P, 2, Q])
        node_f = a.sb("node_f", [P, 1])
        node_i = a.sb("node_i", [P, 1], U32)
        end_f = a.sb("end_f", [P, 1])
        limit = a.sb("limit", [P, 1])
        blocks_f = a.sb("blocks_f", [P, 1])
        beyond = a.sb("beyond", [P, 1])
        last_i = a.sb("last_i", [P, 1], U32)
        old = a.sb("old", [P, ROW])
        new = a.sb("new", [P, ROW])
        gap2 = a.sb("gap2", [P, 2, HEADS])
        exp2 = a.sb("exp2", [P, 2, HEADS])
        part2 = a.sb("part2", [P, 2, Q])
        turned = a.ps("turned", [Q, 4 * P])
        returned = a.ps("returned", [P, 2 * Q])
        steps = a.sem("join_steps")
        cols_turned = a.sem("cols_turned")
        gaps_ready = a.sem("gaps_ready")
        exps_ready = a.sem("exps_ready")
        carry_turned = a.sem("carry_turned")
        end_in = a.sem("end_in")
        old_in = a.sem("old_in")
        gap2_ready = a.sem("gap2_ready")
        exp2_ready = a.sem("exp2_ready")
        fixed = a.sem("rows_fixed")
        marks = {}
        block = ctx.enter_context(nc.Block())

        @block.vector
        def _(dve):
            st = Steps(dve, steps)
            per_head = cols[:, 1, :].rearrange("p (h k) -> p h k", h=HEADS)
            st.mark(dve.tensor_copy(cols[:, 0, :], state[:, 0:Q]))
            st.mark(dve.tensor_copy(per_head, per_channel(state[:, Q:ROW], NE + 1)))
            st.mark(dve.tensor_copy(cols[:, 2, :], last_dst[:, :].to_broadcast([P, Q])))
            st.link(dve.tensor_copy(cols[:, 3, :], first_dst[:, :].to_broadcast([P, Q])))
            marks["cols"] = st.n
            st.link(dve.tensor_scalar(node_f[:, :], first_dst[:, :], 1.0, float(N), ALU.add, ALU.min))
            st.link(dve.tensor_copy(node_i[:, :], node_f[:, :]))
            marks["node"] = st.n
            st.mark(dve.memset(old[:, :], 0.0))
            st.link(dve.tensor_copy(blocks_f[:, :], blocks_i[:, :]))
            st.link(dve.tensor_tensor(limit[:, :], chunk_f[:, :], blocks_f[:, :], ALU.add))
            st.link(dve.tensor_scalar(limit[:, :], limit[:, :], float(BLK), None, ALU.mult))
            dve.wait_ge(end_in, 16)
            st.link(dve.tensor_tensor(beyond[:, :], end_f[:, :], limit[:, :], ALU.is_gt))
            st.link(dve.scalar_tensor_tensor(beyond[:, :], first_dst[:, :], float(N), beyond[:, :], ALU.is_ge, ALU.add))
            st.link(dve.tensor_scalar(end_f[:, :], end_f[:, :], 1.0, None, ALU.subtract))
            st.link(dve.scalar_tensor_tensor(end_f[:, :], beyond[:, :], float(2 * E), end_f[:, :], ALU.mult, ALU.add))
            st.link(dve.tensor_copy(last_i[:, :], end_f[:, :]))
            marks["last"] = st.n
            dve.wait_ge(cols_turned, 1)
            st.link(dve.tensor_copy(row[:, :, :], turned[:, :].rearrange("q (n p) -> q n p", n=4)))
            st.mark(dve.memset(same[:, 0:1], 0.0))
            st.mark(dve.memset(joined[:, 0:1], 0.0))
            st.mark(dve.tensor_tensor(same[:, 1:P], row[:, 2, 1:P], row[:, 2, 0:P - 1], ALU.is_equal))
            st.link(dve.tensor_tensor(joined[:, 1:P], row[:, 3, 1:P], row[:, 2, 0:P - 1], ALU.is_equal))
            st.link(dve.tensor_scalar(pens[:, :], same[:, :], 1.0, -FAR, ALU.subtract, ALU.mult))
            st.link(dve.tensor_tensor_scan(tops[:, :], pens[:, :], row[:, 1, :], 0.0, ALU.add, ALU.max))
            st.mark(dve.tensor_tensor(gaps[:, 1, :], row[:, 1, :], tops[:, :], ALU.subtract))
            st.mark(dve.memset(gaps[:, 0, 0:1], FAR))
            st.link(dve.tensor_tensor(gaps[:, 0, 1:P], tops[:, 0:P - 1], pens[:, 1:P], ALU.add))
            dve.tensor_tensor(gaps[:, 0, 1:P], gaps[:, 0, 1:P], tops[:, 1:P], ALU.subtract).then_inc(gaps_ready, 1)
            dve.wait_ge(exps_ready, 1)
            st.link(dve.tensor_tensor(terms[:, :], row[:, 0, :], exps[:, 1, :], ALU.mult))
            st.link(dve.tensor_tensor_scan(sums[:, :], exps[:, 0, :], terms[:, :], 0.0, ALU.mult, ALU.add))
            st.link(dve.memset(carry[:, :, :], 0.0))
            st.mark(dve.tensor_tensor(carry[:, 0, 1:P], sums[:, 0:P - 1], joined[:, 1:P], ALU.mult))
            st.link(dve.tensor_tensor(carry[:, 1, 1:P], tops[:, 0:P - 1], joined[:, 1:P], ALU.mult))
            st.link(dve.tensor_scalar(none[:, :], joined[:, :], 1.0, -NONE, ALU.subtract, ALU.mult))
            st.link(dve.tensor_tensor(carry[:, 1, :], carry[:, 1, :], none[:, :], ALU.add))
            marks["carry"] = st.n
            dve.wait_ge(carry_turned, 1)
            st.link(dve.tensor_copy(back[:, :, :], returned[:, :].rearrange("p (n q) -> p n q", n=2)))
            dve.wait_ge(old_in, 16)
            carried = back[:, 1, 0:Q:NE + 1]
            st.link(dve.tensor_tensor(new[:, Q:ROW], old[:, Q:ROW], carried, ALU.max))
            st.mark(dve.tensor_tensor(gap2[:, 0, :], old[:, Q:ROW], new[:, Q:ROW], ALU.subtract))
            dve.tensor_tensor(gap2[:, 1, :], carried, new[:, Q:ROW], ALU.subtract).then_inc(gap2_ready, 1)
            dve.wait_ge(steps, st.n)
            dve.wait_ge(exp2_ready, 1)
            for n, sums_n in enumerate((old[:, 0:Q], back[:, 0, :])):
                st.link(dve.tensor_tensor(part2[:, n, :].rearrange("p (h k) -> p h k", h=HEADS),
                                          sums_n.rearrange("p (h k) -> p h k", h=HEADS),
                                          per_channel(exp2[:, n, :], NE + 1), ALU.mult))
            st.link(dve.tensor_tensor(new[:, 0:Q], part2[:, 0, :], part2[:, 1, :], ALU.add))
            marks["new"] = st.n

        @block.tensor
        def _(pe):
            pe.wait_ge(steps, marks["cols"])
            for n in range(4):
                ins = pe.transpose(turned[:, n * P:(n + 1) * P], cols[:, n, :], ident[:, :])
            ins.then_inc(cols_turned, 1)
            pe.wait_ge(steps, marks["carry"])
            for n in range(2):
                ins = pe.transpose(returned[:, n * Q:(n + 1) * Q], carry[:, n, :], ident[0:Q, 0:Q])
            ins.then_inc(carry_turned, 1)

        @block.scalar
        def _(act):
            act.wait_ge(gaps_ready, 1)
            act.wait_ge(steps, marks["last"])
            act.activation(exps[:, :, :], gaps[:, :, :], ACT.Exp).then_inc(exps_ready, 1)
            act.wait_ge(gap2_ready, 1)
            act.activation(exp2[:, :, :], gap2[:, :, :], ACT.Exp).then_inc(exp2_ready, 1)

        @block.gpsimd
        def _(pool):
            pool.wait_ge(steps, marks["node"])
            gather(pool, end_f[:, :], ends_dram.rearrange("(n a) -> n a", a=1), node_i[:, :], end_in)
            pool.wait_ge(steps, marks["last"])
            gather(pool, old[:, :], edge_rows_dram, last_i[:, :], old_in, bound=E - 1)
            pool.wait_ge(steps, marks["new"])
            pool.indirect_dma_start(edge_rows_dram, bass.IndirectOffsetOnAxis(ap=last_i[:, :], axis=0), new[:, :], None,
                                    bounds_check=E - 1, oob_is_err=False).then_inc(fixed, 16)
            pool.wait_ge(fixed, 16)


def route(nc, b_gat, ln_gamma, ln_beta, edge_rows_dram, table, ends_f, starts_f, last_ends, last_starts, rows,
          ad_sb, x_sb, eo, out_dram):
    F = HEADS * NE
    PARTS = 4
    TP = T // PARTS
    with ExitStack() as ctx:
        a = Arena(nc, ctx, "route")
        edge = a.sb("edge", [P, T, ROW])
        empty = a.sb("empty", [P, T])
        at_f = a.sb("at_f", [P, T])
        at = a.sb("at", [P, T], U32)
        vec = a.sb("vec", [P, 3, F])
        mine = a.sb("mine", [P, TP, HEADS])
        top = a.sb("top", [P, TP, HEADS])
        last_row = a.sb("last_row", [P, ROW])
        times = a.sb("times", [P, T])
        absent = a.sb("absent", [P, T])
        shared = a.sb("shared", [P, TP, HEADS])
        gap = a.sb("gap", [P, 3, TP, HEADS])
        e2 = a.sb("e2", [P, 3, TP, HEADS])
        part = a.sb("part", [P, TP, Q])
        part3 = a.sb("part3", [P, TP, Q])
        total = a.sb("total", [P, TP, Q])
        inverse = a.sb("inverse", [P, TP, HEADS])
        agg = a.sb("agg", [P, TP, F])
        scores = a.sb("scores", [P, TP, NE])
        gate = a.sb("gate", [P, TP, NE])
        gap2, gap2_exp = a.sb("gap2", [P, TP]), a.sb("gap2_exp", [P, TP])
        weighted = a.sb("weighted", [P, TB, NE * C])
        summed = a.sb("summed", [P, TB, C])
        norm = Norm(a, "norm", TP, F, 1e-5)
        vec_in = a.sem("vec_in")
        last_in = a.sem("last_in")
        steps = a.sem("route_steps")
        edge_in = [a.sem(f"edge_in{n}") for n in range(PARTS)]
        gaps_ready = a.sem("gaps_ready")
        exps_ready = a.sem("exps_ready")
        normed = a.sem("normed")
        gap2_ready = a.sem("gap2_ready")
        gap2_exp_ready = a.sem("gap2_exp_ready")
        result = a.sem("result_ready")
        stored = a.sem("result_stored")
        marks, gaps_marks = {}, []
        block = ctx.enter_context(nc.Block())

        @block.vector
        def _(dve):
            st = Steps(dve, steps)
            st.mark(dve.memset(edge[:, :, 0:Q], 0.0))
            st.mark(dve.memset(edge[:, :, Q:ROW], NONE))
            st.mark(dve.tensor_tensor(empty[:, :], starts_f[:, :], ends_f[:, :], ALU.is_equal))
            st.link(dve.tensor_scalar(at_f[:, :], ends_f[:, :], 1.0, None, ALU.subtract))
            st.link(dve.scalar_tensor_tensor(at_f[:, :], empty[:, :], float(2 * E), at_f[:, :], ALU.mult, ALU.add))
            st.link(dve.tensor_scalar(at_f[:, :], at_f[:, :], 0.0, None, ALU.max))
            st.link(dve.tensor_copy(at[:, :], at_f[:, :]))
            marks["at"] = st.n
            dve.wait_ge(last_in, 16)
            dve.wait_ge(vec_in, 48)
            st.link(dve.tensor_tensor(times[:, :], last_ends[:, :], last_starts[:, :], ALU.subtract))
            st.link(dve.tensor_scalar(absent[:, :], times[:, :], 0.0, NONE, ALU.is_le, ALU.mult))
            for n in range(PARTS):
                now = slice(n * TP, (n + 1) * TP)
                st.link(dve.tensor_tensor(mine[:, :, :], rows[:, now, Q:ROW], ad_sb[:, now, :], ALU.add))
                st.link(dve.scalar_tensor_tensor(mine[:, :, :], mine[:, :, :], 0.2, mine[:, :, :], ALU.mult, ALU.max))
                st.link(dve.tensor_tensor(shared[:, :, :], last_row[:, Q:ROW].unsqueeze(1).to_broadcast([P, TP, HEADS]),
                                          ad_sb[:, now, :], ALU.add))
                st.link(dve.scalar_tensor_tensor(shared[:, :, :], shared[:, :, :], 0.2, shared[:, :, :], ALU.mult, ALU.max))
                st.link(dve.tensor_tensor(shared[:, :, :], shared[:, :, :], per_channel(absent[:, now], HEADS), ALU.add))
                st.link(dve.tensor_tensor(top[:, :, :], mine[:, :, :], shared[:, :, :], ALU.max))
                dve.wait_ge(edge_in[n], 16 * TP)
                st.link(dve.tensor_tensor(top[:, :, :], top[:, :, :], edge[:, now, Q:ROW], ALU.max))
                st.mark(dve.tensor_tensor(gap[:, 2, :, :], shared[:, :, :], top[:, :, :], ALU.subtract))
                st.mark(dve.tensor_tensor(gap[:, 0, :, :], edge[:, now, Q:ROW], top[:, :, :], ALU.subtract))
                gaps_marks.append(st.n)
                dve.tensor_tensor(gap[:, 1, :, :], mine[:, :, :], top[:, :, :], ALU.subtract).then_inc(gaps_ready, 1)
                dve.wait_ge(exps_ready, n + 1)

                def by_head(v):
                    return v.rearrange("p t (h k) -> p t h k", h=HEADS)

                def wide(v):
                    return v.unsqueeze(3).to_broadcast([P, TP, HEADS, NE + 1])

                st.mark(dve.tensor_tensor(by_head(total[:, :, :]), by_head(edge[:, now, 0:Q]), wide(e2[:, 0, :, :]), ALU.mult))
                st.mark(dve.tensor_tensor(by_head(part[:, :, :]), by_head(rows[:, now, 0:Q]), wide(e2[:, 1, :, :]), ALU.mult))
                st.link(dve.tensor_tensor(e2[:, 2, :, :], e2[:, 2, :, :], per_channel(times[:, now], HEADS), ALU.mult))
                st.mark(dve.tensor_tensor(by_head(part3[:, :, :]), by_head(last_row[:, 0:Q].unsqueeze(1).to_broadcast([P, TP, Q])),
                                          wide(e2[:, 2, :, :]), ALU.mult))
                st.link(dve.tensor_tensor(total[:, :, :], total[:, :, :], part[:, :, :], ALU.add))
                st.link(dve.tensor_tensor(total[:, :, :], total[:, :, :], part3[:, :, :], ALU.add))
                st.link(dve.tensor_scalar(inverse[:, :, :], by_head(total[:, :, :])[:, :, :, 0], 1e-16, None, ALU.add))
                st.link(dve.reciprocal(inverse[:, :, :], inverse[:, :, :]))
                st.link(dve.tensor_tensor(by_head(agg[:, :, :]), by_head(total[:, :, :])[:, :, :, 1:NE + 1],
                                          inverse[:, :, :].unsqueeze(3).to_broadcast([P, TP, HEADS, NE]), ALU.mult))
                def vector(m):
                    return vec[:, m, :].unsqueeze(1).to_broadcast([P, TP, F])

                st.link(dve.tensor_tensor(agg[:, :, :], agg[:, :, :], vector(0), ALU.add))
                norm.vector(dve, st, agg[:, :, :], agg[:, :, :], n, normed)
                st.link(dve.tensor_tensor(agg[:, :, :], agg[:, :, :], vector(1), ALU.mult))
                st.link(dve.tensor_tensor(agg[:, :, :], agg[:, :, :], vector(2), ALU.add))
                st.link(dve.tensor_reduce(scores[:, :, :], agg[:, :, :].rearrange("p t (h k) -> p t k h", h=HEADS), X, ALU.add))
                st.link(dve.tensor_scalar(scores[:, :, :], scores[:, :, :], 1.0 / HEADS, None, ALU.mult))
                masks, tops = top_two(dve, st, a, f"best{n}", scores[:, :, :], TP, NE)
                two_weights(dve, st, a, f"best{n}", gate[:, :, :], tops, masks, gap2, gap2_exp, gap2_ready, gap2_exp_ready, n)
                for b in range(n * B // PARTS, (n + 1) * B // PARTS):
                    tiles = slice(b * TB, (b + 1) * TB)
                    st.link(dve.tensor_tensor(weighted[:, :, :].rearrange("p t (e c) -> p t e c", e=NE),
                                              eo[:, tiles, :].rearrange("p t (e c) -> p t e c", e=NE),
                                              gate[:, b * TB - n * TP:(b + 1) * TB - n * TP, :].unsqueeze(3).to_broadcast([P, TB, NE, C]), ALU.mult))
                    st.link(dve.tensor_reduce(summed[:, :, :], weighted[:, :, :].rearrange("p t (e c) -> p t c e", e=NE),
                                              X, ALU.add))
                    dve.tensor_tensor(x_sb[:, tiles, :], x_sb[:, tiles, :], summed[:, :, :], ALU.add).then_inc(result, 1)
                    dve.wait_ge(result, b + 1)

        @block.scalar
        def _(act):
            for n in range(PARTS):
                act.wait_ge(gaps_ready, n + 1)
                act.wait_ge(steps, gaps_marks[n])
                act.activation(e2[:, :, :, :], gap[:, :, :, :], ACT.Exp).then_inc(exps_ready, 1)
                norm.scalar(act, n)
                act.wait_ge(gap2_ready, n + 1)
                act.activation(gap2_exp[:, :], gap2[:, :], ACT.Exp).then_inc(gap2_exp_ready, 1)

        @block.gpsimd
        def _(pool):
            pool.wait_ge(steps, marks["at"])
            for t in range(T):
                gather(pool, edge[:, t, :], edge_rows_dram, at[:, t:t + 1], edge_in[t // TP], bound=E - 1)

        @block.sync
        def _(sp):
            sp.dma_start(last_row[:, :], table[N - 1, :].partition_broadcast(P)).then_inc(last_in, 16)
            for n, v in enumerate((b_gat, ln_gamma, ln_beta)):
                sp.dma_start(vec[:, n, :], v.partition_broadcast(P)).then_inc(vec_in, 16)
            for b in range(B):
                sp.wait_ge(result, b + 1)
                sp.dma_start(out_dram[b, :, :, :].rearrange("(t r) w c -> (r w) t c", t=TB), x_sb[:, b * TB:(b + 1) * TB, :])\
                    .then_inc(stored, 16)
            sp.wait_ge(stored, 16 * B)


def build(nc, x, gamma, gate_w, gate_b, w1, w2, w3, kernel_w, W_gat, att_src, att_dst, b_gat, ln_gamma, ln_beta,
          W1, b1, W2, b2, edge_index, out):
    keys_dram = nc.dram_tensor("keys_dram", (E,), F32).ap()
    pivots_dram = nc.dram_tensor("pivots_dram", (E // BLK,), F32).ap()
    ends_dram = nc.dram_tensor("ends_dram", (N + 1,), F32).ap()
    last_src_dram = nc.dram_tensor("last_src_dram", (N + 1,), F32).ap()
    table = nc.dram_tensor("table", (N, ROW), F32).ap()
    a_dst_dram = nc.dram_tensor("a_dst_dram", (N, HEADS), F32).ap()
    edge_ad_dram = nc.dram_tensor("edge_ad_dram", (E, HEADS), F32).ap()
    edge_rows_dram = nc.dram_tensor("edge_rows_dram", (E, ROW), F32).ap()
    with ExitStack() as ctx:
        a = Arena(nc, ctx, "all")
        ident = a.sb("ident", [P, P])
        p_sign = a.sb("p_sign", [P, 2])
        x_sb = a.sb("x_sb", [P, T, C])
        blocks_i = a.sb("blocks_i", [P, 1], I32)
        chunk_f = a.sb("chunk_f", [P, 1])
        first_dst = a.sb("first_dst", [P, 1])
        last_dst = a.sb("last_dst", [P, 1])
        state = a.sb("state", [P, ROW])
        ends_f = a.sb("ends_f", [P, T])
        starts_f = a.sb("starts_f", [P, T])
        kept = a.sb("kept", [P, 1])
        last_ends, last_starts = a.sb("last_ends", [P, T]), a.sb("last_starts", [P, T])
        ad_sb = a.sb("ad_sb", [P, T, HEADS])
        rows = a.sb("rows", [P, T, ROW])
        stacks = [a.sb(f"stack{n}", [P, N], BF16) for n in range(2)]
        x_in = a.sem("x_in")
        with ExitStack() as sorting:
            b = Arena(nc, sorting, "sorting")
            keys = [b.sb(f"keys{n}", [P, EC]) for n in range(3)]
            zeros = b.sb("zeros", [P, EC])
            sort = Sort(b, keys, p_sign)
            weights = SplitWeights(b, w1, w2)
            constants(nc, edge_index, ident, p_sign, keys, zeros, x, x_sb, x_in)
            with ExitStack() as inner:
                weightsT = Arena(nc, inner, "inner").sb("weightsT", [3 * w1.shape[0], N], BF16)
                attention(nc, gamma, x_sb, x_in, stacks, ident, sort, weights)
                gates(nc, gate_w, gate_b, stacks, weightsT, ident, sort)
                experts(nc, weights, w3, x_sb, stacks, weightsT, ident, sort, keys_dram, pivots_dram, zeros,
                        [v.rearrange("n k -> (n k)") for v in (edge_ad_dram, edge_rows_dram)])
        eo = a.sb("eo", [P, T, NE * C])
        with ExitStack() as inner:
            b = Arena(nc, inner, "graph")
            find_last = Search(nc, b, "last_src", N, kept[0:1, :], keys_dram, pivots_dram, last_src_dram, last_ends,
                               last_starts, b.sb("less", [P, T, Search.L], BF16))
            last_weights = LastWeights(b, W_gat, W1)
            convolve(nc, kernel_w, x_sb, stacks, ident, keys_dram, pivots_dram, ends_dram, kept, blocks_i, ends_f, starts_f,
                     find_last, last_weights, eo[:, :, 0:Search.L])
            publish(nc, last_weights, find_last, att_src, att_dst, b1, W2, b2, stacks, eo, ident, rows, ad_sb, table,
                    a_dst_dram, keys_dram, ends_f, starts_f, edge_ad_dram, blocks_i, chunk_f, first_dst)
        edge_loop(nc, keys_dram, table, edge_ad_dram, edge_rows_dram, blocks_i, chunk_f, last_dst, state)
        join_chunks(nc, ends_dram, edge_rows_dram, ident, chunk_f, blocks_i, first_dst, last_dst, state)
        route(nc, b_gat, ln_gamma, ln_beta, edge_rows_dram, table, ends_f, starts_f, last_ends, last_starts, rows, ad_sb,
              x_sb, eo, out)


_INS = ["x", "L0_conv_gamma", "L0_ffn_gate_w", "L0_ffn_gate_b", "L0_ffn_w1", "L0_ffn_w2", "L0_ffn_w3",
        "L1_conv_kernel", "L1_ffn_W_gat", "L1_ffn_att_src", "L1_ffn_att_dst", "L1_ffn_b_gat", "L1_ffn_ln_gamma",
        "L1_ffn_ln_beta", "L1_ffn_W1", "L1_ffn_b1", "L1_ffn_W2", "L1_ffn_b2", "L1_ffn_edge_index"]
_OUTS = [((B, 32, 32, C), "float32")]


def kernel(**inputs):
    import numpy as _np
    import concourse.bacc as _bacc
    from concourse import mybir as _mybir
    from concourse.bass_utils import run_bass_kernel_spmd as _run
    nc = _bacc.Bacc("TRN2", target_bir_lowering=False, num_devices=1)
    arrays, args = {}, []
    for name in _INS:
        a = _np.ascontiguousarray(inputs[name])
        arrays[f"in_{name}_dram"] = a
        args.append(nc.dram_tensor(f"in_{name}_dram", a.shape, _mybir.dt.from_np(a.dtype), kind="ExternalInput").ap())
    for i, (shape, dtype) in enumerate(_OUTS):
        dt = _mybir.dt.from_np(_np.dtype(dtype))
        args.append(nc.dram_tensor(f"out_{i}_dram", shape, dt, kind="ExternalOutput").ap())
    build(nc, *args)
    r = _run(nc, [arrays], core_ids=[0])
    got = tuple(r.results[0][f"out_{i}_dram"] for i in range(len(_OUTS)))
    return got if len(got) > 1 else got[0]
```
